# Optimizing a Trainium2 kernel written in Bass

```python
import numpy as np
import jax
import jax.numpy as jnp

def _softmax(x, axis=-1):
    return jax.nn.softmax(x, axis=axis)

def _gelu(x):
    return jax.nn.gelu(x, approximate=True)

def _silu(x):
    return jax.nn.silu(x)

def _sigmoid(x):
    return jax.nn.sigmoid(x)

def _layernorm(x, axis=-1, eps=1e-05):
    m = jnp.mean(x, axis=axis, keepdims=True)
    v = jnp.var(x, axis=axis, keepdims=True)
    return (x - m) / jnp.sqrt(v + eps)

def _scatter_add(tgt, idx, src, axis=0):
    return tgt.at[idx].add(src)

def _segment_sum(src, seg, n):
    return jax.ops.segment_sum(src, seg, n)
kernel_name = 'mk_xattn_ffn_d1_seqx_r4_282c24'

def setup_inputs(seed: int=0):
    np.random.seed(seed)
    _w = jnp.asarray

    def _rec_inputs():
        import jax
        import jax.numpy as jnp
        _rk = jax.random.key(seed)
        x = -0.0002928 + 1 * jax.random.normal(jax.random.fold_in(_rk, 1), (32, 256, 256), jnp.float32)
        _lenS = 256 - jax.random.randint(jax.random.fold_in(_rk, 7), (32,), 0, max(1, 256 // 4) + 1, jnp.int32)
        _lenS2 = 120 - jax.random.randint(jax.random.fold_in(_rk, 8), (32,), 0, max(1, 120 // 4) + 1, jnp.int32)
        _ctx_1024P = jax.random.normal(jax.random.fold_in(_rk, 11), (32, 16, 256), jnp.float32)
        _ctx_1024c = jax.random.dirichlet(jax.random.fold_in(_rk, 511), 0.3 * jnp.ones((16,), jnp.float32), (32, 120))
        _ctx_1024t = jnp.einsum('bsk,bkd->bsd', _ctx_1024c, _ctx_1024P)
        _ctx_1024t = _ctx_1024t * jax.lax.rsqrt(jnp.mean(jnp.square(_ctx_1024t)) + 1e-12) * 0.953939
        ctx_1024 = -1.39393e-06 + 0.999914 * (_ctx_1024t + 0.3 * jax.random.normal(jax.random.fold_in(_rk, 611), (32, 120, 256), jnp.float32))
        return (x, ctx_1024)
    x, ctx_1024 = _rec_inputs()

    def _L0_xattn_setup():
        import jax, jax.numpy as jnp
        import numpy as np
        DIM = 256
        HEADS = 16
        HEAD_DIM = DIM // HEADS
        SCALE = HEAD_DIM ** (-0.5)

        def _split_heads(t):
            b, n, _ = t.shape
            return t.reshape(b, n, HEADS, HEAD_DIM).transpose(0, 2, 1, 3)
        key = jax.random.key(seed)
        ks = jax.random.split(key, 7)
        B, N, M = (2, 512, 512)
        x = jax.random.normal(ks[0], (B, N, DIM), dtype=jnp.float32)
        y = jax.random.normal(ks[1], (B, M, DIM), dtype=jnp.float32)
        s = DIM ** (-0.5)
        Wq = jax.random.normal(ks[2], (DIM, DIM), dtype=jnp.float32) * s
        Wk = jax.random.normal(ks[3], (DIM, DIM), dtype=jnp.float32) * s
        Wv = jax.random.normal(ks[4], (DIM, DIM), dtype=jnp.float32) * s
        Wp = jax.random.normal(ks[5], (DIM, DIM), dtype=jnp.float32) * s
        bp = jax.random.normal(ks[6], (DIM,), dtype=jnp.float32) * 0.01
        return {'x': x, 'y': y, 'Wq': Wq, 'Wk': Wk, 'Wv': Wv, 'Wp': Wp, 'bp': bp}
    _L0_xattn_all = _L0_xattn_setup()
    _L0_xattn_in = {k: v for k, v in _L0_xattn_all.items() if k in ('Wq', 'Wk', 'Wv', 'Wp', 'bp')}
    del _L0_xattn_all

    def _L0_ffn_setup():
        import jax, jax.numpy as jnp
        import numpy as np
        import math
        B, L, D = (4, 1024, 256)
        F = 1024
        E = 16
        CAP_FACTOR = 1.0
        EPS = 1e-05
        key = jax.random.key(seed)
        ks = jax.random.split(key, 8)
        std = 0.02
        return {'x': jax.random.normal(ks[0], (B, L, D), dtype=jnp.float32), 'norm_weight': jnp.ones((D,), dtype=jnp.float32), 'router_weight': jax.random.normal(ks[1], (E, D), dtype=jnp.float32) * std, 'router_bias': jnp.zeros((E,), dtype=jnp.float32), 'fc1_weight': jax.random.normal(ks[2], (E, F, D), dtype=jnp.float32) * std, 'fc1_bias': jnp.zeros((E, F), dtype=jnp.float32), 'fc2_weight': jax.random.normal(ks[3], (E, D, F), dtype=jnp.float32) * std, 'fc2_bias': jnp.zeros((E, D), dtype=jnp.float32)}
    _L0_ffn_all = _L0_ffn_setup()
    _L0_ffn_in = {k: v for k, v in _L0_ffn_all.items() if k in ('norm_weight', 'router_weight', 'router_bias', 'fc1_weight', 'fc1_bias', 'fc2_weight', 'fc2_bias')}
    del _L0_ffn_all
    return {'x': x, 'ctx_1024': ctx_1024, 'L0_xattn_Wq': _L0_xattn_in['Wq'], 'L0_xattn_Wk': _L0_xattn_in['Wk'], 'L0_xattn_Wv': _L0_xattn_in['Wv'], 'L0_xattn_Wp': _L0_xattn_in['Wp'], 'L0_xattn_bp': _L0_xattn_in['bp'], 'L0_ffn_norm_weight': _L0_ffn_in['norm_weight'], 'L0_ffn_router_weight': _L0_ffn_in['router_weight'], 'L0_ffn_router_bias': _L0_ffn_in['router_bias'], 'L0_ffn_fc1_weight': _L0_ffn_in['fc1_weight'], 'L0_ffn_fc1_bias': _L0_ffn_in['fc1_bias'], 'L0_ffn_fc2_weight': _L0_ffn_in['fc2_weight'], 'L0_ffn_fc2_bias': _L0_ffn_in['fc2_bias']}

def reference(x, ctx_1024, L0_xattn_Wq, L0_xattn_Wk, L0_xattn_Wv, L0_xattn_Wp, L0_xattn_bp, L0_ffn_norm_weight, L0_ffn_router_weight, L0_ffn_router_bias, L0_ffn_fc1_weight, L0_ffn_fc1_bias, L0_ffn_fc2_weight, L0_ffn_fc2_bias):
    import jax
    import jax.numpy as jnp

    def _L0_xattn_ref(x, y, Wq, Wk, Wv, Wp, bp):
        import jax, jax.numpy as jnp
        import numpy as np
        DIM = 256
        HEADS = 16
        HEAD_DIM = DIM // HEADS
        SCALE = HEAD_DIM ** (-0.5)

        def _split_heads(t):
            b, n, _ = t.shape
            return t.reshape(b, n, HEADS, HEAD_DIM).transpose(0, 2, 1, 3)
        q = _split_heads(x @ Wq)
        k = _split_heads(y @ Wk)
        v = _split_heads(y @ Wv)
        attn = jnp.einsum('bhid,bhjd->bhij', q, k) * SCALE
        attn = jax.nn.softmax(attn, axis=-1)
        out = jnp.einsum('bhij,bhjd->bhid', attn, v)
        b, h, n, d = out.shape
        out = out.transpose(0, 2, 1, 3).reshape(b, n, h * d)
        return out @ Wp + bp

    def _L0_ffn_ref(x, norm_weight, router_weight, router_bias, fc1_weight, fc1_bias, fc2_weight, fc2_bias):
        import jax, jax.numpy as jnp
        import numpy as np
        import math
        B, L, D = (4, 1024, 256)
        F = 1024
        E = 16
        CAP_FACTOR = 1.0
        EPS = 1e-05
        b, l, d = x.shape
        n_tokens = b * l
        n_experts = router_weight.shape[0]
        capacity = max(1, math.ceil(CAP_FACTOR * n_tokens / n_experts))
        top_k = min(capacity, n_tokens)
        xf = x.reshape(n_tokens, d)
        rms = jnp.sqrt(jnp.mean(xf * xf, axis=-1, keepdims=True) + EPS)
        xn = xf / rms * norm_weight
        logits = xn @ router_weight.T + router_bias
        probs = jax.nn.softmax(logits, axis=-1)
        _, idx = jax.lax.top_k(logits.T, top_k)
        xe = xn[idx]
        h = jnp.einsum('ecd,efd->ecf', xe, fc1_weight) + fc1_bias[:, None, :]
        h = jax.nn.gelu(h, approximate=False)
        y = jnp.einsum('ecf,edf->ecd', h, fc2_weight) + fc2_bias[:, None, :]
        gates = jnp.take_along_axis(probs.T, idx, axis=1)
        flat_idx = idx.reshape(-1)
        contrib = (y * gates[:, :, None]).reshape(-1, d)
        output = jnp.zeros((n_tokens, d), dtype=x.dtype).at[flat_idx].add(contrib)
        gate_sums = jnp.zeros((n_tokens, 1), dtype=x.dtype).at[flat_idx].add(gates.reshape(-1, 1))
        assigned = gate_sums > 0
        output = jnp.where(assigned, output / jnp.where(assigned, gate_sums, 1.0), output)
        return output.reshape(b, l, d)
    x = x + _L0_xattn_ref(_layernorm(x, axis=-1), ctx_1024, L0_xattn_Wq, L0_xattn_Wk, L0_xattn_Wv, L0_xattn_Wp, L0_xattn_bp)
    x = x + _L0_ffn_ref(_layernorm(x, axis=-1), L0_ffn_norm_weight, L0_ffn_router_weight, L0_ffn_router_bias, L0_ffn_fc1_weight, L0_ffn_fc1_bias, L0_ffn_fc2_weight, L0_ffn_fc2_bias)
    return x

_drawn_inputs = setup_inputs


def setup_inputs(seed=0):
    import zlib

    import numpy as np

    out = dict(_drawn_inputs(seed))
    spreads = {'L0_ffn_norm_weight': (1.0, 0.2),
     'L0_ffn_router_bias': (0.0, 2.0),
     'L0_ffn_fc1_bias': (0.0, 0.366),
     'L0_ffn_fc2_bias': (0.0, 0.1)}
    factors = {'L0_xattn_bp': 5.57}
    for name, (base, spread) in spreads.items():
        noise = np.random.default_rng([zlib.crc32(name.encode()), seed]).standard_normal(out[name].shape)
        drawn = base * np.exp(spread * noise) if base else spread * noise
        out[name] = jnp.asarray(drawn.astype(out[name].dtype))
    for name, factor in factors.items():
        out[name] = (out[name] * factor).astype(out[name].dtype)
    return out
```

```python
import concourse.bass as bass
from concourse import mybir
from contextlib import ExitStack

FP32 = mybir.dt.float32
FP32R = mybir.dt.float32r
BF16 = mybir.dt.bfloat16
I32 = mybir.dt.int32
U32 = mybir.dt.uint32
ALU = mybir.AluOpType
ACT = mybir.ActivationFunctionType
AX = mybir.AxisListType

P = 128
B, S, D = 32, 256, 256
M = 120
H, DH = 16, 16
KD = D // P
TB = S // P
N = B * S
NT = N // P
E = 16
F = 1024
KF = F // P
CAP = N // E
NC = 8
CT = N // NC
TC = NT // NC
GT = CAP // P
EG = 4
SA, SB = 32, 16
EPS = 1e-5
SCALE = DH ** -0.5
HV = DH + 1
SU = 2
NU = H // SU
MU = 4
NQ = TB * H // MU
GMAX = float(CAP) - 0.5
BACK = (2, 2, 5, 3)


def attention_phase(nc, ctx, sem, bank, ident, L, x, ctxT, wq, wk, wv, wp, bp, nw, rw, rb, out, xn_table):
    def sb(name, shape, dt):
        return ctx.enter_context(nc.sbuf_tensor(name, shape, dt))

    def pair(name, shape, dt):
        return [sb(f"{name}{u}", shape, dt) for u in range(2)]

    wq_sb, wk_sb, wv_sb, wp_sb = (sb(n, [P, KD, D], FP32) for n in ("wq_sb", "wk_sb", "wv_sb", "wp_sb"))
    bp_sb = sb("bp_sb", [P, D], FP32)
    nw_sb = sb("nw_sb", [P, KD], FP32)
    rw_sb = sb("rw_sb", [P, KD, E], FP32)
    rb_sb = sb("rb_sb", [P, E], FP32)
    head_rows = sb("head_rows", [P, P // DH], FP32)
    row_pick_f = sb("row_pick_f", [P, H, M], FP32)
    row_pick = sb("row_pick", [P, H, M], FP32R)
    minus_half = sb("minus_half", [P, TB], FP32)

    X = pair("X", [P, TB, D], FP32)
    XB = pair("XB", [P, TB, D], FP32)
    CTX = pair("CTX", [P, KD, M], FP32)
    bn1, mv1, rstd1 = pair("bn1", [P, TB, 6], FP32), pair("mv1", [P, TB, 2], FP32), pair("rstd1", [P, TB], FP32)
    ve1 = pair("ve1", [P, TB], FP32)
    XN = pair("XN", [P, TB, D], FP32)
    XNT = pair("XNT", [P, KD, S], FP32)
    QH, QL = pair("QH", [P, KD, S], FP32R), pair("QL", [P, KD, S], FP32R)
    KH, KL = pair("KH", [P, KD, M], FP32R), pair("KL", [P, KD, M], FP32R)
    KHZ, KLZ = pair("KHZ", [P, H, M], FP32R), pair("KLZ", [P, H, M], FP32R)
    VA = pair("VA", [P, H, HV], FP32)
    NM = pair("NM", [P, TB, P], FP32)
    NMT = pair("NMT", [P, S], FP32R)
    PT = pair("PT", [P, H, S], FP32)
    RS = pair("RS", [P, TB, H], FP32)
    ON = pair("ON", [P, TB, D], FP32)
    OT = pair("OT", [P, KD, S], FP32)
    X1 = pair("X1", [P, TB, D], FP32)
    bn2, mv2, rstd2 = pair("bn2", [P, TB, 6], FP32), pair("mv2", [P, TB, 2], FP32), pair("rstd2", [P, TB], FP32)
    ve2 = pair("ve2", [P, TB], FP32)
    XN2 = pair("XN2", [P, TB, D], FP32)
    XN2T = pair("XN2T", [P, KD, S], FP32)

    smax_bank = bank[0:2]
    score_bank = bank[2:5]
    pv_bank = bank[5:7]
    misc = bank[7]

    w_loaded = sem("w_loaded")
    x_loaded = [sem(f"x_loaded{u}") for u in range(2)]
    ctx_loaded = [sem(f"ctx_loaded{u}") for u in range(2)]
    x1_stored = [sem(f"x1_stored{u}") for u in range(2)]
    xn2_stored = [sem(f"xn2_stored{u}") for u in range(2)]
    pool_const = sem("pool_const")
    const_ready = sem("const_ready")
    stats1_a, stats1_ready = sem("stats1_a"), sem("stats1_ready")
    ve1_ready, rstd1_ready = sem("ve1_ready"), sem("rstd1_ready")
    xn_ready = sem("xn_ready")
    xnT_done, xnT_ready = sem("xnT_done"), sem("xnT_ready")
    q_done, qh_ready, ql_ready = sem("q_done"), sem("qh_ready"), sem("ql_ready")
    kv_done, kh_ready, va_ready, kl_ready = sem("kv_done"), sem("kh_ready"), sem("va_ready"), sem("kl_ready")
    khz_ready, klz_ready = sem("khz_ready"), sem("klz_ready")
    xb_ready = sem("xb_ready")
    smax_done, max_ready = sem("smax_done"), sem("max_ready")
    nmT_done, nmT_ready = sem("nmT_done"), sem("nmT_ready")
    score_done, exp_ready = sem("score_done"), sem("exp_ready")
    pv_done, rs_ready, on_ready = sem("pv_done"), sem("rs_ready"), sem("on_ready")
    oT_done, oT_ready = sem("oT_done"), sem("oT_ready")
    proj_done, x1_ready = sem("proj_done"), sem("x1_ready")
    stats2_a, stats2_ready = sem("stats2_a"), sem("stats2_ready")
    ve2_ready, rstd2_ready = sem("ve2_ready"), sem("rstd2_ready")
    xn2_ready = sem("xn2_ready")
    xn2T_done, xn2T_ready = sem("xn2T_done"), sem("xn2T_ready")
    logit_done, logit_ready = sem("logit_done"), sem("logit_ready")

    def wait(eng, s, value):
        if not isinstance(value, int) or value > 0:
            eng.wait_ge(s, value)

    def run(eng, step):
        step(0, -1, prepare=True, score=False, finish=False, stats=True)
        step(0, 0, prepare=True, score=True, finish=False, stats=True)
        step(0, 1, prepare=True, score=True, finish=True, stats=True)
        with eng.Fori(1, B // 2 - 1) as i:
            step(i, 0, prepare=True, score=True, finish=True, stats=True)
            step(i, 1, prepare=True, score=True, finish=True, stats=True)
        step(B // 2 - 1, 0, prepare=True, score=True, finish=True, stats=False)
        step(B // 2 - 1, 1, prepare=False, score=True, finish=True, stats=False)
        step(B // 2 - 1, 2, prepare=False, score=False, finish=True, stats=False)

    pool_passed, dve_passed = sem("pool_passed"), sem("dve_passed")
    block = ctx.enter_context(nc.Block())

    @block.sync
    def _(sp):
        def load_x(i, c):
            b, u = 2 * i + c, c % 2
            sp.dma_start(X[u][:, :, :], x[bass.ds(b, 1), :, :].rearrange("o (t p) d -> p (o t) d", p=P)) \
                .then_inc(x_loaded[u], 16)

        def load_ctx(i, c):
            b, u = 2 * i + c, c % 2
            sp.dma_start(CTX[u][:, :, :], ctxT[bass.ds(b, 1), :, :].rearrange("o (k p) m -> p (o k) m", p=P)) \
                .then_inc(ctx_loaded[u], 16)

        load_x(0, 0)
        load_ctx(0, 0)
        for t, w in ((wk_sb, wk), (wv_sb, wv), (wq_sb, wq), (wp_sb, wp)):
            sp.dma_start(t[:, :, :], w.rearrange("(k p) c -> p k c", p=P)).then_inc(w_loaded, 16)
        load_x(0, 1)
        sp.dma_start(bp_sb[:, :], bp.rearrange("(o d) -> o d", o=1).to_broadcast([P, D])).then_inc(w_loaded, 16)
        sp.dma_start(nw_sb[:, :], nw).then_inc(w_loaded, 16)
        sp.dma_start(rw_sb[:, :, :], rw.rearrange("(k p) e -> p k e", p=P)).then_inc(w_loaded, 16)
        sp.dma_start(rb_sb[:, :], rb.rearrange("(o d) -> o d", o=1).to_broadcast([P, E])).then_inc(w_loaded, 16)
        load_ctx(0, 1)

        def step(i, c, prepare, score, finish, stats):
            s, u, v = 2 * i + c, c % 2, (c + 1) % 2
            if prepare and score and stats:
                wait(sp, kv_done, s + 1)
                load_ctx(i, c + 2)
            if finish:
                sp.wait_ge(x1_ready, s)
                sp.dma_start(out[bass.ds(s - 1, 1), :, :].rearrange("o (t p) d -> p (o t) d", p=P),
                             X1[v][:, :, :]).then_inc(x1_stored[v], 16)
                sp.wait_ge(xn2_ready, s)
                sp.dma_start(xn_table.rearrange("(p t) d -> p t d", t=NT)[:, bass.ds(TB * (s - 1), TB), :],
                             XN2[v][:, :, :]).then_inc(xn2_stored[v], 16)
            if stats and not (isinstance(s, int) and s + 3 >= B):
                sp.wait_ge(xn_ready, s + 2)
                sp.wait_ge(xb_ready, s + 2)
                load_x(i, c + 3)

        step(0, -1, True, False, False, True)
        step(0, 0, True, True, False, True)
        step(0, 1, True, True, True, True)
        with sp.Fori(1, B // 2 - 2) as i:
            step(i, 0, True, True, True, True)
            step(i, 1, True, True, True, True)
        step(B // 2 - 2, 0, True, True, True, True)
        step(B // 2 - 2, 1, True, True, True, True)
        step(B // 2 - 1, 0, True, True, True, False)
        step(B // 2 - 1, 1, False, True, True, False)
        step(B // 2 - 1, 2, False, False, True, False)
        for u in range(2):
            sp.wait_ge(x1_stored[u], 16 * (B // 2))
            sp.wait_ge(xn2_stored[u], 16 * (B // 2))

    @block.gpsimd
    def _(pool):
        pool.memset(ident[:, :], 0.0).then_inc(pool_const, 1)
        pool.memset(row_pick_f[:, :, :], 0.0).then_inc(pool_const, 1)
        pool.memset(head_rows[:, :], 1.0).then_inc(pool_const, 1)
        pool.memset(minus_half[:, :], -0.5).then_inc(pool_const, 1)
        for u in range(2):
            pool.memset(NM[u][:, :, :], 0.0).then_inc(pool_const, 1)
            pool.memset(VA[u][:, :, :], 1.0).then_inc(pool_const, 1)
        pool.wait_ge(pool_const, 8)
        pool.affine_select(out=ident[:, :], in_=ident[:, :], compare_op=ALU.not_equal, fill=1.0, base=0,
                           pattern=[[-1, P]], channel_multiplier=1).then_inc(pool_const, 1)
        pool.affine_select(out=row_pick_f[:, :, :], in_=row_pick_f[:, :, :], compare_op=ALU.not_equal, fill=1.0,
                           base=0, pattern=[[-1, H], [0, M]], channel_multiplier=1).then_inc(pool_const, 1)
        pool.affine_select(out=head_rows[:, :], in_=head_rows[:, :], compare_op=ALU.is_ge, fill=0.0,
                           base=0, pattern=[[-DH, P // DH]], channel_multiplier=1).then_inc(pool_const, 1)
        pool.wait_ge(pool_const, 11)
        pool.affine_select(out=head_rows[:, :], in_=head_rows[:, :], compare_op=ALU.is_ge, fill=0.0,
                           base=DH - 1, pattern=[[DH, P // DH]], channel_multiplier=-1).then_inc(pool_const, 1)
        pool.wait_ge(pool_const, 12)

        def mask_heads(dst, src, ready):
            hc = P // DH
            for g in range(KD):
                ins = pool.tensor_tensor(
                    dst[:, g * hc:(g + 1) * hc, :],
                    src[:, g:g + 1, :].bitcast(FP32).to_broadcast([P, hc, M]),
                    head_rows[:, :].rearrange("p (a o) -> p a o", o=1).to_broadcast([P, hc, M]), ALU.mult)
            ins.then_inc(ready, 1)

        def step(i, c, prepare, score, finish, stats):
            s, u, v = 2 * i + c, c % 2, (c + 1) % 2
            if prepare:
                pool.wait_ge(stats1_ready, s + 2)
                pool.sem_inc(pool_passed, 1)
                pool.tensor_scalar(ve1[v][:, :], mv1[v][:, :, 1], 1.0, EPS, ALU.mult, ALU.add).then_inc(ve1_ready, 1)
                pool.wait_ge(ve1_ready, s + 2)
                pool.tensor_tensor(rstd1[v][:, :], ve1[v][:, :], minus_half[:, :], ALU.pow).then_inc(rstd1_ready, 1)
                pool.wait_ge(kh_ready, s + 2)
                wait(pool, score_done, NU * s)
                mask_heads(KHZ[v], KH[v], khz_ready)
            if finish:
                pool.wait_ge(stats2_ready, s)
                pool.sem_inc(pool_passed, 1)
                pool.tensor_scalar(ve2[v][:, :], mv2[v][:, :, 1], 1.0 + EPS, EPS * EPS, ALU.mult, ALU.add) \
                    .then_inc(ve2_ready, 1)
                pool.wait_ge(ve2_ready, s)
                pool.tensor_tensor(rstd2[v][:, :], ve2[v][:, :], minus_half[:, :], ALU.pow).then_inc(rstd2_ready, 1)
            if prepare:
                pool.wait_ge(kl_ready, s + 2)
                mask_heads(KLZ[v], KL[v], klz_ready)
                if finish:
                    pool.wait_ge(x1_ready, s)
                if isinstance(s, int) and s == -1:
                    pool.wait_ge(w_loaded, 16 * 8)
                pool.tensor_tensor(XB[v][:, :, :], X[v][:, :, :],
                                   bp_sb[:, :].rearrange("p (o d) -> p o d", o=1).to_broadcast([P, TB, D]),
                                   ALU.add).then_inc(xb_ready, 1)

        run(pool, step)

    @block.scalar
    def _(act):
        def step(i, c, prepare, score, finish, stats):
            s, u, v = 2 * i + c, c % 2, (c + 1) % 2

            def exp(j):
                if not score:
                    return
                act.wait_ge(score_done, NU * s + j + 1)
                wait(act, pv_done, NU * (s - 2) + j + 1)
                act.activation(PT[u][0:M, SU * j:SU * (j + 1), :], score_bank[j % 3][0:M, :], ACT.Exp, scale=SCALE) \
                    .then_inc(exp_ready, 1)

            if prepare:
                act.wait_ge(kv_done, s + 2)
                wait(act, khz_ready, s)
                act.activation(KH[v][:, :, :], misc[:, 0:KD * M], ACT.Copy).then_inc(kh_ready, 1)
                wait(act, pv_done, NU * s)
                act.activation(VA[v][0:M, :, 0:DH], misc[0:M, KD * M:KD * M + D], ACT.Copy).then_inc(va_ready, 1)
            exp(0)
            exp(1)
            if prepare:
                act.wait_ge(xnT_done, s + 2)
                act.activation(XNT[v][:, :, :], misc[:, :], ACT.Copy).then_inc(xnT_ready, 1)
            exp(2)
            if finish:
                act.wait_ge(oT_done, s)
                act.activation(OT[v][:, :, :], misc[:, :], ACT.Copy).then_inc(oT_ready, 1)
            exp(3)
            if prepare:
                act.wait_ge(q_done, s + 2)
                act.activation(QH[v][:, :, :], misc[:, :], ACT.Copy).then_inc(qh_ready, 1)
            exp(4)
            exp(5)
            if finish:
                act.wait_ge(xn2T_done, s)
                for k in range(KD):
                    ins = act.activation(XN2T[v][:, k, :], misc[:, k * S:(k + 1) * S], ACT.Copy, scale=nw_sb[:, k:k + 1])
                ins.then_inc(xn2T_ready, 1)
            exp(6)
            exp(7)
            if prepare:
                act.wait_ge(nmT_done, s + 2)
                act.activation(NMT[v][:, :], misc[:, 0:S], ACT.Copy).then_inc(nmT_ready, 1)

        run(act, step)

    @block.vector
    def _(dve):
        dve.wait_ge(pool_const, 12)
        dve.tensor_copy(row_pick[:, :, :], row_pick_f[:, :, :]).then_inc(const_ready, 1)

        def stats1(i, c):
            b, u = 2 * i + c, c % 2
            dve.wait_ge(x_loaded[u], 16 * (i + c // 2 + 1))
            for t in range(TB):
                dve.bn_stats(bn1[u][:, t, :], X[u][:, t, :]).then_inc(stats1_a, 1)
            dve.wait_ge(stats1_a, TB * (b + 1))
            dve.sem_inc(dve_passed, 1)
            for t in range(TB):
                ins = dve.bn_aggr(mv1[u][:, t, :], bn1[u][:, t, :])
            ins.then_inc(stats1_ready, 1)

        def step(i, c, prepare, score, finish, stats):
            s, u, v = 2 * i + c, c % 2, (c + 1) % 2

            def row_max(q):
                t, hq = q // (H // MU), q % (H // MU)
                dve.wait_ge(smax_done, NQ * (s + 1) + q + 1)
                dve.tensor_reduce(NM[v][:, t, MU * hq:MU * (hq + 1)],
                                  smax_bank[q % 2][:, 0:MU * M].rearrange("p (h m) -> p h m", m=M),
                                  axis=AX.X, op=ALU.max, negate=True).then_inc(max_ready, 1)

            if finish:
                dve.wait_ge(pv_done, NU * s)
                pv = [pv_bank[t][:, 0:H * HV].rearrange("p (h e) -> p h e", e=HV) for t in range(TB)]
                for t in range(TB):
                    dve.reciprocal(RS[v][:, t, :], pv[t][:, :, DH]).then_inc(rs_ready, 1)
                dve.wait_ge(rs_ready, TB * s)
                for t in range(TB):
                    ins = dve.tensor_tensor(
                        ON[v][:, t, :].rearrange("p (h e) -> p h e", e=DH), pv[t][:, :, 0:DH],
                        RS[v][:, t, :].rearrange("p (h o) -> p h o", o=1).to_broadcast([P, H, DH]), ALU.mult)
                ins.then_inc(on_ready, 1)
            if prepare:
                dve.wait_ge(rstd1_ready, s + 2)
                for t in range(TB):
                    ins = dve.tensor_scalar(XN[v][:, t, :], X[v][:, t, :], mv1[v][:, t, 0:1], rstd1[v][:, t:t + 1],
                                            ALU.subtract, ALU.mult)
                ins.then_inc(xn_ready, 1)
                dve.wait_ge(va_ready, s + 2)
                wait(dve, klz_ready, s)
                dve.tensor_tensor(KL[v][:, :, :], misc[:, 0:KD * M].rearrange("p (k m) -> p k m", m=M),
                                  KH[v][:, :, :].bitcast(FP32), ALU.subtract).then_inc(kl_ready, 1)
                dve.wait_ge(qh_ready, s + 2)
                dve.tensor_tensor(QL[v][:, :, :], misc[:, :].rearrange("p (k m) -> p k m", m=S),
                                  QH[v][:, :, :].bitcast(FP32), ALU.subtract).then_inc(ql_ready, 1)
            if finish:
                dve.wait_ge(proj_done, s)
                dve.wait_ge(xb_ready, s)
                if not isinstance(s, int) or s >= 3:
                    dve.wait_ge(x1_stored[v], 16 * (i + (c - 1) // 2))
                dve.tensor_tensor(X1[v][:, :, :], misc[:, :].rearrange("p (t d) -> p t d", d=D), XB[v][:, :, :],
                                  ALU.add).then_inc(x1_ready, 1)
                dve.wait_ge(x1_ready, s)
                for t in range(TB):
                    dve.bn_stats(bn2[v][:, t, :], X1[v][:, t, :]).then_inc(stats2_a, 1)
                dve.wait_ge(stats2_a, TB * s)
                dve.sem_inc(dve_passed, 1)
                for t in range(TB):
                    ins = dve.bn_aggr(mv2[v][:, t, :], bn2[v][:, t, :])
                ins.then_inc(stats2_ready, 1)
            if prepare:
                row_max(0)
                row_max(1)
            if finish:
                dve.wait_ge(rstd2_ready, s)
                if not isinstance(s, int) or s >= 3:
                    dve.wait_ge(xn2_stored[v], 16 * (i + (c - 1) // 2))
                for t in range(TB):
                    ins = dve.tensor_scalar(XN2[v][:, t, :], X1[v][:, t, :], mv2[v][:, t, 0:1], rstd2[v][:, t:t + 1],
                                            ALU.subtract, ALU.mult)
                ins.then_inc(xn2_ready, 1)
            if prepare:
                for q in range(2, NQ):
                    row_max(q)
            if finish:
                dve.wait_ge(logit_done, s)
                dve.tensor_tensor(L[:, bass.ds(TB * (s - 1), TB), :], misc[:, 0:TB * E].rearrange("p (t e) -> p t e", e=E),
                                  rb_sb[:, :].rearrange("p (o e) -> p o e", o=1).to_broadcast([P, TB, E]),
                                  ALU.add).then_inc(logit_ready, 1)
            if stats:
                stats1(i, c + 2)

        stats1(0, 0)
        run(dve, step)

    @block.tensor
    def _(pe):
        pe.wait_ge(const_ready, 1)
        pe.wait_ge(w_loaded, 16 * 8)

        def step(i, c, prepare, score, finish, stats):
            s, u, v = 2 * i + c, c % 2, (c + 1) % 2

            def keys_values():
                if not prepare:
                    return
                pe.wait_ge(ctx_loaded[v], 16 * (i + (c + 1) // 2 + 1))
                wait(pe, nmT_ready, s + 1)
                wait(pe, logit_ready, s - 1)
                for g in range(KD):
                    for k in range(KD):
                        pe.matmul(misc[:, g * M:(g + 1) * M], wk_sb[:, k, g * P:(g + 1) * P], CTX[v][:, k, :],
                                  start=k == 0, stop=k == KD - 1)
                for k in range(KD):
                    ins = pe.matmul(misc[0:M, KD * M:KD * M + D], CTX[v][:, k, :], wv_sb[:, k, :],
                                    start=k == 0, stop=k == KD - 1)
                ins.then_inc(kv_done, 1)

            def transpose_rows(src, done):
                for k in range(KD):
                    for t in range(TB):
                        ins = pe.transpose(misc[:, k * S + t * P:k * S + (t + 1) * P], src[:, t, k * P:(k + 1) * P],
                                           ident[:, :])
                ins.then_inc(done, 1)

            def scores(j):
                if not score:
                    return
                if j == 0:
                    pe.wait_ge(nmT_ready, s + 1)
                    pe.wait_ge(klz_ready, s + 1)
                    pe.wait_ge(ql_ready, s + 1)
                wait(pe, exp_ready, NU * s + j + 1 - BACK[min(j, 3)])
                for r in range(SU):
                    h = SU * j + r
                    g = h // (P // DH)
                    o = score_bank[j % 3][0:M, r * S:(r + 1) * S]
                    pe.matmul(o, row_pick[:, h, :], NMT[u][:, :], start=True, stop=False)
                    pe.matmul(o, KHZ[u][:, h, :], QH[u][:, g, :], start=False, stop=False)
                    pe.matmul(o, KHZ[u][:, h, :], QL[u][:, g, :], start=False, stop=False)
                    ins = pe.matmul(o, KLZ[u][:, h, :], QH[u][:, g, :], start=False, stop=True)
                ins.then_inc(score_done, 1)

            def weigh(j):
                if not score:
                    return
                if j == 0:
                    wait(pe, on_ready, s)
                    pe.wait_ge(va_ready, s + 1)
                pe.wait_ge(exp_ready, NU * s + j + 1)
                for h in range(SU * j, SU * (j + 1)):
                    for t in range(TB):
                        ins = pe.matmul(pv_bank[t][:, h * HV:(h + 1) * HV], PT[u][0:M, h, t * P:(t + 1) * P],
                                        VA[u][0:M, h, :], start=True, stop=True)
                ins.then_inc(pv_done, 1)

            def max_scores(q):
                if not prepare:
                    return
                t, hq = q // (H // MU), q % (H // MU)
                if q == 0:
                    pe.wait_ge(qh_ready, s + 2)
                    pe.wait_ge(khz_ready, s + 2)
                wait(pe, max_ready, NQ * (s + 1) + q - 1)
                pe.matmul(smax_bank[q % 2][:, 0:MU * M], QH[v][:, MU * hq // (P // DH), t * P:(t + 1) * P],
                          KHZ[v][:, MU * hq:MU * (hq + 1), :], start=True, stop=True).then_inc(smax_done, 1)

            keys_values()
            scores(0)
            scores(1)
            if prepare:
                pe.wait_ge(xn_ready, s + 2)
                pe.wait_ge(va_ready, s + 2)
                pe.wait_ge(kl_ready, s + 2)
                transpose_rows(XN[v], xnT_done)
            scores(2)
            weigh(0)
            if finish:
                pe.wait_ge(on_ready, s)
                if prepare:
                    pe.wait_ge(xnT_ready, s + 2)
                else:
                    pe.wait_ge(logit_ready, s - 1)
                transpose_rows(ON[v], oT_done)
            scores(3)
            weigh(1)
            if prepare:
                pe.wait_ge(xnT_ready, s + 2)
                if finish:
                    pe.wait_ge(oT_ready, s)
                for g in range(KD):
                    for k in range(KD):
                        ins = pe.matmul(misc[:, g * S:(g + 1) * S], wq_sb[:, k, g * P:(g + 1) * P], XNT[v][:, k, :],
                                        start=k == 0, stop=k == KD - 1)
                ins.then_inc(q_done, 1)
            scores(4)
            weigh(2)
            if finish:
                pe.wait_ge(oT_ready, s)
                if prepare:
                    pe.wait_ge(ql_ready, s + 2)
                for t in range(TB):
                    for k in range(KD):
                        ins = pe.matmul(misc[:, t * D:(t + 1) * D], OT[v][:, k, t * P:(t + 1) * P], wp_sb[:, k, :],
                                        start=k == 0, stop=k == KD - 1)
                ins.then_inc(proj_done, 1)
            scores(5)
            weigh(3)
            max_scores(0)
            max_scores(1)
            scores(6)
            weigh(4)
            if finish:
                pe.wait_ge(xn2_ready, s)
                transpose_rows(XN2[v], xn2T_done)
            max_scores(2)
            max_scores(3)
            scores(7)
            weigh(5)
            max_scores(4)
            max_scores(5)
            if finish:
                pe.wait_ge(xn2T_ready, s)
                for t in range(TB):
                    for k in range(KD):
                        ins = pe.matmul(misc[:, t * E:(t + 1) * E], XN2T[v][:, k, t * P:(t + 1) * P], rw_sb[:, k, :],
                                        start=k == 0, stop=k == KD - 1)
                ins.then_inc(logit_done, 1)
            weigh(6)
            max_scores(6)
            max_scores(7)
            weigh(7)
            if prepare:
                pe.wait_ge(max_ready, NQ * (s + 2))
                if finish:
                    pe.wait_ge(logit_ready, s)
                else:
                    pe.wait_ge(ql_ready, s + 2)
                for t in range(TB):
                    ins = pe.transpose(misc[:, t * P:(t + 1) * P], NM[v][:, t, :], ident[:, :])
                ins.then_inc(nmT_done, 1)

        run(pe, step)


def routing_phase(nc, ctx, sem, bank, ident, L, idx_in, idx_out, gate_table):
    def sb(name, shape, dt):
        return ctx.enter_context(nc.sbuf_tensor(name, shape, dt))

    LT = sb("LT", [P, CT], FP32)
    LP = sb("LP", [P, TC, NC * E], FP32)
    junk = sb("junk", [P, CT], FP32)
    eq = sb("eq", [P, CT], FP32)
    gt = sb("gt", [P, CT], FP32)
    zero_row = sb("zero_row", [P, CT], FP32)
    prefix = sb("prefix", [P, CT], FP32)
    chosen = sb("chosen", [P, CT], FP32)
    slot = sb("slot", [P, CT], FP32)
    same_e = sb("same_e", [P, P], FP32)
    same_e_below = sb("same_e_below", [P, P], FP32)
    ge_mod = sb("ge_mod", [P, P], FP32)
    prior, cand, mask_x, bit, taken = (sb(n, [P, 1], U32) for n in ("prior", "cand", "mask_x", "bit", "taken"))
    prior_i = sb("prior_i", [P, 1], I32)
    counts = sb("counts", [P, 2], FP32)
    need = sb("need", [P, 8], FP32)

    mx, sm, rsm = (sb(n, [P, NT], FP32) for n in ("mx", "sm", "rsm"))
    probs = sb("probs", [P, NT, E], FP32)
    expl = sb("expl", [P, NT, E], FP32)
    slot_t = sb("slot_t", [P, NT, E], I32)
    slot_a_i, slot_b_i = sb("slot_a_i", [P, NT, E], I32), sb("slot_b_i", [P, NT, E], I32)
    slot_a, slot_b = sb("slot_a", [P, NT, E], BF16), sb("slot_b", [P, NT, E], BF16)
    taken_f = sb("taken_f", [P, NT, E], FP32)
    gates = sb("gates", [P, NT, E], FP32)
    p_col = sb("p_col", [P, 1], FP32)
    t_val = sb("t_val", [P, NT, EG], BF16)
    hot_a = sb("hot_a", [P, SA, NT * EG], BF16)
    hot_b = sb("hot_b", [P, SB, NT * EG], BF16)
    val_b = sb("val_b", [P, 2, SB, NT * EG], BF16)
    pt = [sb(f"pt{g}", [P, 2, SB], FP32) for g in range(E // EG)]
    ids = [sb(f"ids{g}", [P, 2, SB], I32) for g in range(E // EG)]

    logits_t = bank[0:2]
    cnt_bank = bank[2]
    slots_t = bank[3:5]
    idx_bank = bank[5:7]

    consts = sem("consts")
    cvt = sem("cvt")
    lp_ready, lt_done = sem("lp_ready"), sem("lt_done")
    step_dve = sem("step_dve")
    count_ready, total_done = sem("count_ready"), sem("total_done")
    mx_ready, lx_ready, ex_ready = sem("mx_ready"), sem("lx_ready"), sem("ex_ready")
    slot_ready, slotT_done = sem("slot_ready"), sem("slotT_done")
    hot_ready, idx_done, ids_ready = sem("hot_ready"), sem("idx_done"), sem("ids_ready")
    gates_ready = sem("gates_ready")
    gates_stored, ids_moved = sem("gates_stored"), sem("ids_moved")

    block = ctx.enter_context(nc.Block())

    @block.gpsimd
    def _(pool):
        pool.memset(same_e[:, :], 0.0).then_inc(consts, 1)
        pool.memset(zero_row[:, :], 0.0).then_inc(consts, 1)
        pool.iota(p_col[:, :], pattern=[[0, 1]], base=0, channel_multiplier=1,
                  allow_small_or_imprecise_dtypes=True).then_inc(consts, 1)
        pool.iota(t_val[:, :, :], pattern=[[1, NT], [0, EG]], base=0, channel_multiplier=0,
                  allow_small_or_imprecise_dtypes=True).then_inc(consts, 1)
        n = 4
        for k in range(-(NC - 1), NC):
            pool.wait_ge(consts, n)
            pool.affine_select(out=same_e[:, :], in_=same_e[:, :], compare_op=ALU.not_equal, fill=1.0, base=k * E,
                               pattern=[[-1, P]], channel_multiplier=1).then_inc(consts, 1)
            n += 1
        pool.wait_ge(consts, n)
        pool.affine_select(out=same_e_below[:, :], in_=same_e[:, :], compare_op=ALU.is_gt, fill=0.0, base=0,
                           pattern=[[1, P]], channel_multiplier=-1).then_inc(consts, 1)

    n_consts = 4 + 2 * NC - 1 + 1

    @block.scalar
    def _(act):
        act.wait_ge(lx_ready, 1)
        act.activation(expl[:, :, :], expl[:, :, :], ACT.Exp).then_inc(ex_ready, 1)

    @block.vector
    def _(dve):
        n = [0]

        def then(ins):
            n[0] += 1
            ins.then_inc(step_dve, 1)
            dve.wait_ge(step_dve, n[0])

        dve.tensor_copy(LP[:, :, :].rearrange("p j (c e) -> p j c e", e=E),
                        L[:, :, :].rearrange("p (c j) e -> p j c e", j=TC)).then_inc(lp_ready, 1)
        dve.wait_ge(lt_done, 1)
        for j in range(2):
            ins = dve.tensor_copy(LT[:, 512 * j:512 * (j + 1)], logits_t[j][:, :])
        then(ins)
        dve.wait_ge(consts, n_consts)

        dve.tensor_scalar(junk[:, :], LT[:, :], 0.0, None, ALU.is_ge, ALU.add, accum_out=counts[:, 0:1]) \
            .then_inc(count_ready, 1)
        dve.wait_ge(total_done, 1)
        then(dve.tensor_scalar(prior_i[:, :], cnt_bank[:, 0:1], GMAX, None, ALU.is_ge))
        then(dve.tensor_scalar(prior[:, :], prior_i[:, :].bitcast(U32), 31, None, ALU.logical_shift_left))
        then(dve.tensor_scalar(prior_i[:, :], prior[:, :].bitcast(I32), 31, None, ALU.arith_shift_right))
        then(dve.memset(bit[:, :], 1 << 30))
        then(dve.memset(taken[:, :], 0x80000000))
        then(dve.tensor_scalar(cand[:, :], prior_i[:, :].bitcast(U32), 0xFFFFFFFF, None, ALU.bitwise_xor))
        then(dve.tensor_tensor(mask_x[:, :], cand[:, :], taken[:, :], ALU.bitwise_or))
        base = n[0]
        with dve.Fori(0, 31) as i:
            dve.tensor_tensor(cand[:, :], prior[:, :], bit[:, :], ALU.bitwise_or).then_inc(step_dve, 1)
            dve.wait_ge(step_dve, 5 * i + (base + 1))
            dve.tensor_tensor(cand[:, :], cand[:, :], mask_x[:, :], ALU.bitwise_xor).then_inc(step_dve, 1)
            dve.wait_ge(step_dve, 5 * i + (base + 2))
            dve.tensor_scalar(junk[:, :], LT[:, :], cand[:, :].bitcast(FP32), None, ALU.is_ge, ALU.add,
                              accum_out=counts[:, 0:1]).then_inc(count_ready, 1)
            dve.wait_ge(total_done, i + 2)
            dve.tensor_scalar(taken[:, :], cnt_bank[:, 0:1], GMAX, bit[:, :], ALU.is_ge, ALU.mult).then_inc(step_dve, 1)
            dve.wait_ge(step_dve, 5 * i + (base + 3))
            dve.tensor_tensor(prior[:, :], prior[:, :], taken[:, :], ALU.bitwise_or).then_inc(step_dve, 1)
            dve.tensor_scalar(bit[:, :], bit[:, :], 1, None, ALU.logical_shift_right).then_inc(step_dve, 1)
            dve.wait_ge(step_dve, 5 * i + (base + 5))
        n[0] = base + 5 * 31
        then(dve.tensor_tensor(cand[:, :], prior[:, :], mask_x[:, :], ALU.bitwise_xor))
        thr = cand[:, :].bitcast(FP32)
        dve.tensor_scalar(gt[:, :], LT[:, :], thr, None, ALU.is_gt, ALU.add, accum_out=counts[:, 0:1]) \
            .then_inc(step_dve, 1)
        dve.tensor_scalar(eq[:, :], LT[:, :], thr, None, ALU.is_equal, ALU.add, accum_out=counts[:, 1:2]) \
            .then_inc(step_dve, 1)
        n[0] += 2
        dve.wait_ge(step_dve, n[0])
        dve.sem_inc(count_ready, 1)
        dve.wait_ge(total_done, 33)
        then(dve.tensor_copy(need[:, 0:4], cnt_bank[:, 0:4]))
        then(dve.tensor_scalar(need[:, 4:5], need[:, 0:1], -1.0, float(CAP), ALU.mult, ALU.add))
        then(dve.tensor_tensor(need[:, 5:6], need[:, 3:4], need[:, 4:5], ALU.min))
        then(dve.tensor_tensor(need[:, 6:7], need[:, 5:6], need[:, 2:3], ALU.add))
        then(dve.tensor_tensor_scan(prefix[:, :], eq[:, :], zero_row[:, :], need[:, 3:4], ALU.add, ALU.add))
        then(dve.tensor_scalar(junk[:, :], prefix[:, :], need[:, 4:5], None, ALU.is_le))
        then(dve.tensor_tensor(eq[:, :], eq[:, :], junk[:, :], ALU.mult))
        then(dve.tensor_tensor(chosen[:, :], gt[:, :], eq[:, :], ALU.add))
        then(dve.tensor_tensor_scan(prefix[:, :], chosen[:, :], zero_row[:, :], need[:, 6:7], ALU.add, ALU.add))
        then(dve.tensor_tensor(slot[:, :], prefix[:, :], chosen[:, :], ALU.mult))
        dve.tensor_scalar(slot[:, :], slot[:, :], -1.0, None, ALU.add).then_inc(slot_ready, 1)

        then(dve.tensor_reduce(mx[:, :], L[:, :, :], axis=AX.X, op=ALU.max))
        dve.tensor_tensor(expl[:, :, :], L[:, :, :],
                          mx[:, :].rearrange("p (t o) -> p t o", o=1).to_broadcast([P, NT, E]),
                          ALU.subtract).then_inc(lx_ready, 1)
        dve.wait_ge(slotT_done, 1)
        for j in range(TC):
            ins = dve.tensor_copy(slot_t[:, j::TC, :],
                                  slots_t[j // 4][:, P * (j % 4):P * (j % 4 + 1)].rearrange("p (c e) -> p c e", e=E))
        then(ins)
        dve.tensor_scalar(slot_a_i[:, :, :], slot_t[:, :, :], 4, None, ALU.arith_shift_right).then_inc(cvt, 1)
        dve.tensor_scalar(slot_b_i[:, :, :], slot_t[:, :, :], SB - 1, None, ALU.bitwise_and).then_inc(cvt, 1)
        dve.wait_ge(cvt, 2)
        dve.tensor_copy(slot_a[:, :, :], slot_a_i[:, :, :]).then_inc(cvt, 1)
        dve.tensor_copy(slot_b[:, :, :], slot_b_i[:, :, :]).then_inc(cvt, 1)
        dve.tensor_scalar(taken_f[:, :, :], slot_t[:, :, :], 0.0, None, ALU.is_ge).then_inc(cvt, 1)
        dve.wait_ge(cvt, 5)

        dve.wait_ge(ex_ready, 1)
        then(dve.tensor_reduce(sm[:, :], expl[:, :, :], axis=AX.X, op=ALU.add))
        then(dve.reciprocal(rsm[:, :], sm[:, :]))

        def along_e(a):
            return a[:, :].rearrange("p (t o) -> p t o", o=1).to_broadcast([P, NT, E])

        then(dve.tensor_tensor(probs[:, :, :], expl[:, :, :], along_e(rsm), ALU.mult))
        then(dve.tensor_tensor(gates[:, :, :], probs[:, :, :], taken_f[:, :, :], ALU.mult))
        then(dve.tensor_reduce(sm[:, :], gates[:, :, :], axis=AX.X, op=ALU.add))
        then(dve.tensor_scalar(mx[:, :], sm[:, :], 0.0, None, ALU.is_equal))
        then(dve.tensor_tensor(sm[:, :], sm[:, :], mx[:, :], ALU.add))
        then(dve.reciprocal(rsm[:, :], sm[:, :]))
        dve.tensor_tensor(gates[:, :, :], probs[:, :, :], along_e(rsm), ALU.mult).then_inc(gates_ready, 1)

        def hot(g):
            es = slice(EG * g, EG * (g + 1))
            if g:
                dve.wait_ge(idx_done, g)
            for a in range(SA):
                dve.tensor_scalar(hot_a[:, a, :].rearrange("p (t e) -> p t e", e=EG), slot_a[:, :, es], float(a), None,
                                  ALU.is_equal)
            for b in range(SB):
                dve.tensor_scalar(hot_b[:, b, :].rearrange("p (t e) -> p t e", e=EG), slot_b[:, :, es], float(b), None,
                                  ALU.is_equal).then_inc(step_dve, 1)
                dve.tensor_scalar(val_b[:, 0, b, :].rearrange("p (t e) -> p t e", e=EG), slot_b[:, :, es], float(b),
                                  p_col[:, :], ALU.is_equal, ALU.mult)
            n[0] += SB
            dve.wait_ge(step_dve, n[0])
            dve.tensor_tensor(val_b[:, 1, :, :], hot_b[:, :, :],
                              t_val[:, :, :].rearrange("p (o t) e -> p o (t e)", o=1).to_broadcast([P, SB, NT * EG]),
                              ALU.mult).then_inc(hot_ready, 1)

        def finish_ids(g):
            dve.wait_ge(idx_done, g + 1)
            then(dve.tensor_copy(pt[g][:, :, :], idx_bank[g % 2][:, 0:2 * SB].rearrange("p (k b) -> p k b", k=2)))
            dve.tensor_scalar(junk[:, 0:SB], pt[g][:, 0, :], float(NT), None, ALU.mult).then_inc(step_dve, 1)
            dve.tensor_scalar(junk[:, SB:2 * SB], pt[g][:, 1, :], float(P), None, ALU.mult).then_inc(step_dve, 1)
            n[0] += 2
            dve.wait_ge(step_dve, n[0])
            dve.tensor_tensor(ids[g][:, 0, :], junk[:, 0:SB], pt[g][:, 1, :], ALU.add).then_inc(ids_ready, 1)
            dve.tensor_tensor(ids[g][:, 1, :], junk[:, SB:2 * SB], pt[g][:, 0, :], ALU.add).then_inc(ids_ready, 1)

        for g in range(E // EG):
            hot(g)
            finish_ids(g)

    @block.tensor
    def _(pe):
        pe.wait_ge(lp_ready, 1)
        for j in range(TC):
            ins = pe.transpose(logits_t[j // 4][:, P * (j % 4):P * (j % 4 + 1)],
                               LP[:, j, :], ident[:, :])
        ins.then_inc(lt_done, 1)
        pe.wait_ge(consts, n_consts)
        pe.wait_ge(count_ready, 1)
        pe.matmul(cnt_bank[:, 0:1], same_e[:, :], counts[:, 0:1], start=True, stop=True).then_inc(total_done, 1)
        with pe.Fori(0, 31) as i:
            pe.wait_ge(count_ready, i + 2)
            pe.matmul(cnt_bank[:, 0:1], same_e[:, :], counts[:, 0:1], start=True, stop=True).then_inc(total_done, 1)
        pe.wait_ge(count_ready, 33)
        pe.matmul(cnt_bank[:, 0:2], same_e[:, :], counts[:, :], start=True, stop=True)
        pe.matmul(cnt_bank[:, 2:4], same_e_below[:, :], counts[:, :], start=True, stop=True).then_inc(total_done, 1)
        pe.wait_ge(slot_ready, 1)
        for j in range(TC):
            ins = pe.transpose(slots_t[j // 4][:, P * (j % 4):P * (j % 4 + 1)], slot[:, P * j:P * (j + 1)], ident[:, :])
        ins.then_inc(slotT_done, 1)
        for g in range(E // EG):
            pe.wait_ge(hot_ready, g + 1)
            if g >= 2:
                pe.wait_ge(ids_ready, 2 * (g - 1))
            for t in range(NT):
                for e in range(EG):
                    ins = pe.matmul(idx_bank[g % 2][SA * e:SA * (e + 1), 0:2 * SB], hot_a[:, :, EG * t + e],
                                    val_b[:, :, :, EG * t + e], start=t == 0, stop=t == NT - 1)
            ins.then_inc(idx_done, 1)

    @block.sync
    def _(sp):
        for g in range(E // EG):
            sp.wait_ge(ids_ready, 2 * (g + 1))
            for e in range(EG):
                for kind, dst in enumerate((idx_in, idx_out)):
                    sp.dma_start(dst[:, EG * g + e, :], ids[g][SA * e:SA * (e + 1), kind, :]) \
                        .then_inc(ids_moved, 16)
            if g == 0:
                sp.wait_ge(gates_ready, 1)
                sp.dma_start(gate_table.rearrange("(p r) o -> p (r o)", p=P), gates[:, :, :].rearrange("p t e -> p (t e)")) \
                    .then_inc(gates_stored, 16)
        sp.wait_ge(ids_moved, 16 * 2 * E)
        sp.wait_ge(gates_stored, 16)


def expert_phase(nc, ctx, sem, bank, ident, idx_in, idx_out, gate_table, xn_table, w1T, b1, w2T, b2, nw, out):
    def sb(name, shape, dt):
        return ctx.enter_context(nc.sbuf_tensor(name, shape, dt))

    def pair(name, shape, dt):
        return [sb(f"{name}{u}", shape, dt) for u in range(2)]

    W1 = pair("W1", [P, KD, F], FP32)
    W2 = pair("W2", [P, KF, D], FP32)
    B2 = pair("B2", [P, D], FP32)
    B1 = sb("B1", [P, E * KF], FP32)
    NW = sb("NW", [P, KD], FP32)
    gate_row = sb("gate_row", [P, E, GT], I32)
    e_off = sb("e_off", [P, E, GT], I32)
    gate_row0 = sb("gate_row0", [P, E, GT], I32)
    II, IG, IO = pair("II", [P, GT], I32), pair("IG", [P, GT], I32), pair("IO", [P, GT], I32)
    XG = pair("XG", [P, GT, D], FP32)
    G = pair("G", [P, GT], FP32)
    XT = pair("XT", [P, KD, CAP], FP32)
    HT = pair("HT", [P, KF, CAP], FP32)
    Y0 = sb("Y0", [P, GT, D], FP32)
    C = pair("C", [P, GT, D], FP32)

    xt_bank = bank[0:2]
    h_bank = bank[2:5]
    y_bank = bank[5:7]

    w_loaded = [sem(f"ew_loaded{u}") for u in range(2)]
    c_loaded = sem("c_loaded")
    e_off_ready, gi_a, gi_ready = sem("e_off_ready"), sem("gi_a"), sem("gi_ready")
    idx_ready, idx_out_ready = sem("idx_ready"), sem("idx_out_ready")
    gathered = [sem(f"gathered{u}") for u in range(2)]
    xt_done, xt_ready = sem("xt_done"), sem("xt_ready")
    h_done, h_ready = sem("h_done"), sem("h_ready")
    y_done, c0_ready, c_ready = sem("y_done"), sem("c0_ready"), sem("c_ready")
    added = sem("added")
    pool_passed = sem("pool_passed_e")

    block = ctx.enter_context(nc.Block())

    @block.sync
    def _(sp):
        sp.dma_start(NW[:, :], nw).then_inc(c_loaded, 16)
        sp.dma_start(B1[:, :], b1).then_inc(c_loaded, 16)

        def load(i, u):
            e = 2 * i + u
            sp.dma_start(W1[u][:, :, :], w1T[bass.ds(e, 1), :, :].rearrange("o (k p) f -> p (o k) f", p=P)) \
                .then_inc(w_loaded[u], 16)
            sp.dma_start(W2[u][:, :, :], w2T[bass.ds(e, 1), :, :].rearrange("o (k p) d -> p (o k) d", p=P)) \
                .then_inc(w_loaded[u], 16)
            sp.dma_start(B2[u][:, :], b2[bass.ds(e, 1), :].to_broadcast([P, D])).then_inc(w_loaded[u], 16)

        load(0, 0)
        load(0, 1)
        with sp.Fori(1, E // 2) as i:
            for u in range(2):
                sp.wait_ge(y_done, 2 * i + (u - 1))
                sp.wait_ge(c0_ready, 2 * i + (u - 1))
                load(i, u)

    @block.gpsimd
    def _(pool):
        pool.iota(e_off[:, :, :], pattern=[[1, E], [0, GT]], base=0, channel_multiplier=0).then_inc(e_off_ready, 1)

        def expert(i, u, first):
            e = 2 * i + u
            pool.wait_ge(idx_ready, e + 1)
            if not first:
                pool.wait_ge(xt_done, e - 1)
                pool.wait_ge(c_ready, e - 1)
            pool.sem_inc(pool_passed, 1)
            for g in range(GT):
                pool.indirect_dma_start(out=XG[u][:, g, :], out_offset=None, in_=xn_table,
                                        in_offset=bass.IndirectOffsetOnAxis(ap=II[u][:, g:g + 1], axis=0)) \
                    .then_inc(gathered[u], 16)
                pool.indirect_dma_start(out=G[u][:, g:g + 1], out_offset=None, in_=gate_table,
                                        in_offset=bass.IndirectOffsetOnAxis(ap=IG[u][:, g:g + 1], axis=0)) \
                    .then_inc(gathered[u], 16)

        def add_up(i, u, first):
            e = 2 * i + u
            pool.wait_ge(c_ready, e + 1)
            if not first:
                pool.wait_ge(added, 16 * GT * e)
            pool.sem_inc(pool_passed, 1)
            for g in range(GT):
                pool.indirect_dma_start(out=out, in_=C[u][:, g, :], in_offset=None, compute_op=ALU.add,
                                        out_offset=bass.IndirectOffsetOnAxis(ap=IO[u][:, g:g + 1], axis=0)) \
                    .then_inc(added, 16)

        expert(0, 0, True)
        expert(0, 1, True)
        add_up(0, 0, True)
        with pool.Fori(1, E // 2) as i:
            expert(i, 0, False)
            add_up(i - 1, 1, False)
            expert(i, 1, False)
            add_up(i, 0, False)
        add_up(E // 2 - 1, 1, False)
        pool.wait_ge(added, 16 * GT * E)

    @block.vector
    def _(dve):
        dve.tensor_scalar(gate_row0[:, :, :], idx_in[:, :, :], float(E), None, ALU.mult).then_inc(gi_a, 1)
        dve.wait_ge(gi_a, 1)
        dve.wait_ge(e_off_ready, 1)
        dve.tensor_tensor(gate_row[:, :, :], gate_row0[:, :, :], e_off[:, :, :], ALU.add).then_inc(gi_ready, 1)
        dve.wait_ge(gi_ready, 1)

        def indices(i, u, first):
            e = 2 * i + u
            if not first:
                dve.wait_ge(gathered[u], 16 * 2 * GT * i)
                dve.wait_ge(added, 16 * GT * (2 * i + u - 1))
            dve.tensor_copy(II[u][:, :], idx_in[:, bass.ds(e, 1), :].rearrange("p o g -> p (o g)"))
            dve.tensor_copy(IG[u][:, :], gate_row[:, bass.ds(e, 1), :].rearrange("p o g -> p (o g)")).then_inc(idx_ready, 1)
            dve.tensor_copy(IO[u][:, :], idx_out[:, bass.ds(e, 1), :].rearrange("p o g -> p (o g)")).then_inc(idx_out_ready, 1)

        def columns(i, u):
            e = 2 * i + u
            dve.wait_ge(xt_done, e + 1)
            for k in range(KD):
                ins = dve.tensor_scalar(XT[u][:, k, :], xt_bank[k][:, :], NW[:, k:k + 1], None, ALU.mult)
            ins.then_inc(xt_ready, 1)

        def contributions(i, u, first=False):
            e = 2 * i + u
            if not first:
                dve.wait_ge(c_ready, e)
                dve.wait_ge(added, 16 * GT * (e - 1))
            dve.wait_ge(y_done, e + 1)
            dve.wait_ge(w_loaded[u], 16 * 3 * (i + 1))
            for j in range(2):
                ins = dve.tensor_tensor(Y0[:, 2 * j:2 * j + 2, :], y_bank[j][:, :].rearrange("p (g d) -> p g d", d=D),
                                        B2[u][:, :].rearrange("p (o d) -> p o d", o=1).to_broadcast([P, 2, D]), ALU.add)
            ins.then_inc(c0_ready, 1)
            dve.wait_ge(c0_ready, e + 1)
            for g in range(GT):
                ins = dve.tensor_scalar(C[u][:, g, :], Y0[:, g, :], G[u][:, g:g + 1], None, ALU.mult)
            ins.then_inc(c_ready, 1)

        dve.wait_ge(c_loaded, 32)
        indices(0, 0, True)
        indices(0, 1, True)
        columns(0, 0)
        columns(0, 1)
        contributions(0, 0, True)
        with dve.Fori(1, E // 2) as i:
            indices(i, 0, False)
            columns(i, 0)
            contributions(i - 1, 1)
            indices(i, 1, False)
            columns(i, 1)
            contributions(i, 0)
        contributions(E // 2 - 1, 1)

    @block.scalar
    def _(act):
        act.wait_ge(c_loaded, 32)

        def hidden(i, u, first):
            if not first:
                act.wait_ge(y_done, 2 * i + (u - 1))
            for f in range(KF):
                act.wait_ge(h_done, KF * (2 * i + u) + (f + 1))
                act.activation(HT[u][:, f, :], h_bank[f % 3][:, :], ACT.Gelu,
                               bias=B1[:, bass.ds(KF * (2 * i + u) + f, 1)]).then_inc(h_ready, 1)

        hidden(0, 0, True)
        hidden(0, 1, True)
        with act.Fori(1, E // 2) as i:
            hidden(i, 0, False)
            hidden(i, 1, False)

    @block.tensor
    def _(pe):
        def columns(i, u, first):
            e = 2 * i + u
            pe.wait_ge(gathered[u], 16 * 2 * GT * (i + 1))
            if not first:
                pe.wait_ge(xt_ready, e)
            for k in range(KD):
                for g in range(GT):
                    ins = pe.transpose(xt_bank[k][:, g * P:(g + 1) * P], XG[u][:, g, k * P:(k + 1) * P], ident[:, :])
            ins.then_inc(xt_done, 1)

        def up(i, u, first):
            e = 2 * i + u
            pe.wait_ge(xt_ready, e + 1)
            pe.wait_ge(w_loaded[u], 16 * 3 * (i + 1))
            for f in range(KF):
                if not first or f >= 3:
                    pe.wait_ge(h_ready, KF * e + (f + 1 - BACK[min(f, 3)]))
                for k in range(KD):
                    ins = pe.matmul(h_bank[f % 3][:, :], W1[u][:, k, f * P:(f + 1) * P], XT[u][:, k, :],
                                    start=k == 0, stop=k == KD - 1)
                ins.then_inc(h_done, 1)

        def down(i, u, first):
            e = 2 * i + u
            if not first:
                pe.wait_ge(c0_ready, e)
            pe.wait_ge(h_ready, KF * (e + 1))
            for g in range(GT):
                for f in range(KF):
                    ins = pe.matmul(y_bank[g // 2][:, (g % 2) * D:(g % 2 + 1) * D], HT[u][:, f, g * P:(g + 1) * P],
                                    W2[u][:, f, :], start=f == 0, stop=f == KF - 1)
            ins.then_inc(y_done, 1)

        columns(0, 0, True)
        up(0, 0, True)
        columns(0, 1, False)
        up(0, 1, False)
        down(0, 0, True)
        with pe.Fori(1, E // 2) as i:
            columns(i, 0, False)
            up(i, 0, False)
            down(i - 1, 1, False)
            columns(i, 1, False)
            up(i, 1, False)
            down(i, 0, False)
        down(E // 2 - 1, 1, False)


def program(nc, x, ctxT, wq, wk, wv, wp, bp, nw, rw, rb, w1T, b1, w2T, b2, out):
    xn_table = nc.dram_tensor("xn_table", [N, D], FP32, kind="Internal").ap()
    gate_table = nc.dram_tensor("gate_table", [N * E, 1], FP32, kind="Internal").ap()
    with ExitStack() as ctx:
        def sem(name):
            return ctx.enter_context(nc.semaphore(name))

        bank = [ctx.enter_context(nc.psum_tensor(f"bank{n}", [P, 512], FP32)) for n in range(8)]
        ident = ctx.enter_context(nc.sbuf_tensor("ident", [P, P], FP32))
        L = ctx.enter_context(nc.sbuf_tensor("L", [P, NT, E], FP32))
        idx_in = ctx.enter_context(nc.sbuf_tensor("idx_in", [P, E, GT], I32))
        idx_out = ctx.enter_context(nc.sbuf_tensor("idx_out", [P, E, GT], I32))
        with ExitStack() as phase:
            attention_phase(nc, phase, sem, bank, ident, L, x, ctxT, wq, wk, wv, wp, bp, nw, rw, rb, out, xn_table)
        with ExitStack() as phase:
            routing_phase(nc, phase, sem, bank, ident, L, idx_in, idx_out, gate_table)
        with ExitStack() as phase:
            expert_phase(nc, phase, sem, bank, ident, idx_in, idx_out, gate_table, xn_table, w1T, b1, w2T, b2, nw,
                         out.rearrange("b s d -> (b s) d"))


def kernel(**inputs):
    import numpy as np
    import concourse.bacc as bacc
    from concourse.bass_utils import run_bass_kernel_spmd

    t = np.ascontiguousarray
    laid = {
        "x": t(inputs["x"]),
        "ctxT": t(np.transpose(inputs["ctx_1024"], (0, 2, 1))),
        "wq": t(inputs["L0_xattn_Wq"]), "wk": t(inputs["L0_xattn_Wk"]),
        "wv": t(inputs["L0_xattn_Wv"]), "wp": t(inputs["L0_xattn_Wp"]), "bp": t(inputs["L0_xattn_bp"]),
        "nw": t(np.transpose(np.reshape(inputs["L0_ffn_norm_weight"], (KD, P)))),
        "rw": t(np.transpose(inputs["L0_ffn_router_weight"])), "rb": t(inputs["L0_ffn_router_bias"]),
        "w1T": t(np.transpose(inputs["L0_ffn_fc1_weight"], (0, 2, 1))),
        "b1": t(np.transpose(np.reshape(inputs["L0_ffn_fc1_bias"], (E * KF, P)))),
        "w2T": t(np.transpose(inputs["L0_ffn_fc2_weight"], (0, 2, 1))),
        "b2": t(inputs["L0_ffn_fc2_bias"]),
    }
    nc = bacc.Bacc("TRN2", target_bir_lowering=False, num_devices=1)
    args = [nc.dram_tensor(f"{name}_dram", a.shape, mybir.dt.from_np(a.dtype), kind="ExternalInput").ap()
            for name, a in laid.items()]
    out = nc.dram_tensor("out_dram", (B, S, D), FP32, kind="ExternalOutput").ap()
    program(nc, *args, out)
    r = run_bass_kernel_spmd(nc, [{f"{name}_dram": a for name, a in laid.items()}], core_ids=[0])
    return r.results[0]["out_dram"]
```

```python
import concourse.bass as bass
from concourse import mybir
from contextlib import ExitStack

FP32 = mybir.dt.float32
FP32R = mybir.dt.float32r
BF16 = mybir.dt.bfloat16
I32 = mybir.dt.int32
U32 = mybir.dt.uint32
ALU = mybir.AluOpType
ACT = mybir.ActivationFunctionType
AX = mybir.AxisListType

P = 128
B, S, D = 32, 256, 256
M = 120
H, DH = 16, 16
KD = D // P
TB = S // P
N = B * S
NT = N // P
E = 16
F = 1024
KF = F // P
CAP = N // E
NC = 8
CT = N // NC
TC = NT // NC
GT = CAP // P
EG = 4
SA, SB = 32, 16
EPS = 1e-5
SCALE = DH ** -0.5
SU = 2
NU = H // SU
NP = H // 4
MU = 4
NQ = TB * H // MU
GMAX = float(CAP) - 0.5
BACK = (2, 2, 5, 3)


def attention_phase(nc, ctx, sem, bank, ident, L, x, ctxT, wq, wk, wv, wp, bp, nw, rw, rb, out, xn_table):
    def sb(name, shape, dt):
        return ctx.enter_context(nc.sbuf_tensor(name, shape, dt))

    def pair(name, shape, dt):
        return [sb(f"{name}{u}", shape, dt) for u in range(2)]

    wq_sb, wk_sb, wv_sb, wp_sb = (sb(n, [P, KD, D], FP32) for n in ("wq_sb", "wk_sb", "wv_sb", "wp_sb"))
    bp_sb = sb("bp_sb", [P, D], FP32)
    nw_sb = sb("nw_sb", [P, KD], FP32)
    rw_sb = sb("rw_sb", [P, KD, E], FP32)
    rb_sb = sb("rb_sb", [P, E], FP32)
    head_rows = sb("head_rows", [P, P // DH], FP32)
    row_pick_f = sb("row_pick_f", [P, H, M], FP32)
    row_pick = sb("row_pick", [P, H, M], FP32R)
    minus_half = sb("minus_half", [P, TB], FP32)

    X = pair("X", [P, TB, D], FP32)
    XB = pair("XB", [P, TB, D], FP32)
    CTX = pair("CTX", [P, KD, M], FP32)
    bn1, mv1, rstd1 = pair("bn1", [P, TB, 6], FP32), pair("mv1", [P, TB, 2], FP32), pair("rstd1", [P, TB], FP32)
    ve1 = pair("ve1", [P, TB], FP32)
    XN = pair("XN", [P, TB, D], FP32)
    XNT = pair("XNT", [P, KD, S], FP32)
    QH, QL = pair("QH", [P, KD, S], FP32R), pair("QL", [P, KD, S], FP32R)
    KH, KL = pair("KH", [P, KD, M], FP32R), pair("KL", [P, KD, M], FP32R)
    KHZ, KLZ = pair("KHZ", [P, H, M], FP32R), pair("KLZ", [P, H, M], FP32R)
    VA = pair("VA", [P, H, 2 * DH], FP32)
    NM = pair("NM", [P, TB, P], FP32)
    NMT = pair("NMT", [P, S], FP32R)
    PT = pair("PT", [P, H, S], FP32)
    PVS = sb("PVS", [P, 2, 2 * S], FP32)
    RS = pair("RS", [P, TB, H], FP32)
    ON = pair("ON", [P, TB, D], FP32)
    OT = pair("OT", [P, KD, S], FP32)
    X1 = pair("X1", [P, TB, D], FP32)
    bn2, mv2, rstd2 = pair("bn2", [P, TB, 6], FP32), pair("mv2", [P, TB, 2], FP32), pair("rstd2", [P, TB], FP32)
    ve2 = pair("ve2", [P, TB], FP32)
    XN2 = pair("XN2", [P, TB, D], FP32)
    XN2T = pair("XN2T", [P, KD, S], FP32)

    smax_bank = bank[0:2]
    score_bank = bank[2:4]
    pv_bank = bank[4:6]
    misc_a, misc_b = bank[6], bank[7]

    w_loaded = sem("w_loaded")
    x_loaded = [sem(f"x_loaded{u}") for u in range(2)]
    ctx_loaded = [sem(f"ctx_loaded{u}") for u in range(2)]
    x1_stored = [sem(f"x1_stored{u}") for u in range(2)]
    xn2_stored = [sem(f"xn2_stored{u}") for u in range(2)]
    pool_const = sem("pool_const")
    const_ready = sem("const_ready")
    stats1_a, stats1_ready = sem("stats1_a"), sem("stats1_ready")
    ve1_ready, rstd1_ready = sem("ve1_ready"), sem("rstd1_ready")
    xn_ready = sem("xn_ready")
    xnT_done, xnT_ready = sem("xnT_done"), sem("xnT_ready")
    q_done, qh_ready, ql_ready = sem("q_done"), sem("qh_ready"), sem("ql_ready")
    k_done, v_done, kh_ready, va_ready, kl_ready = (sem(n) for n in ("k_done", "v_done", "kh_ready", "va_ready", "kl_ready"))
    khz_ready, klz_ready = sem("khz_ready"), sem("klz_ready")
    xb_ready = sem("xb_ready")
    smax_done, max_ready = sem("smax_done"), sem("max_ready")
    nmT_done, nmT_ready = sem("nmT_done"), sem("nmT_ready")
    score_done, exp_ready = sem("score_done"), sem("exp_ready")
    pv_done, pvs_ready, tok_done = sem("pv_done"), sem("pvs_ready"), sem("tok_done")
    rs_ready, on_ready = sem("rs_ready"), sem("on_ready")
    oT_done, oT_ready = sem("oT_done"), sem("oT_ready")
    proj_done, x1_ready = sem("proj_done"), sem("x1_ready")
    stats2_a, stats2_ready = sem("stats2_a"), sem("stats2_ready")
    ve2_ready, rstd2_ready = sem("ve2_ready"), sem("rstd2_ready")
    xn2_ready = sem("xn2_ready")
    xn2T_done, xn2T_ready = sem("xn2T_done"), sem("xn2T_ready")
    logit_done, logit_ready = sem("logit_done"), sem("logit_ready")

    def wait(eng, s, value):
        if not isinstance(value, int) or value > 0:
            eng.wait_ge(s, value)

    def run(eng, step):
        step(0, -2, nxt2=True, nxt1=False, now=False, fin=False)
        step(0, -1, nxt2=True, nxt1=True, now=False, fin=False)
        step(0, 0, nxt2=True, nxt1=True, now=True, fin=False)
        step(0, 1, nxt2=True, nxt1=True, now=True, fin=True)
        with eng.Fori(1, B // 2 - 1) as i:
            step(i, 0, nxt2=True, nxt1=True, now=True, fin=True)
            step(i, 1, nxt2=True, nxt1=True, now=True, fin=True)
        step(B // 2 - 1, 0, nxt2=False, nxt1=True, now=True, fin=True)
        step(B // 2 - 1, 1, nxt2=False, nxt1=False, now=True, fin=True)
        step(B // 2 - 1, 2, nxt2=False, nxt1=False, now=False, fin=True)

    pool_passed, dve_passed = sem("pool_passed"), sem("dve_passed")
    block = ctx.enter_context(nc.Block())

    @block.sync
    def _(sp):
        def load_x(i, c):
            b, u = 2 * i + c, c % 2
            sp.dma_start(X[u][:, :, :], x[bass.ds(b, 1), :, :].rearrange("o (t p) d -> p (o t) d", p=P)) \
                .then_inc(x_loaded[u], 16)

        def load_ctx(i, c):
            b, u = 2 * i + c, c % 2
            sp.dma_start(CTX[u][:, :, :], ctxT[bass.ds(b, 1), :, :].rearrange("o (k p) m -> p (o k) m", p=P)) \
                .then_inc(ctx_loaded[u], 16)

        load_x(0, 0)
        load_ctx(0, 0)
        for t, w in ((wk_sb, wk), (wq_sb, wq), (wv_sb, wv), (wp_sb, wp)):
            sp.dma_start(t[:, :, :], w.rearrange("(k p) c -> p k c", p=P)).then_inc(w_loaded, 16)
        load_x(0, 1)
        load_ctx(0, 1)
        sp.dma_start(bp_sb[:, :], bp.rearrange("(o d) -> o d", o=1).to_broadcast([P, D])).then_inc(w_loaded, 16)
        sp.dma_start(nw_sb[:, :], nw).then_inc(w_loaded, 16)
        sp.dma_start(rw_sb[:, :, :], rw.rearrange("(k p) e -> p k e", p=P)).then_inc(w_loaded, 16)
        sp.dma_start(rb_sb[:, :], rb.rearrange("(o d) -> o d", o=1).to_broadcast([P, E])).then_inc(w_loaded, 16)

        def step(i, c, load, fin):
            s, v = 2 * i + c, (c + 1) % 2
            if load:
                sp.wait_ge(v_done, s + 2)
                load_ctx(i, c + 3)
            if fin:
                sp.wait_ge(x1_ready, s)
                sp.dma_start(out[bass.ds(s - 1, 1), :, :].rearrange("o (t p) d -> p (o t) d", p=P),
                             X1[v][:, :, :]).then_inc(x1_stored[v], 16)
            if load:
                sp.wait_ge(xn_ready, s + 2)
                sp.wait_ge(xb_ready, s + 2)
                load_x(i, c + 3)
            if fin:
                sp.wait_ge(xn2_ready, s)
                sp.dma_start(xn_table.rearrange("(p t) d -> p t d", t=NT)[:, bass.ds(TB * (s - 1), TB), :],
                             XN2[v][:, :, :]).then_inc(xn2_stored[v], 16)

        step(0, -1, True, False)
        step(0, 0, True, False)
        step(0, 1, True, True)
        with sp.Fori(1, B // 2 - 2) as i:
            step(i, 0, True, True)
            step(i, 1, True, True)
        step(B // 2 - 2, 0, True, True)
        for c in range(1, 5):
            step(B // 2 - 2, c, False, True)
        for u in range(2):
            sp.wait_ge(x1_stored[u], 16 * (B // 2))
            sp.wait_ge(xn2_stored[u], 16 * (B // 2))

    @block.gpsimd
    def _(pool):
        pool.memset(ident[:, :], 0.0).then_inc(pool_const, 1)
        pool.memset(row_pick_f[:, :, :], 0.0).then_inc(pool_const, 1)
        pool.memset(head_rows[:, :], 1.0).then_inc(pool_const, 1)
        pool.memset(minus_half[:, :], -0.5).then_inc(pool_const, 1)
        for u in range(2):
            pool.memset(NM[u][:, :, :], 0.0).then_inc(pool_const, 1)
            pool.memset(VA[u][:, :, :], 1.0).then_inc(pool_const, 1)
        pool.wait_ge(pool_const, 8)
        pool.affine_select(out=ident[:, :], in_=ident[:, :], compare_op=ALU.not_equal, fill=1.0, base=0,
                           pattern=[[-1, P]], channel_multiplier=1).then_inc(pool_const, 1)
        pool.affine_select(out=row_pick_f[:, :, :], in_=row_pick_f[:, :, :], compare_op=ALU.not_equal, fill=1.0,
                           base=0, pattern=[[-1, H], [0, M]], channel_multiplier=1).then_inc(pool_const, 1)
        pool.affine_select(out=head_rows[:, :], in_=head_rows[:, :], compare_op=ALU.is_ge, fill=0.0,
                           base=0, pattern=[[-DH, P // DH]], channel_multiplier=1).then_inc(pool_const, 1)
        pool.wait_ge(pool_const, 11)
        pool.affine_select(out=head_rows[:, :], in_=head_rows[:, :], compare_op=ALU.is_ge, fill=0.0,
                           base=DH - 1, pattern=[[DH, P // DH]], channel_multiplier=-1).then_inc(pool_const, 1)
        pool.wait_ge(pool_const, 12)

        def mask_heads(dst, src, ready):
            hc = P // DH
            for g in range(KD):
                ins = pool.tensor_tensor(
                    dst[:, g * hc:(g + 1) * hc, :],
                    src[:, g:g + 1, :].bitcast(FP32).to_broadcast([P, hc, M]),
                    head_rows[:, :].rearrange("p (a o) -> p a o", o=1).to_broadcast([P, hc, M]), ALU.mult)
            ins.then_inc(ready, 1)

        def step(i, c, nxt2, nxt1, now, fin):
            s, u, v = 2 * i + c, c % 2, (c + 1) % 2
            if nxt1:
                pool.wait_ge(kl_ready, s + 2)
                wait(pool, score_done, NU * s)
                mask_heads(KLZ[v], KL[v], klz_ready)
            if fin:
                pool.wait_ge(stats2_ready, s)
                pool.sem_inc(pool_passed, 1)
                pool.tensor_scalar(ve2[v][:, :], mv2[v][:, :, 1], 1.0 + EPS, EPS * EPS, ALU.mult, ALU.add) \
                    .then_inc(ve2_ready, 1)
                pool.wait_ge(ve2_ready, s)
                pool.tensor_tensor(rstd2[v][:, :], ve2[v][:, :], minus_half[:, :], ALU.pow).then_inc(rstd2_ready, 1)
            if nxt2:
                pool.wait_ge(stats1_ready, s + 3)
                pool.sem_inc(pool_passed, 1)
                pool.tensor_scalar(ve1[u][:, :], mv1[u][:, :, 1], 1.0, EPS, ALU.mult, ALU.add).then_inc(ve1_ready, 1)
                pool.wait_ge(ve1_ready, s + 3)
                pool.tensor_tensor(rstd1[u][:, :], ve1[u][:, :], minus_half[:, :], ALU.pow).then_inc(rstd1_ready, 1)
            if nxt1:
                if fin:
                    pool.wait_ge(x1_ready, s)
                if isinstance(s, int) and s == -1:
                    pool.wait_ge(w_loaded, 16 * 8)
                pool.tensor_tensor(XB[v][:, :, :], X[v][:, :, :],
                                   bp_sb[:, :].rearrange("p (o d) -> p o d", o=1).to_broadcast([P, TB, D]),
                                   ALU.add).then_inc(xb_ready, 1)
            if nxt2:
                pool.wait_ge(kh_ready, s + 3)
                wait(pool, score_done, NU * (s + 1))
                mask_heads(KHZ[u], KH[u], khz_ready)

        run(pool, step)

    @block.scalar
    def _(act):
        act.wait_ge(w_loaded, 16 * 8)

        def step(i, c, nxt2, nxt1, now, fin):
            s, u, v = 2 * i + c, c % 2, (c + 1) % 2

            def exp(j):
                if not now:
                    return
                act.wait_ge(score_done, NU * s + j + 1)
                wait(act, pv_done, NP * (s - 2) + j // 2 + 1)
                act.activation(PT[u][0:M, SU * j:SU * (j + 1), :], score_bank[j % 2][0:M, :], ACT.Exp, scale=SCALE) \
                    .then_inc(exp_ready, 1)

            def save_pv(half, b):
                act.wait_ge(pv_done, NP * b + 2 * (half + 1))
                wait(act, tok_done, b)
                act.activation(PVS[:, half, :], pv_bank[half][:, :], ACT.Copy).then_inc(pvs_ready, 1)

            exp(0)
            if fin:
                save_pv(1, s - 1)
            exp(1)
            if nxt1:
                act.wait_ge(v_done, s + 2)
                wait(act, pv_done, NP * s)
                act.activation(VA[v][0:M, :, 0:DH], misc_b[0:M, 0:D], ACT.Copy).then_inc(va_ready, 1)
            exp(2)
            exp(3)
            if fin:
                act.wait_ge(oT_done, s)
                act.activation(OT[v][:, :, :], misc_a[:, :], ACT.Copy).then_inc(oT_ready, 1)
            exp(4)
            exp(5)
            if now:
                save_pv(0, s)
            exp(6)
            if nxt2:
                act.wait_ge(k_done, s + 3)
                wait(act, khz_ready, s + 1)
                act.activation(KH[u][:, :, :], misc_a[:, 0:KD * M], ACT.Copy).then_inc(kh_ready, 1)
            exp(7)
            if fin:
                act.wait_ge(xn2T_done, s)
                for k in range(KD):
                    ins = act.activation(XN2T[v][:, k, :], misc_b[:, k * S:(k + 1) * S], ACT.Copy, scale=nw_sb[:, k:k + 1])
                ins.then_inc(xn2T_ready, 1)
            if nxt2:
                act.wait_ge(xnT_done, s + 3)
                act.activation(XNT[u][:, :, :], misc_b[:, :], ACT.Copy).then_inc(xnT_ready, 1)
            if nxt1:
                act.wait_ge(nmT_done, s + 2)
                act.activation(NMT[v][:, :], misc_a[:, 0:S], ACT.Copy).then_inc(nmT_ready, 1)
            if nxt2:
                act.wait_ge(q_done, s + 3)
                wait(act, score_done, NU * (s + 1))
                act.activation(QH[u][:, :, :], misc_b[:, :], ACT.Copy).then_inc(qh_ready, 1)

        run(act, step)

    @block.vector
    def _(dve):
        dve.wait_ge(pool_const, 12)
        dve.tensor_copy(row_pick[:, :, :], row_pick_f[:, :, :]).then_inc(const_ready, 1)

        def step(i, c, nxt2, nxt1, now, fin):
            s, u, v = 2 * i + c, c % 2, (c + 1) % 2

            def row_max(q):
                if not nxt1:
                    return
                t, hq = q // (H // MU), q % (H // MU)
                dve.wait_ge(smax_done, NQ * (s + 1) + q + 1)
                dve.tensor_reduce(NM[v][:, t, MU * hq:MU * (hq + 1)],
                                  smax_bank[q % 2][:, 0:MU * M].rearrange("p (h m) -> p h m", m=M),
                                  axis=AX.X, op=ALU.max, negate=True).then_inc(max_ready, 1)

            if fin:
                dve.wait_ge(tok_done, s)
                pv = [pv_bank[t][:, :].rearrange("p (h e) -> p h e", e=2 * DH) for t in range(TB)]
                for t in range(TB):
                    dve.reciprocal(RS[v][:, t, :], pv[t][:, :, DH]).then_inc(rs_ready, 1)
                dve.wait_ge(rs_ready, TB * s)
                for t in range(TB):
                    ins = dve.tensor_tensor(
                        ON[v][:, t, :].rearrange("p (h e) -> p h e", e=DH), pv[t][:, :, 0:DH],
                        RS[v][:, t, :].rearrange("p (h o) -> p h o", o=1).to_broadcast([P, H, DH]), ALU.mult)
                ins.then_inc(on_ready, 1)
            row_max(0)
            row_max(1)
            row_max(2)
            if fin:
                dve.wait_ge(proj_done, s)
                dve.wait_ge(xb_ready, s)
                if not isinstance(s, int) or s >= 3:
                    dve.wait_ge(x1_stored[v], 16 * (i + (c - 1) // 2))
                dve.tensor_tensor(X1[v][:, :, :], misc_b[:, :].rearrange("p (t d) -> p t d", d=D), XB[v][:, :, :],
                                  ALU.add).then_inc(x1_ready, 1)
                dve.wait_ge(x1_ready, s)
                for t in range(TB):
                    dve.bn_stats(bn2[v][:, t, :], X1[v][:, t, :]).then_inc(stats2_a, 1)
                dve.wait_ge(stats2_a, TB * s)
                dve.sem_inc(dve_passed, 1)
                for t in range(TB):
                    ins = dve.bn_aggr(mv2[v][:, t, :], bn2[v][:, t, :])
                ins.then_inc(stats2_ready, 1)
            row_max(3)
            if nxt2:
                dve.wait_ge(x_loaded[u], 16 * (i + (c + 2) // 2 + 1))
                for t in range(TB):
                    dve.bn_stats(bn1[u][:, t, :], X[u][:, t, :]).then_inc(stats1_a, 1)
                dve.wait_ge(stats1_a, TB * (s + 3))
                dve.sem_inc(dve_passed, 1)
                for t in range(TB):
                    ins = dve.bn_aggr(mv1[u][:, t, :], bn1[u][:, t, :])
                ins.then_inc(stats1_ready, 1)
            row_max(4)
            if fin:
                dve.wait_ge(rstd2_ready, s)
                if not isinstance(s, int) or s >= 3:
                    dve.wait_ge(xn2_stored[v], 16 * (i + (c - 1) // 2))
                for t in range(TB):
                    ins = dve.tensor_scalar(XN2[v][:, t, :], X1[v][:, t, :], mv2[v][:, t, 0:1], rstd2[v][:, t:t + 1],
                                            ALU.subtract, ALU.mult)
                ins.then_inc(xn2_ready, 1)
            row_max(5)
            if nxt2:
                dve.wait_ge(kh_ready, s + 3)
                wait(dve, klz_ready, s + 1)
                dve.tensor_tensor(KL[u][:, :, :], misc_a[:, 0:KD * M].rearrange("p (k m) -> p k m", m=M),
                                  KH[u][:, :, :].bitcast(FP32), ALU.subtract).then_inc(kl_ready, 1)
                dve.wait_ge(rstd1_ready, s + 3)
                for t in range(TB):
                    ins = dve.tensor_scalar(XN[u][:, t, :], X[u][:, t, :], mv1[u][:, t, 0:1], rstd1[u][:, t:t + 1],
                                            ALU.subtract, ALU.mult)
                ins.then_inc(xn_ready, 1)
            row_max(6)
            row_max(7)
            if fin:
                dve.wait_ge(logit_done, s)
                dve.tensor_tensor(L[:, bass.ds(TB * (s - 1), TB), :],
                                  misc_a[:, 0:TB * E].rearrange("p (t e) -> p t e", e=E),
                                  rb_sb[:, :].rearrange("p (o e) -> p o e", o=1).to_broadcast([P, TB, E]),
                                  ALU.add).then_inc(logit_ready, 1)
            if nxt2:
                dve.wait_ge(qh_ready, s + 3)
                dve.tensor_tensor(QL[u][:, :, :], misc_b[:, :].rearrange("p (k m) -> p k m", m=S),
                                  QH[u][:, :, :].bitcast(FP32), ALU.subtract).then_inc(ql_ready, 1)

        run(dve, step)

    @block.tensor
    def _(pe):
        pe.wait_ge(const_ready, 1)
        pe.wait_ge(w_loaded, 16 * 8)

        def step(i, c, nxt2, nxt1, now, fin):
            s, u, v = 2 * i + c, c % 2, (c + 1) % 2

            def transpose_rows(misc, src, done):
                for k in range(KD):
                    for t in range(TB):
                        ins = pe.transpose(misc[:, k * S + t * P:k * S + (t + 1) * P], src[:, t, k * P:(k + 1) * P],
                                           ident[:, :])
                ins.then_inc(done, 1)

            def scores(j):
                if not now:
                    return
                if j == 0:
                    pe.wait_ge(nmT_ready, s + 1)
                    pe.wait_ge(klz_ready, s + 1)
                    pe.wait_ge(ql_ready, s + 1)
                wait(pe, exp_ready, NU * s + j - 1)
                for r in range(SU):
                    h = SU * j + r
                    g = h // (P // DH)
                    o = score_bank[j % 2][0:M, r * S:(r + 1) * S]
                    pe.matmul(o, row_pick[:, h, :], NMT[u][:, :], start=True, stop=False)
                    pe.matmul(o, KHZ[u][:, h, :], QH[u][:, g, :], start=False, stop=False)
                    pe.matmul(o, KHZ[u][:, h, :], QL[u][:, g, :], start=False, stop=False)
                    ins = pe.matmul(o, KLZ[u][:, h, :], QH[u][:, g, :], start=False, stop=True)
                ins.then_inc(score_done, 1)

            def weigh(k, b, w):
                if k == 0:
                    wait(pe, on_ready, b)
                    pe.wait_ge(va_ready, b + 1)
                pe.wait_ge(exp_ready, NU * b + 2 * (k + 1))
                for c4 in range(4):
                    h = 4 * k + c4
                    ins = pe.matmul(pv_bank[k // 2][2 * DH * c4:2 * DH * (c4 + 1), (k % 2) * S:(k % 2 + 1) * S],
                                    VA[w][0:M, h, :], PT[w][0:M, h, :], start=True, stop=True)
                ins.then_inc(pv_done, 1)

            def max_scores(q):
                if not nxt1:
                    return
                t, hq = q // (H // MU), q % (H // MU)
                if q == 0:
                    pe.wait_ge(qh_ready, s + 2)
                    pe.wait_ge(khz_ready, s + 2)
                wait(pe, max_ready, NQ * (s + 1) + q - 1)
                pe.matmul(smax_bank[q % 2][:, 0:MU * M], QH[v][:, MU * hq // (P // DH), t * P:(t + 1) * P],
                          KHZ[v][:, MU * hq:MU * (hq + 1), :], start=True, stop=True).then_inc(smax_done, 1)

            scores(0)
            if fin:
                weigh(3, s - 1, v)
            scores(1)
            if nxt1:
                pe.wait_ge(ctx_loaded[v], 16 * (i + (c + 1) // 2 + 1))
                pe.wait_ge(ql_ready, s + 2)
                for k in range(KD):
                    ins = pe.matmul(misc_b[0:M, 0:D], CTX[v][:, k, :], wv_sb[:, k, :], start=k == 0, stop=k == KD - 1)
                ins.then_inc(v_done, 1)
            scores(2)
            if fin:
                pe.wait_ge(pvs_ready, 2 * s)
                for k in range(4):
                    for t in range(TB):
                        ins = pe.transpose(pv_bank[t][:, k * P:(k + 1) * P],
                                           PVS[:, k // 2, (k % 2) * S + t * P:(k % 2) * S + (t + 1) * P], ident[:, :])
                ins.then_inc(tok_done, 1)
            max_scores(0)
            max_scores(1)
            scores(3)
            if fin:
                pe.wait_ge(on_ready, s)
                wait(pe, nmT_ready, s + 1 if now else 0)
                transpose_rows(misc_a, ON[v], oT_done)
            max_scores(2)
            if now:
                weigh(0, s, u)
            scores(4)
            if fin:
                pe.wait_ge(oT_ready, s)
                if nxt1:
                    pe.wait_ge(va_ready, s + 2)
                for t in range(TB):
                    for k in range(KD):
                        ins = pe.matmul(misc_b[:, t * D:(t + 1) * D], OT[v][:, k, t * P:(t + 1) * P], wp_sb[:, k, :],
                                        start=k == 0, stop=k == KD - 1)
                ins.then_inc(proj_done, 1)
            max_scores(3)
            scores(5)
            if now:
                weigh(1, s, u)
            max_scores(4)
            scores(6)
            if nxt2:
                pe.wait_ge(ctx_loaded[u], 16 * (i + (c + 2) // 2 + 1))
                if fin:
                    pe.wait_ge(oT_ready, s)
                elif nxt1:
                    wait(pe, nmT_ready, s + 1)
                for g in range(KD):
                    for k in range(KD):
                        ins = pe.matmul(misc_a[:, g * M:(g + 1) * M], wk_sb[:, k, g * P:(g + 1) * P], CTX[u][:, k, :],
                                        start=k == 0, stop=k == KD - 1)
                ins.then_inc(k_done, 1)
            max_scores(5)
            scores(7)
            if fin:
                pe.wait_ge(xn2_ready, s)
                transpose_rows(misc_b, XN2[v], xn2T_done)
            if now:
                weigh(2, s, u)
            max_scores(6)
            max_scores(7)
            if fin:
                pe.wait_ge(xn2T_ready, s)
                if nxt2:
                    pe.wait_ge(kl_ready, s + 3)
                for t in range(TB):
                    for k in range(KD):
                        ins = pe.matmul(misc_a[:, t * E:(t + 1) * E], XN2T[v][:, k, t * P:(t + 1) * P], rw_sb[:, k, :],
                                        start=k == 0, stop=k == KD - 1)
                ins.then_inc(logit_done, 1)
            if nxt2:
                pe.wait_ge(xn_ready, s + 3)
                if fin:
                    pe.wait_ge(xn2T_ready, s)
                elif nxt1:
                    pe.wait_ge(va_ready, s + 2)
                transpose_rows(misc_b, XN[u], xnT_done)
            if nxt1:
                pe.wait_ge(max_ready, NQ * (s + 2))
                if fin:
                    pe.wait_ge(logit_ready, s)
                elif nxt2:
                    pe.wait_ge(kl_ready, s + 3)
                for t in range(TB):
                    ins = pe.transpose(misc_a[:, t * P:(t + 1) * P], NM[v][:, t, :], ident[:, :])
                ins.then_inc(nmT_done, 1)
            if nxt2:
                pe.wait_ge(xnT_ready, s + 3)
                for g in range(KD):
                    for k in range(KD):
                        ins = pe.matmul(misc_b[:, g * S:(g + 1) * S], wq_sb[:, k, g * P:(g + 1) * P], XNT[u][:, k, :],
                                        start=k == 0, stop=k == KD - 1)
                ins.then_inc(q_done, 1)

        run(pe, step)


def routing_phase(nc, ctx, sem, bank, ident, L, idx_in, idx_out, gate_table):
    def sb(name, shape, dt):
        return ctx.enter_context(nc.sbuf_tensor(name, shape, dt))

    LT = sb("LT", [P, CT], FP32)
    LP = sb("LP", [P, TC, NC * E], FP32)
    junk = sb("junk", [P, CT], FP32)
    eq = sb("eq", [P, CT], FP32)
    gt = sb("gt", [P, CT], FP32)
    zero_row = sb("zero_row", [P, CT], FP32)
    prefix = sb("prefix", [P, CT], FP32)
    chosen = sb("chosen", [P, CT], FP32)
    slot = sb("slot", [P, CT], FP32)
    same_e = sb("same_e", [P, P], FP32)
    same_e_below = sb("same_e_below", [P, P], FP32)
    ge_mod = sb("ge_mod", [P, P], FP32)
    prior, cand, mask_x, bit, taken = (sb(n, [P, 1], U32) for n in ("prior", "cand", "mask_x", "bit", "taken"))
    prior_i = sb("prior_i", [P, 1], I32)
    counts = sb("counts", [P, 2], FP32)
    need = sb("need", [P, 8], FP32)

    mx, sm, rsm = (sb(n, [P, NT], FP32) for n in ("mx", "sm", "rsm"))
    probs = sb("probs", [P, NT, E], FP32)
    expl = sb("expl", [P, NT, E], FP32)
    slot_t = sb("slot_t", [P, NT, E], I32)
    slot_a_i, slot_b_i = sb("slot_a_i", [P, NT, E], I32), sb("slot_b_i", [P, NT, E], I32)
    slot_a, slot_b = sb("slot_a", [P, NT, E], BF16), sb("slot_b", [P, NT, E], BF16)
    taken_f = sb("taken_f", [P, NT, E], FP32)
    gates = sb("gates", [P, NT, E], FP32)
    p_col = sb("p_col", [P, 1], FP32)
    t_val = sb("t_val", [P, NT, EG], BF16)
    hot_a = sb("hot_a", [P, SA, NT * EG], BF16)
    hot_b = sb("hot_b", [P, SB, NT * EG], BF16)
    val_b = sb("val_b", [P, 2, SB, NT * EG], BF16)
    pt = [sb(f"pt{g}", [P, 2, SB], FP32) for g in range(E // EG)]
    ids = [sb(f"ids{g}", [P, 2, SB], I32) for g in range(E // EG)]

    logits_t = bank[0:2]
    cnt_bank = bank[2]
    slots_t = bank[3:5]
    idx_bank = bank[5:7]

    consts = sem("consts")
    cvt = sem("cvt")
    lp_ready, lt_done = sem("lp_ready"), sem("lt_done")
    step_dve = sem("step_dve")
    count_ready, total_done = sem("count_ready"), sem("total_done")
    mx_ready, lx_ready, ex_ready = sem("mx_ready"), sem("lx_ready"), sem("ex_ready")
    slot_ready, slotT_done = sem("slot_ready"), sem("slotT_done")
    hot_ready, idx_done, ids_ready = sem("hot_ready"), sem("idx_done"), sem("ids_ready")
    gates_ready = sem("gates_ready")
    gates_stored, ids_moved = sem("gates_stored"), sem("ids_moved")

    block = ctx.enter_context(nc.Block())

    @block.gpsimd
    def _(pool):
        pool.memset(same_e[:, :], 0.0).then_inc(consts, 1)
        pool.memset(zero_row[:, :], 0.0).then_inc(consts, 1)
        pool.iota(p_col[:, :], pattern=[[0, 1]], base=0, channel_multiplier=1,
                  allow_small_or_imprecise_dtypes=True).then_inc(consts, 1)
        pool.iota(t_val[:, :, :], pattern=[[1, NT], [0, EG]], base=0, channel_multiplier=0,
                  allow_small_or_imprecise_dtypes=True).then_inc(consts, 1)
        n = 4
        for k in range(-(NC - 1), NC):
            pool.wait_ge(consts, n)
            pool.affine_select(out=same_e[:, :], in_=same_e[:, :], compare_op=ALU.not_equal, fill=1.0, base=k * E,
                               pattern=[[-1, P]], channel_multiplier=1).then_inc(consts, 1)
            n += 1
        pool.wait_ge(consts, n)
        pool.affine_select(out=same_e_below[:, :], in_=same_e[:, :], compare_op=ALU.is_gt, fill=0.0, base=0,
                           pattern=[[1, P]], channel_multiplier=-1).then_inc(consts, 1)

    n_consts = 4 + 2 * NC - 1 + 1

    @block.scalar
    def _(act):
        act.wait_ge(lx_ready, 1)
        act.activation(expl[:, :, :], expl[:, :, :], ACT.Exp).then_inc(ex_ready, 1)

    @block.vector
    def _(dve):
        n = [0]

        def then(ins):
            n[0] += 1
            ins.then_inc(step_dve, 1)
            dve.wait_ge(step_dve, n[0])

        dve.tensor_copy(LP[:, :, :].rearrange("p j (c e) -> p j c e", e=E),
                        L[:, :, :].rearrange("p (c j) e -> p j c e", j=TC)).then_inc(lp_ready, 1)
        dve.wait_ge(lt_done, 1)
        for j in range(2):
            ins = dve.tensor_copy(LT[:, 512 * j:512 * (j + 1)], logits_t[j][:, :])
        then(ins)
        dve.wait_ge(consts, n_consts)

        dve.tensor_scalar(junk[:, :], LT[:, :], 0.0, None, ALU.is_ge, ALU.add, accum_out=counts[:, 0:1]) \
            .then_inc(count_ready, 1)
        dve.wait_ge(total_done, 1)
        then(dve.tensor_scalar(prior_i[:, :], cnt_bank[:, 0:1], GMAX, None, ALU.is_ge))
        then(dve.tensor_scalar(prior[:, :], prior_i[:, :].bitcast(U32), 31, None, ALU.logical_shift_left))
        then(dve.tensor_scalar(prior_i[:, :], prior[:, :].bitcast(I32), 31, None, ALU.arith_shift_right))
        then(dve.memset(bit[:, :], 1 << 30))
        then(dve.memset(taken[:, :], 0x80000000))
        then(dve.tensor_scalar(cand[:, :], prior_i[:, :].bitcast(U32), 0xFFFFFFFF, None, ALU.bitwise_xor))
        then(dve.tensor_tensor(mask_x[:, :], cand[:, :], taken[:, :], ALU.bitwise_or))
        base = n[0]
        with dve.Fori(0, 31) as i:
            dve.tensor_tensor(cand[:, :], prior[:, :], bit[:, :], ALU.bitwise_or).then_inc(step_dve, 1)
            dve.wait_ge(step_dve, 5 * i + (base + 1))
            dve.tensor_tensor(cand[:, :], cand[:, :], mask_x[:, :], ALU.bitwise_xor).then_inc(step_dve, 1)
            dve.wait_ge(step_dve, 5 * i + (base + 2))
            dve.tensor_scalar(junk[:, :], LT[:, :], cand[:, :].bitcast(FP32), None, ALU.is_ge, ALU.add,
                              accum_out=counts[:, 0:1]).then_inc(count_ready, 1)
            dve.wait_ge(total_done, i + 2)
            dve.tensor_scalar(taken[:, :], cnt_bank[:, 0:1], GMAX, bit[:, :], ALU.is_ge, ALU.mult).then_inc(step_dve, 1)
            dve.wait_ge(step_dve, 5 * i + (base + 3))
            dve.tensor_tensor(prior[:, :], prior[:, :], taken[:, :], ALU.bitwise_or).then_inc(step_dve, 1)
            dve.tensor_scalar(bit[:, :], bit[:, :], 1, None, ALU.logical_shift_right).then_inc(step_dve, 1)
            dve.wait_ge(step_dve, 5 * i + (base + 5))
        n[0] = base + 5 * 31
        then(dve.tensor_tensor(cand[:, :], prior[:, :], mask_x[:, :], ALU.bitwise_xor))
        thr = cand[:, :].bitcast(FP32)
        dve.tensor_scalar(gt[:, :], LT[:, :], thr, None, ALU.is_gt, ALU.add, accum_out=counts[:, 0:1]) \
            .then_inc(step_dve, 1)
        dve.tensor_scalar(eq[:, :], LT[:, :], thr, None, ALU.is_equal, ALU.add, accum_out=counts[:, 1:2]) \
            .then_inc(step_dve, 1)
        n[0] += 2
        dve.wait_ge(step_dve, n[0])
        dve.sem_inc(count_ready, 1)
        dve.wait_ge(total_done, 33)
        then(dve.tensor_copy(need[:, 0:4], cnt_bank[:, 0:4]))
        then(dve.tensor_scalar(need[:, 4:5], need[:, 0:1], -1.0, float(CAP), ALU.mult, ALU.add))
        then(dve.tensor_tensor(need[:, 5:6], need[:, 3:4], need[:, 4:5], ALU.min))
        then(dve.tensor_tensor(need[:, 6:7], need[:, 5:6], need[:, 2:3], ALU.add))
        then(dve.tensor_tensor_scan(prefix[:, :], eq[:, :], zero_row[:, :], need[:, 3:4], ALU.add, ALU.add))
        then(dve.tensor_scalar(junk[:, :], prefix[:, :], need[:, 4:5], None, ALU.is_le))
        then(dve.tensor_tensor(eq[:, :], eq[:, :], junk[:, :], ALU.mult))
        then(dve.tensor_tensor(chosen[:, :], gt[:, :], eq[:, :], ALU.add))
        then(dve.tensor_tensor_scan(prefix[:, :], chosen[:, :], zero_row[:, :], need[:, 6:7], ALU.add, ALU.add))
        then(dve.tensor_tensor(slot[:, :], prefix[:, :], chosen[:, :], ALU.mult))
        dve.tensor_scalar(slot[:, :], slot[:, :], -1.0, None, ALU.add).then_inc(slot_ready, 1)

        then(dve.tensor_reduce(mx[:, :], L[:, :, :], axis=AX.X, op=ALU.max))
        dve.tensor_tensor(expl[:, :, :], L[:, :, :],
                          mx[:, :].rearrange("p (t o) -> p t o", o=1).to_broadcast([P, NT, E]),
                          ALU.subtract).then_inc(lx_ready, 1)
        dve.wait_ge(slotT_done, 1)
        for j in range(TC):
            ins = dve.tensor_copy(slot_t[:, j::TC, :],
                                  slots_t[j // 4][:, P * (j % 4):P * (j % 4 + 1)].rearrange("p (c e) -> p c e", e=E))
        then(ins)
        dve.tensor_scalar(slot_a_i[:, :, :], slot_t[:, :, :], 4, None, ALU.arith_shift_right).then_inc(cvt, 1)
        dve.tensor_scalar(slot_b_i[:, :, :], slot_t[:, :, :], SB - 1, None, ALU.bitwise_and).then_inc(cvt, 1)
        dve.wait_ge(cvt, 2)
        dve.tensor_copy(slot_a[:, :, :], slot_a_i[:, :, :]).then_inc(cvt, 1)
        dve.tensor_copy(slot_b[:, :, :], slot_b_i[:, :, :]).then_inc(cvt, 1)
        dve.tensor_scalar(taken_f[:, :, :], slot_t[:, :, :], 0.0, None, ALU.is_ge).then_inc(cvt, 1)
        dve.wait_ge(cvt, 5)

        dve.wait_ge(ex_ready, 1)
        then(dve.tensor_reduce(sm[:, :], expl[:, :, :], axis=AX.X, op=ALU.add))
        then(dve.reciprocal(rsm[:, :], sm[:, :]))

        def along_e(a):
            return a[:, :].rearrange("p (t o) -> p t o", o=1).to_broadcast([P, NT, E])

        then(dve.tensor_tensor(probs[:, :, :], expl[:, :, :], along_e(rsm), ALU.mult))
        then(dve.tensor_tensor(gates[:, :, :], probs[:, :, :], taken_f[:, :, :], ALU.mult))
        then(dve.tensor_reduce(sm[:, :], gates[:, :, :], axis=AX.X, op=ALU.add))
        then(dve.tensor_scalar(mx[:, :], sm[:, :], 0.0, None, ALU.is_equal))
        then(dve.tensor_tensor(sm[:, :], sm[:, :], mx[:, :], ALU.add))
        then(dve.reciprocal(rsm[:, :], sm[:, :]))
        dve.tensor_tensor(gates[:, :, :], probs[:, :, :], along_e(rsm), ALU.mult).then_inc(gates_ready, 1)

        def hot(g):
            es = slice(EG * g, EG * (g + 1))
            if g:
                dve.wait_ge(idx_done, g)
            for a in range(SA):
                dve.tensor_scalar(hot_a[:, a, :].rearrange("p (t e) -> p t e", e=EG), slot_a[:, :, es], float(a), None,
                                  ALU.is_equal)
            for b in range(SB):
                dve.tensor_scalar(hot_b[:, b, :].rearrange("p (t e) -> p t e", e=EG), slot_b[:, :, es], float(b), None,
                                  ALU.is_equal).then_inc(step_dve, 1)
                dve.tensor_scalar(val_b[:, 0, b, :].rearrange("p (t e) -> p t e", e=EG), slot_b[:, :, es], float(b),
                                  p_col[:, :], ALU.is_equal, ALU.mult)
            n[0] += SB
            dve.wait_ge(step_dve, n[0])
            dve.tensor_tensor(val_b[:, 1, :, :], hot_b[:, :, :],
                              t_val[:, :, :].rearrange("p (o t) e -> p o (t e)", o=1).to_broadcast([P, SB, NT * EG]),
                              ALU.mult).then_inc(hot_ready, 1)

        def finish_ids(g):
            dve.wait_ge(idx_done, g + 1)
            then(dve.tensor_copy(pt[g][:, :, :], idx_bank[g % 2][:, 0:2 * SB].rearrange("p (k b) -> p k b", k=2)))
            dve.tensor_scalar(junk[:, 0:SB], pt[g][:, 0, :], float(NT), None, ALU.mult).then_inc(step_dve, 1)
            dve.tensor_scalar(junk[:, SB:2 * SB], pt[g][:, 1, :], float(P), None, ALU.mult).then_inc(step_dve, 1)
            n[0] += 2
            dve.wait_ge(step_dve, n[0])
            dve.tensor_tensor(ids[g][:, 0, :], junk[:, 0:SB], pt[g][:, 1, :], ALU.add).then_inc(ids_ready, 1)
            dve.tensor_tensor(ids[g][:, 1, :], junk[:, SB:2 * SB], pt[g][:, 0, :], ALU.add).then_inc(ids_ready, 1)

        for g in range(E // EG):
            hot(g)
            finish_ids(g)

    @block.tensor
    def _(pe):
        pe.wait_ge(lp_ready, 1)
        for j in range(TC):
            ins = pe.transpose(logits_t[j // 4][:, P * (j % 4):P * (j % 4 + 1)],
                               LP[:, j, :], ident[:, :])
        ins.then_inc(lt_done, 1)
        pe.wait_ge(consts, n_consts)
        pe.wait_ge(count_ready, 1)
        pe.matmul(cnt_bank[:, 0:1], same_e[:, :], counts[:, 0:1], start=True, stop=True).then_inc(total_done, 1)
        with pe.Fori(0, 31) as i:
            pe.wait_ge(count_ready, i + 2)
            pe.matmul(cnt_bank[:, 0:1], same_e[:, :], counts[:, 0:1], start=True, stop=True).then_inc(total_done, 1)
        pe.wait_ge(count_ready, 33)
        pe.matmul(cnt_bank[:, 0:2], same_e[:, :], counts[:, :], start=True, stop=True)
        pe.matmul(cnt_bank[:, 2:4], same_e_below[:, :], counts[:, :], start=True, stop=True).then_inc(total_done, 1)
        pe.wait_ge(slot_ready, 1)
        for j in range(TC):
            ins = pe.transpose(slots_t[j // 4][:, P * (j % 4):P * (j % 4 + 1)], slot[:, P * j:P * (j + 1)], ident[:, :])
        ins.then_inc(slotT_done, 1)
        for g in range(E // EG):
            pe.wait_ge(hot_ready, g + 1)
            if g >= 2:
                pe.wait_ge(ids_ready, 2 * (g - 1))
            for t in range(NT):
                for e in range(EG):
                    ins = pe.matmul(idx_bank[g % 2][SA * e:SA * (e + 1), 0:2 * SB], hot_a[:, :, EG * t + e],
                                    val_b[:, :, :, EG * t + e], start=t == 0, stop=t == NT - 1)
            ins.then_inc(idx_done, 1)

    @block.sync
    def _(sp):
        for g in range(E // EG):
            sp.wait_ge(ids_ready, 2 * (g + 1))
            for e in range(EG):
                for kind, dst in enumerate((idx_in, idx_out)):
                    sp.dma_start(dst[:, EG * g + e, :], ids[g][SA * e:SA * (e + 1), kind, :]) \
                        .then_inc(ids_moved, 16)
            if g == 0:
                sp.wait_ge(gates_ready, 1)
                sp.dma_start(gate_table.rearrange("(p r) o -> p (r o)", p=P), gates[:, :, :].rearrange("p t e -> p (t e)")) \
                    .then_inc(gates_stored, 16)
        sp.wait_ge(ids_moved, 16 * 2 * E)
        sp.wait_ge(gates_stored, 16)


def expert_phase(nc, ctx, sem, bank, ident, idx_in, idx_out, gate_table, xn_table, w1T, b1, w2T, b2, nw, out):
    def sb(name, shape, dt):
        return ctx.enter_context(nc.sbuf_tensor(name, shape, dt))

    def pair(name, shape, dt):
        return [sb(f"{name}{u}", shape, dt) for u in range(2)]

    W1, W2 = sb("W1", [P, KD, F], FP32), sb("W2", [P, KF, D], FP32)
    W1H, W1L = sb("W1H", [P, KD, F], FP32R), sb("W1L", [P, KD, F], FP32R)
    W2H, W2L = sb("W2H", [P, KF, D], FP32R), sb("W2L", [P, KF, D], FP32R)
    B2 = pair("B2", [P, D], FP32)
    B1 = sb("B1", [P, E * KF], FP32)
    NW = sb("NW", [P, KD], FP32)
    gate_row = sb("gate_row", [P, E, GT], I32)
    e_off = sb("e_off", [P, E, GT], I32)
    gate_row0 = sb("gate_row0", [P, E, GT], I32)
    II, IG, IO = pair("II", [P, GT], I32), pair("IG", [P, GT], I32), pair("IO", [P, GT], I32)
    XG = pair("XG", [P, GT, D], FP32)
    G, GK = pair("G", [P, GT], FP32), pair("GK", [P, GT], FP32)
    XTH, XTL = pair("XTH", [P, KD, CAP], FP32R), pair("XTL", [P, KD, CAP], FP32R)
    HF = [sb(f"HF{n}", [P, CAP], FP32) for n in range(4)]
    HH, HL = pair("HH", [P, KF, CAP], FP32R), pair("HL", [P, KF, CAP], FP32R)
    Y0 = sb("Y0", [P, GT, D], FP32)
    C = pair("C", [P, GT, D], FP32)

    xt_bank = bank[0:2]
    h_bank = bank[2:6]
    y_bank = bank[6:8]

    w1_loaded, w2_loaded = sem("w1_loaded"), sem("w2_loaded")
    b2_loaded = [sem(f"b2_loaded{u}") for u in range(2)]
    w1h_ready, w1l_ready, w2h_ready, w2l_ready = (sem(n) for n in ("w1h_ready", "w1l_ready", "w2h_ready", "w2l_ready"))
    c_loaded = sem("c_loaded")
    e_off_ready, gi_a, gi_ready = sem("e_off_ready"), sem("gi_a"), sem("gi_ready")
    idx_ready, idx_out_ready = sem("idx_ready"), sem("idx_out_ready")
    gathered = [sem(f"gathered{u}") for u in range(2)]
    xt_done, xth_ready, xt_ready = sem("xt_done"), sem("xth_ready"), sem("xt_ready")
    h_done, hf_ready, hh_ready, hl_ready = sem("h_done"), sem("hf_ready"), sem("hh_ready"), sem("hl_ready")
    y_done, y0_ready, c_ready = sem("y_done"), sem("y0_ready"), sem("c_ready")
    added, gk_ready = sem("added"), sem("gk_ready")
    pool_passed = sem("pool_passed_e")

    block = ctx.enter_context(nc.Block())

    @block.sync
    def _(sp):
        def load_1(e, first=False):
            if not first:
                sp.wait_ge(w1l_ready, e)
            sp.dma_start(W1[:, :, :], w1T[bass.ds(e, 1), :, :].rearrange("o (k p) f -> p (o k) f", p=P)) \
                .then_inc(w1_loaded, 16)

        def load_2(e, first=False):
            if not first:
                sp.wait_ge(w2l_ready, e)
            sp.dma_start(W2[:, :, :], w2T[bass.ds(e, 1), :, :].rearrange("o (k p) d -> p (o k) d", p=P)) \
                .then_inc(w2_loaded, 16)

        def load_b(e, u, first=False):
            if not first:
                sp.wait_ge(y0_ready, e - 1)
            sp.dma_start(B2[u][:, :], b2[bass.ds(e, 1), :].to_broadcast([P, D])).then_inc(b2_loaded[u], 16)

        load_1(0, True)
        sp.dma_start(NW[:, :], nw).then_inc(c_loaded, 16)
        sp.dma_start(B1[:, :], b1).then_inc(c_loaded, 16)
        load_2(0, True)
        load_b(0, 0, True)
        load_b(1, 1, True)
        load_1(1)
        load_2(1)
        with sp.Fori(1, E // 2) as i:
            for u in range(2):
                load_1(2 * i + u)
                load_2(2 * i + u)
                load_b(2 * i + u, u)

    @block.gpsimd
    def _(pool):
        pool.iota(e_off[:, :, :], pattern=[[1, E], [0, GT]], base=0, channel_multiplier=0).then_inc(e_off_ready, 1)

        def gather(i, u, first):
            e = 2 * i + u
            pool.wait_ge(idx_ready, e + 1)
            if not first:
                pool.wait_ge(xt_done, e - 1)
                pool.wait_ge(gk_ready, e - 1)
            pool.sem_inc(pool_passed, 1)
            for g in range(GT):
                pool.indirect_dma_start(out=XG[u][:, g, :], out_offset=None, in_=xn_table,
                                        in_offset=bass.IndirectOffsetOnAxis(ap=II[u][:, g:g + 1], axis=0)) \
                    .then_inc(gathered[u], 16)
                pool.indirect_dma_start(out=G[u][:, g:g + 1], out_offset=None, in_=gate_table,
                                        in_offset=bass.IndirectOffsetOnAxis(ap=IG[u][:, g:g + 1], axis=0)) \
                    .then_inc(gathered[u], 16)

        def add_up(i, u, first):
            e = 2 * i + u
            pool.wait_ge(c_ready, e + 1)
            if not first:
                pool.wait_ge(added, 16 * GT * e)
            pool.sem_inc(pool_passed, 1)
            for g in range(GT):
                pool.indirect_dma_start(out=out, in_=C[u][:, g, :], in_offset=None, compute_op=ALU.add,
                                        out_offset=bass.IndirectOffsetOnAxis(ap=IO[u][:, g:g + 1], axis=0)) \
                    .then_inc(added, 16)

        gather(0, 0, True)
        gather(0, 1, True)
        gather(1, 0, False)
        with pool.Fori(1, E // 2 - 1) as i:
            gather(i, 1, False)
            add_up(i - 1, 0, False)
            gather(i + 1, 0, False)
            add_up(i - 1, 1, False)
        gather(E // 2 - 1, 1, False)
        add_up(E // 2 - 2, 0, False)
        add_up(E // 2 - 2, 1, False)
        add_up(E // 2 - 1, 0, False)
        add_up(E // 2 - 1, 1, False)
        pool.wait_ge(added, 16 * GT * E)

    @block.vector
    def _(dve):
        dve.tensor_scalar(gate_row0[:, :, :], idx_in[:, :, :], float(E), None, ALU.mult).then_inc(gi_a, 1)
        dve.wait_ge(gi_a, 1)
        dve.wait_ge(e_off_ready, 1)
        dve.tensor_tensor(gate_row[:, :, :], gate_row0[:, :, :], e_off[:, :, :], ALU.add).then_inc(gi_ready, 1)
        dve.wait_ge(gi_ready, 1)

        def indices(i, u, first):
            e = 2 * i + u
            if not first:
                dve.wait_ge(gathered[u], 16 * 2 * GT * i)
            dve.tensor_copy(II[u][:, :], idx_in[:, bass.ds(e, 1), :].rearrange("p o g -> p (o g)"))
            dve.tensor_copy(IG[u][:, :], gate_row[:, bass.ds(e, 1), :].rearrange("p o g -> p (o g)")).then_inc(idx_ready, 1)

        def split_1(e, first=False):
            dve.wait_ge(w1h_ready, e + 1)
            if not first:
                dve.wait_ge(h_done, KF * e)
            dve.tensor_tensor(W1L[:, :, :], W1[:, :, :], W1H[:, :, :].bitcast(FP32), ALU.subtract).then_inc(w1l_ready, 1)

        def split_2(e, first=False):
            dve.wait_ge(w2h_ready, e + 1)
            if not first:
                dve.wait_ge(y_done, e)
            dve.tensor_tensor(W2L[:, :, :], W2[:, :, :], W2H[:, :, :].bitcast(FP32), ALU.subtract).then_inc(w2l_ready, 1)

        def columns(i, u):
            e = 2 * i + u
            dve.wait_ge(xt_done, e + 1)
            for k in range(KD):
                ins = dve.tensor_scalar(XTH[u][:, k, :], xt_bank[k][:, :], NW[:, k:k + 1], None, ALU.mult)
            ins.then_inc(xth_ready, 1)
            dve.wait_ge(xth_ready, e + 1)
            for k in range(KD):
                ins = dve.scalar_tensor_tensor(XTL[u][:, k, :], xt_bank[k][:, :], NW[:, k:k + 1],
                                               XTH[u][:, k, :].bitcast(FP32), ALU.mult, ALU.subtract)
            ins.then_inc(xt_ready, 1)

        def keep_gates(i, u):
            e = 2 * i + u
            if not isinstance(e, int) or e >= 2:
                dve.wait_ge(c_ready, e - 1)
            dve.wait_ge(gathered[u], 16 * 2 * GT * (i + 1))
            dve.tensor_copy(GK[u][:, :], G[u][:, :]).then_inc(gk_ready, 1)

        def hidden(i, u):
            e = 2 * i + u
            for f in range(KF):
                dve.wait_ge(hh_ready, KF * e + (f + 1))
                dve.tensor_tensor(HL[u][:, f, :], HF[f % 4][:, :], HH[u][:, f, :].bitcast(FP32), ALU.subtract) \
                    .then_inc(hl_ready, 1)

        def contributions(i, u, first=False):
            e = 2 * i + u
            if not first:
                dve.wait_ge(added, 16 * GT * (e - 1))
            if not first or u:
                dve.wait_ge(c_ready, e)
            dve.tensor_copy(IO[u][:, :], idx_out[:, bass.ds(e, 1), :].rearrange("p o g -> p (o g)"))
            dve.wait_ge(y_done, e + 1)
            dve.wait_ge(b2_loaded[u], 16 * (i + 1))
            for j in range(2):
                ins = dve.tensor_tensor(Y0[:, 2 * j:2 * j + 2, :], y_bank[j][:, :].rearrange("p (g d) -> p g d", d=D),
                                        B2[u][:, :].rearrange("p (o d) -> p o d", o=1).to_broadcast([P, 2, D]), ALU.add)
            ins.then_inc(y0_ready, 1)
            dve.wait_ge(y0_ready, e + 1)
            for g in range(GT):
                ins = dve.tensor_scalar(C[u][:, g, :], Y0[:, g, :], GK[u][:, g:g + 1], None, ALU.mult)
            ins.then_inc(c_ready, 1)

        def turn(i, u, ahead=True, first=False):
            e = 2 * i + u
            split_1(e)
            if ahead:
                indices(i + u, 1 - u, False)
            columns(i, u)
            contributions(i - 1, u, first)
            keep_gates(i, u)
            split_2(e - 1)
            hidden(i, u)

        dve.wait_ge(c_loaded, 32)
        indices(0, 0, True)
        indices(0, 1, True)
        split_1(0, True)
        columns(0, 0)
        keep_gates(0, 0)
        hidden(0, 0)
        split_1(1)
        indices(1, 0, False)
        columns(0, 1)
        keep_gates(0, 1)
        split_2(0, True)
        hidden(0, 1)
        turn(1, 0, first=True)
        turn(1, 1, first=True)
        with dve.Fori(2, E // 2 - 1) as i:
            turn(i, 0)
            turn(i, 1)
        turn(E // 2 - 1, 0)
        turn(E // 2 - 1, 1, ahead=False)
        contributions(E // 2 - 1, 0)
        split_2(E - 1)
        contributions(E // 2 - 1, 1)

    @block.scalar
    def _(act):
        act.wait_ge(c_loaded, 32)

        def split_1(e, first=False):
            act.wait_ge(w1_loaded, 16 * (e + 1))
            if not first:
                act.wait_ge(h_done, KF * e)
            act.activation(W1H[:, :, :], W1[:, :, :], ACT.Copy).then_inc(w1h_ready, 1)

        def split_2(e, first=False):
            act.wait_ge(w2_loaded, 16 * (e + 1))
            if not first:
                act.wait_ge(y_done, e)
            act.activation(W2H[:, :, :], W2[:, :, :], ACT.Copy).then_inc(w2h_ready, 1)

        def hidden(i, u, first):
            e = 2 * i + u

            def high(f):
                act.wait_ge(hf_ready, KF * e + (f + 1))
                act.activation(HH[u][:, f, :], HF[f % 4][:, :], ACT.Copy).then_inc(hh_ready, 1)

            for f in range(KF):
                act.wait_ge(h_done, KF * e + (f + 1))
                if not isinstance(e, int) or e > 0 or f >= 4:
                    act.wait_ge(hl_ready, KF * e + (f - 3))
                act.activation(HF[f % 4][:, :], h_bank[f % 4][:, :], ACT.Gelu,
                               bias=B1[:, bass.ds(KF * e + f, 1)]).then_inc(hf_ready, 1)
                if f == 0 and not first:
                    act.wait_ge(y_done, e - 1)
                if f:
                    high(f - 1)
            high(KF - 1)

        split_1(0, True)
        hidden(0, 0, True)
        split_1(1)
        split_2(0, True)
        hidden(0, 1, True)
        with act.Fori(1, E // 2) as i:
            for u in range(2):
                split_1(2 * i + u)
                split_2(2 * i + (u - 1))
                hidden(i, u, False)
        split_2(E - 1)

    @block.tensor
    def _(pe):
        def columns(i, u, first):
            e = 2 * i + u
            pe.wait_ge(gathered[u], 16 * 2 * GT * (i + 1))
            if not first:
                pe.wait_ge(xt_ready, e)
            for k in range(KD):
                for g in range(GT):
                    ins = pe.transpose(xt_bank[k][:, g * P:(g + 1) * P], XG[u][:, g, k * P:(k + 1) * P], ident[:, :])
            ins.then_inc(xt_done, 1)

        def three(o, wh, wl, xh, xl, first, last):
            pe.matmul(o, wh, xh, start=first, stop=False)
            pe.matmul(o, wh, xl, start=False, stop=False)
            return pe.matmul(o, wl, xh, start=False, stop=last)

        def up(i, u, first):
            e = 2 * i + u
            pe.wait_ge(xt_ready, e + 1)
            pe.wait_ge(w1l_ready, e + 1)
            for f in range(KF):
                if not first or f >= 4:
                    pe.wait_ge(hf_ready, KF * e + (f - 3))
                for k in range(KD):
                    w = slice(f * P, (f + 1) * P)
                    ins = three(h_bank[f % 4][:, :], W1H[:, k, w], W1L[:, k, w], XTH[u][:, k, :], XTL[u][:, k, :],
                                k == 0, k == KD - 1)
                ins.then_inc(h_done, 1)

        def down(i, u, first):
            e = 2 * i + u
            if not first:
                pe.wait_ge(y0_ready, e)
            pe.wait_ge(w2l_ready, e + 1)
            pe.wait_ge(hl_ready, KF * (e + 1))
            for g in range(GT):
                for f in range(KF):
                    w = slice(g * P, (g + 1) * P)
                    ins = three(y_bank[g // 2][:, (g % 2) * D:(g % 2 + 1) * D], HH[u][:, f, w], HL[u][:, f, w],
                                W2H[:, f, :], W2L[:, f, :], f == 0, f == KF - 1)
            ins.then_inc(y_done, 1)

        columns(0, 0, True)
        up(0, 0, True)
        columns(0, 1, False)
        up(0, 1, False)
        columns(1, 0, False)
        down(0, 0, True)
        with pe.Fori(1, E // 2 - 1) as i:
            up(i, 0, False)
            columns(i, 1, False)
            down(i - 1, 1, False)
            up(i, 1, False)
            columns(i + 1, 0, False)
            down(i, 0, False)
        up(E // 2 - 1, 0, False)
        columns(E // 2 - 1, 1, False)
        down(E // 2 - 2, 1, False)
        up(E // 2 - 1, 1, False)
        down(E // 2 - 1, 0, False)
        down(E // 2 - 1, 1, False)


def program(nc, x, ctxT, wq, wk, wv, wp, bp, nw, rw, rb, w1T, b1, w2T, b2, out):
    xn_table = nc.dram_tensor("xn_table", [N, D], FP32, kind="Internal").ap()
    gate_table = nc.dram_tensor("gate_table", [N * E, 1], FP32, kind="Internal").ap()
    with ExitStack() as ctx:
        def sem(name):
            return ctx.enter_context(nc.semaphore(name))

        bank = [ctx.enter_context(nc.psum_tensor(f"bank{n}", [P, 512], FP32)) for n in range(8)]
        ident = ctx.enter_context(nc.sbuf_tensor("ident", [P, P], FP32))
        L = ctx.enter_context(nc.sbuf_tensor("L", [P, NT, E], FP32))
        idx_in = ctx.enter_context(nc.sbuf_tensor("idx_in", [P, E, GT], I32))
        idx_out = ctx.enter_context(nc.sbuf_tensor("idx_out", [P, E, GT], I32))
        with ExitStack() as phase:
            attention_phase(nc, phase, sem, bank, ident, L, x, ctxT, wq, wk, wv, wp, bp, nw, rw, rb, out, xn_table)
        with ExitStack() as phase:
            routing_phase(nc, phase, sem, bank, ident, L, idx_in, idx_out, gate_table)
        with ExitStack() as phase:
            expert_phase(nc, phase, sem, bank, ident, idx_in, idx_out, gate_table, xn_table, w1T, b1, w2T, b2, nw,
                         out.rearrange("b s d -> (b s) d"))


def kernel(**inputs):
    import numpy as np
    import concourse.bacc as bacc
    from concourse.bass_utils import run_bass_kernel_spmd

    t = np.ascontiguousarray
    laid = {
        "x": t(inputs["x"]),
        "ctxT": t(np.transpose(inputs["ctx_1024"], (0, 2, 1))),
        "wq": t(inputs["L0_xattn_Wq"]), "wk": t(inputs["L0_xattn_Wk"]),
        "wv": t(inputs["L0_xattn_Wv"]), "wp": t(inputs["L0_xattn_Wp"]), "bp": t(inputs["L0_xattn_bp"]),
        "nw": t(np.transpose(np.reshape(inputs["L0_ffn_norm_weight"], (KD, P)))),
        "rw": t(np.transpose(inputs["L0_ffn_router_weight"])), "rb": t(inputs["L0_ffn_router_bias"]),
        "w1T": t(np.transpose(inputs["L0_ffn_fc1_weight"], (0, 2, 1))),
        "b1": t(np.transpose(np.reshape(inputs["L0_ffn_fc1_bias"], (E * KF, P)))),
        "w2T": t(np.transpose(inputs["L0_ffn_fc2_weight"], (0, 2, 1))),
        "b2": t(inputs["L0_ffn_fc2_bias"]),
    }
    nc = bacc.Bacc("TRN2", target_bir_lowering=False, num_devices=1)
    args = [nc.dram_tensor(f"{name}_dram", a.shape, mybir.dt.from_np(a.dtype), kind="ExternalInput").ap()
            for name, a in laid.items()]
    out = nc.dram_tensor("out_dram", (B, S, D), FP32, kind="ExternalOutput").ap()
    program(nc, *args, out)
    r = run_bass_kernel_spmd(nc, [{f"{name}_dram": a for name, a in laid.items()}], core_ids=[0])
    return r.results[0]["out_dram"]
```

```python
import concourse.bass as bass
from concourse import mybir
from contextlib import ExitStack

FP32 = mybir.dt.float32
FP32R = mybir.dt.float32r
BF16 = mybir.dt.bfloat16
FP16 = mybir.dt.float16
I32 = mybir.dt.int32
U32 = mybir.dt.uint32
ALU = mybir.AluOpType
ACT = mybir.ActivationFunctionType
AX = mybir.AxisListType

P = 128
B, S, D = 32, 256, 256
M = 120
H, DH = 16, 16
KD = D // P
TB = S // P
N = B * S
NT = N // P
E = 16
F = 1024
KF = F // P
CAP = N // E
NC = 8
CT = N // NC
TC = NT // NC
GT = CAP // P
EG = 4
SA, SB = 32, 16
EPS = 1e-5
SCALE = DH ** -0.5
SU = 2
HP = P // 2
HQ = HP // DH
NU = H // SU
NP = H // 4
MU = 4
NQ = TB * H // MU
GMAX = float(CAP) - 0.5
ROUNDS = 8


def attention_phase(nc, ctx, sem, bank, ident, L, search_consts, x, ctxT, wq, wk, wv, wp, bp, nw, rw, rb, out, xn_table):
    def sb(name, shape, dt):
        return ctx.enter_context(nc.sbuf_tensor(name, shape, dt))

    def pair(name, shape, dt):
        return [sb(f"{name}{u}", shape, dt) for u in range(2)]

    wq_sb, wk_sb, wv_sb, wp_sb = (sb(n, [P, KD, D], FP32) for n in ("wq_sb", "wk_sb", "wv_sb", "wp_sb"))
    bp_sb = sb("bp_sb", [P, D], FP32)
    nw_sb = sb("nw_sb", [P, KD], FP32)
    rw_sb = sb("rw_sb", [P, KD, E], FP32)
    rb_sb = sb("rb_sb", [P, E], FP32)
    head_rows8 = sb("head_rows8", [P, P // DH], FP32)
    head_rows = sb("head_rows", [P, HQ], FP32)
    low_rows = sb("low_rows", [P, H], FP32)
    minus_half = sb("minus_half", [P, TB], FP32)
    warm = sb("warm", [P, 1], FP32)

    X = pair("X", [P, TB, D], FP32)
    XB = pair("XB", [P, TB, D], FP32)
    CTX = pair("CTX", [P, KD, M], FP32)
    bn1, mv1, rstd1 = pair("bn1", [P, TB, 6], FP32), pair("mv1", [P, TB, 2], FP32), pair("rstd1", [P, TB], FP32)
    ve1 = pair("ve1", [P, TB], FP32)
    XN = pair("XN", [P, TB, D], FP32)
    XNT = pair("XNT", [P, KD, S], FP32)
    QHL = pair("QHL", [P, 2, KD, S], FP32R)
    QHM = pair("QHM", [P, 2, KD, S], FP32R)
    KH = pair("KH", [P, 2, KD, M], FP32R)
    KL = pair("KL", [P, 2, KD, M], FP32)
    KHZ = pair("KHZ", [P, H, M], FP32R)
    KLP = pair("KLP", [P, H, M], FP32R)
    VA = pair("VA", [P, H, 2 * DH], FP32)
    NM = pair("NM", [P, TB, P], FP32)
    PT = pair("PT", [P, H, S], FP32)
    PVS = sb("PVS", [P, 2, 2 * S], FP32)
    RS = pair("RS", [P, TB, H], FP32)
    ON = pair("ON", [P, TB, D], FP32)
    OT = pair("OT", [P, KD, S], FP32)
    X1 = pair("X1", [P, TB, D], FP32)
    bn2, mv2, rstd2 = pair("bn2", [P, TB, 6], FP32), pair("mv2", [P, TB, 2], FP32), pair("rstd2", [P, TB], FP32)
    ve2 = pair("ve2", [P, TB], FP32)
    XN2 = pair("XN2", [P, TB, D], FP32)
    XN2T = pair("XN2T", [P, KD, S], FP32)

    smax_bank = bank[0:2]
    score_bank = bank[2:4]
    pv_bank = bank[4:6]
    misc_a, misc_b = bank[6], bank[7]

    wk_loaded, w_loaded = sem("wk_loaded"), sem("w_loaded")
    x_loaded = [sem(f"x_loaded{u}") for u in range(2)]
    ctx_loaded = [sem(f"ctx_loaded{u}") for u in range(2)]
    x1_stored = [sem(f"x1_stored{u}") for u in range(2)]
    xn2_stored = [sem(f"xn2_stored{u}") for u in range(2)]
    pool_const = sem("pool_const")
    const_ready, search_const = sem("const_ready"), sem("search_const")
    stats1_a, stats1_ready = sem("stats1_a"), sem("stats1_ready")
    ve1_ready, rstd1_ready = sem("ve1_ready"), sem("rstd1_ready")
    xn_ready = sem("xn_ready")
    xnT_done, xnT_ready = sem("xnT_done"), sem("xnT_ready")
    q_done, qh_ready, ql_ready = sem("q_done"), sem("qh_ready"), sem("ql_ready")
    qhm_ready = sem("qhm_ready")
    k_done, v_done, kh_ready, va_ready, kl_ready = (sem(n) for n in ("k_done", "v_done", "kh_ready", "va_ready", "kl_ready"))
    khz_ready, klp_ready = sem("khz_ready"), sem("klp_ready")
    xb_ready = sem("xb_ready")
    smax_done, max_ready = sem("smax_done"), sem("max_ready")
    nmT_done, nmT_ready = sem("nmT_done"), sem("nmT_ready")
    score_done, exp_ready = sem("score_done"), sem("exp_ready")
    pv_done, pvs_ready, tok_done = sem("pv_done"), sem("pvs_ready"), sem("tok_done")
    rs_ready, on_ready = sem("rs_ready"), sem("on_ready")
    oT_done, oT_ready = sem("oT_done"), sem("oT_ready")
    proj_done, x1_ready = sem("proj_done"), sem("x1_ready")
    stats2_a, stats2_ready = sem("stats2_a"), sem("stats2_ready")
    ve2_ready, rstd2_ready = sem("ve2_ready"), sem("rstd2_ready")
    xn2_ready = sem("xn2_ready")
    xn2T_done, xn2T_ready = sem("xn2T_done"), sem("xn2T_ready")
    logit_done, logit_ready = sem("logit_done"), sem("logit_ready")

    def wait(eng, s, value):
        if not isinstance(value, int) or value > 0:
            eng.wait_ge(s, value)

    def run(eng, step):
        step(0, -2, nxt2=True, nxt1=False, now=False, fin=False)
        step(0, -1, nxt2=True, nxt1=True, now=False, fin=False)
        step(0, 0, nxt2=True, nxt1=True, now=True, fin=False)
        step(0, 1, nxt2=True, nxt1=True, now=True, fin=True)
        with eng.Fori(1, B // 2 - 1) as i:
            step(i, 0, nxt2=True, nxt1=True, now=True, fin=True)
            step(i, 1, nxt2=True, nxt1=True, now=True, fin=True)
        step(B // 2 - 1, 0, nxt2=False, nxt1=True, now=True, fin=True)
        step(B // 2 - 1, 1, nxt2=False, nxt1=False, now=True, fin=True)
        step(B // 2 - 1, 2, nxt2=False, nxt1=False, now=False, fin=True)

    pool_passed, dve_passed = sem("pool_passed"), sem("dve_passed")
    block = ctx.enter_context(nc.Block())

    @block.sync
    def _(sp):
        def load_x(i, c):
            b, u = 2 * i + c, c % 2
            sp.dma_start(X[u][:, :, :], x[bass.ds(b, 1), :, :].rearrange("o (t p) d -> p (o t) d", p=P)) \
                .then_inc(x_loaded[u], 16)

        def load_ctx(i, c):
            b, u = 2 * i + c, c % 2
            sp.dma_start(CTX[u][:, :, :], ctxT[bass.ds(b, 1), :, :].rearrange("o (k p) m -> p (o k) m", p=P)) \
                .then_inc(ctx_loaded[u], 16)

        load_x(0, 0)
        load_ctx(0, 0)
        for t, w, loaded in ((wk_sb, wk, wk_loaded), (wq_sb, wq, w_loaded), (wv_sb, wv, w_loaded), (wp_sb, wp, w_loaded)):
            sp.dma_start(t[:, :, :], w.rearrange("(k p) c -> p k c", p=P)).then_inc(loaded, 16)
        load_x(0, 1)
        load_ctx(0, 1)
        sp.dma_start(bp_sb[:, :], bp.rearrange("(o d) -> o d", o=1).to_broadcast([P, D])).then_inc(w_loaded, 16)
        sp.dma_start(nw_sb[:, :], nw).then_inc(w_loaded, 16)
        sp.dma_start(rw_sb[:, :, :], rw.rearrange("(k p) e -> p k e", p=P)).then_inc(w_loaded, 16)
        sp.dma_start(rb_sb[:, :], rb.rearrange("(o d) -> o d", o=1).to_broadcast([P, E])).then_inc(w_loaded, 16)

        def step(i, c, load, fin):
            s, v = 2 * i + c, (c + 1) % 2
            if fin:
                sp.wait_ge(x1_ready, s)
                sp.dma_start(out[bass.ds(s - 1, 1), :, :].rearrange("o (t p) d -> p (o t) d", p=P),
                             X1[v][:, :, :]).then_inc(x1_stored[v], 16)
            if load:
                sp.wait_ge(xn_ready, s + 2)
                sp.wait_ge(xb_ready, s + 2)
                load_x(i, c + 3)
            if fin:
                sp.wait_ge(xn2_ready, s)
                sp.dma_start(xn_table.rearrange("(p t) d -> p t d", t=NT)[:, bass.ds(TB * (s - 1), TB), :],
                             XN2[v][:, :, :]).then_inc(xn2_stored[v], 16)
            if load:
                sp.wait_ge(v_done, s + 2)
                load_ctx(i, c + 3)

        step(0, -1, True, False)
        step(0, 0, True, False)
        step(0, 1, True, True)
        with sp.Fori(1, B // 2 - 2) as i:
            step(i, 0, True, True)
            step(i, 1, True, True)
        step(B // 2 - 2, 0, True, True)
        for c in range(1, 5):
            step(B // 2 - 2, c, False, True)
        for u in range(2):
            sp.wait_ge(x1_stored[u], 16 * (B // 2))
            sp.wait_ge(xn2_stored[u], 16 * (B // 2))

    @block.gpsimd
    def _(pool):
        pool.memset(ident[:, :], 0.0).then_inc(pool_const, 1)
        pool.memset(low_rows[:, :], 0.0).then_inc(pool_const, 1)
        pool.memset(head_rows8[:, :], 1.0).then_inc(pool_const, 1)
        pool.memset(minus_half[:, :], -0.5).then_inc(pool_const, 1)
        for u in range(2):
            pool.memset(NM[u][:, :, :], 0.0).then_inc(pool_const, 1)
            pool.memset(VA[u][:, :, :], 1.0).then_inc(pool_const, 1)
            pool.memset(KL[u][:, :, :, :], 1.0).then_inc(pool_const, 1)
        pool.wait_ge(pool_const, 10)
        pool.affine_select(out=ident[:, :], in_=ident[:, :], compare_op=ALU.not_equal, fill=1.0, base=0,
                           pattern=[[-1, P]], channel_multiplier=1).then_inc(pool_const, 1)
        pool.affine_select(out=low_rows[:, :], in_=low_rows[:, :], compare_op=ALU.not_equal, fill=1.0,
                           base=0, pattern=[[-1, H]], channel_multiplier=1).then_inc(pool_const, 1)
        pool.affine_select(out=head_rows8[:, :], in_=head_rows8[:, :], compare_op=ALU.is_ge, fill=0.0,
                           base=0, pattern=[[-DH, P // DH]], channel_multiplier=1).then_inc(pool_const, 1)
        pool.wait_ge(pool_const, 13)
        pool.affine_select(out=low_rows[:, :], in_=low_rows[:, :], compare_op=ALU.not_equal, fill=1.0,
                           base=-HP, pattern=[[-1, H]], channel_multiplier=1).then_inc(pool_const, 1)
        pool.affine_select(out=head_rows8[:, :], in_=head_rows8[:, :], compare_op=ALU.is_ge, fill=0.0,
                           base=DH - 1, pattern=[[DH, P // DH]], channel_multiplier=-1).then_inc(pool_const, 1)
        pool.wait_ge(pool_const, 15)
        pool.tensor_tensor(head_rows[:, :], head_rows8[:, 0:HQ], head_rows8[:, HQ:2 * HQ], ALU.add) \
            .then_inc(pool_const, 1)
        pool.wait_ge(pool_const, 16)
        pool.wait_ge(const_ready, 1)

        def mask_heads(dst, src, g, rows):
            for half in range(2):
                h = HQ * (2 * g + half)
                ins = pool.tensor_tensor(
                    dst[:, h:h + HQ, :], src[:, half, g:g + 1, :].bitcast(FP32).to_broadcast([P, HQ, M]),
                    rows(h).rearrange("p (a o) -> p a o", o=1).to_broadcast([P, HQ, M]), ALU.mult)
            return ins

        def step(i, c, nxt2, nxt1, now, fin):
            s, u, v = 2 * i + c, c % 2, (c + 1) % 2
            if nxt1:
                pool.wait_ge(kh_ready, s + 2)
                wait(pool, score_done, NU * s)
                mask_heads(KHZ[v], KH[v], 0, lambda h: head_rows[:, :])
                mask_heads(KHZ[v], KH[v], 1, lambda h: head_rows[:, :]).then_inc(khz_ready, 1)
            if nxt2:
                pool.wait_ge(stats1_ready, s + 3)
                pool.sem_inc(pool_passed, 1)
                pool.tensor_scalar(ve1[u][:, :], mv1[u][:, :, 1], 1.0, EPS, ALU.mult, ALU.add).then_inc(ve1_ready, 1)
                pool.wait_ge(ve1_ready, s + 3)
                pool.tensor_tensor(rstd1[u][:, :], ve1[u][:, :], minus_half[:, :], ALU.pow).then_inc(rstd1_ready, 1)
            if nxt1:
                pool.wait_ge(kl_ready, s + 2)
                mask_heads(KLP[v], KL[v], 0, lambda h: low_rows[:, h:h + HQ])
            if fin:
                pool.wait_ge(stats2_ready, s)
                pool.sem_inc(pool_passed, 1)
                pool.tensor_scalar(ve2[v][:, :], mv2[v][:, :, 1], 1.0 + EPS, EPS * EPS, ALU.mult, ALU.add) \
                    .then_inc(ve2_ready, 1)
                pool.wait_ge(ve2_ready, s)
                pool.tensor_tensor(rstd2[v][:, :], ve2[v][:, :], minus_half[:, :], ALU.pow).then_inc(rstd2_ready, 1)
            if nxt1:
                mask_heads(KLP[v], KL[v], 1, lambda h: low_rows[:, h:h + HQ]).then_inc(klp_ready, 1)
                if isinstance(s, int) and s == -1:
                    pool.wait_ge(w_loaded, 16 * 7)
                pool.tensor_tensor(XB[v][:, :, :], X[v][:, :, :],
                                   bp_sb[:, :].rearrange("p (o d) -> p o d", o=1).to_broadcast([P, TB, D]),
                                   ALU.add).then_inc(xb_ready, 1)

        run(pool, step)
        search_constants(pool, search_const, *search_consts)

    @block.scalar
    def _(act):
        act.wait_ge(pool_const, 16)
        act.activation(warm[:, :], minus_half[:, 0:1], ACT.Exp)

        def step(i, c, nxt2, nxt1, now, fin):
            s, u, v = 2 * i + c, c % 2, (c + 1) % 2

            def exp(j):
                if not now:
                    return
                act.wait_ge(score_done, NU * s + j + 1)
                wait(act, pv_done, NP * (s - 2) + j // 2 + 1)
                act.activation(PT[u][0:M, SU * j:SU * (j + 1), :], score_bank[j % 2][0:M, :], ACT.Exp, scale=SCALE) \
                    .then_inc(exp_ready, 1)

            def save_pv(half, b):
                act.wait_ge(pv_done, NP * b + 2 * (half + 1))
                wait(act, tok_done, b)
                act.activation(PVS[:, half, :], pv_bank[half][:, :], ACT.Copy).then_inc(pvs_ready, 1)

            def save_q(half):
                act.wait_ge(q_done, s + 2)
                wait(act, score_done, NU * s)
                rows = slice(HP * half, HP * (half + 1))
                act.activation(QHL[v][rows, half, :, :], misc_b[rows, :], ACT.Copy).then_inc(qh_ready, 1)

            if nxt1:
                save_q(0)
            exp(0)
            if fin:
                save_pv(1, s - 1)
            if nxt1:
                save_q(1)
            exp(1)
            exp(2)
            exp(3)
            if nxt1:
                act.wait_ge(v_done, s + 2)
                wait(act, pv_done, NP * s)
                act.activation(VA[v][0:M, :, 0:DH], misc_b[0:M, 0:D], ACT.Copy).then_inc(va_ready, 1)
            if fin:
                act.wait_ge(oT_done, s)
                act.activation(OT[v][:, :, :], misc_a[:, :], ACT.Copy).then_inc(oT_ready, 1)
            if nxt1:
                act.wait_ge(qh_ready, 2 * (s + 2))
                for half in range(2):
                    rows = slice(HP * half, HP * (half + 1))
                    ins = act.activation(QHM[v][rows, half, :, :], QHL[v][rows, half, :, :].bitcast(FP32), ACT.Copy)
                ins.then_inc(qhm_ready, 1)
            exp(4)
            if nxt2:
                act.wait_ge(k_done, s + 3)
                wait(act, khz_ready, s + 1)
                for half in range(2):
                    src = slice(HP * half, HP * (half + 1))
                    for dst in (slice(0, HP), slice(HP, P)):
                        ins = act.activation(KH[u][dst, half, :, :], misc_a[src, 0:KD * M], ACT.Copy)
                ins.then_inc(kh_ready, 1)
            exp(5)
            if now:
                save_pv(0, s)
            if nxt2:
                act.wait_ge(xnT_done, s + 3)
                act.activation(XNT[u][:, :, :], misc_b[:, :], ACT.Copy).then_inc(xnT_ready, 1)
            exp(6)
            exp(7)
            if fin:
                act.wait_ge(xn2T_done, s)
                if isinstance(s, int) and s == 1:
                    act.wait_ge(w_loaded, 16 * 7)
                for k in range(KD):
                    ins = act.activation(XN2T[v][:, k, :], pv_bank[0][:, k * S:(k + 1) * S], ACT.Copy, scale=nw_sb[:, k:k + 1])
                ins.then_inc(xn2T_ready, 1)
            if nxt1:
                act.wait_ge(nmT_done, s + 2)
                for half in range(2):
                    ins = act.activation(QHM[v][HP * (1 - half):HP * (2 - half), half, :, :],
                                         misc_a[0:HP, 0:S].rearrange("p (o q) -> p o q", o=1).to_broadcast([HP, KD, S]),
                                         ACT.Copy)
                ins.then_inc(nmT_ready, 1)

        run(act, step)

    @block.vector
    def _(dve):
        dve.wait_ge(pool_const, 16)
        for half in range(2):
            rows = slice(HP * half, HP * (half + 1))
            ins = dve.tensor_copy(low_rows[rows, :].rearrange("p (g k a) -> p k g a", k=2, a=HQ)[:, half, :, :],
                                  head_rows[rows, :].rearrange("p (o a) -> p o a", o=1).to_broadcast([HP, KD, HQ]))
        ins.then_inc(const_ready, 1)

        def keep_logits(s):
            dve.wait_ge(logit_done, s - 1)
            dve.tensor_tensor(L[:, bass.ds(TB * (s - 2), TB), :],
                              smax_bank[0][:, 0:TB * E].rearrange("p (t e) -> p t e", e=E),
                              rb_sb[:, :].rearrange("p (o e) -> p o e", o=1).to_broadcast([P, TB, E]),
                              ALU.add).then_inc(logit_ready, 1)

        def step(i, c, nxt2, nxt1, now, fin):
            s, u, v = 2 * i + c, c % 2, (c + 1) % 2

            def row_max(q):
                if not nxt1:
                    return
                t, hq = q // (H // MU), q % (H // MU)
                dve.wait_ge(smax_done, NQ * (s + 1) + q + 1)
                dve.tensor_reduce(NM[v][:, t, MU * hq:MU * (hq + 1)],
                                  smax_bank[q % 2][:, 0:MU * M].rearrange("p (h m) -> p h m", m=M),
                                  axis=AX.X, op=ALU.max, negate=True).then_inc(max_ready, 1)

            def low_queries(half):
                dve.wait_ge(qh_ready, 2 * (s + 1) + (half + 1))
                rows, others = slice(HP * half, HP * (half + 1)), slice(HP * (1 - half), HP * (2 - half))
                return dve.tensor_tensor(QHL[v][others, half, :, :], misc_b[rows, :].rearrange("p (k m) -> p k m", m=S),
                                         QHL[v][rows, half, :, :].bitcast(FP32), ALU.subtract)

            if nxt1:
                low_queries(0)
            if not isinstance(s, int) or s >= 2:
                keep_logits(s)
            if nxt1:
                low_queries(1).then_inc(ql_ready, 1)
            if fin:
                dve.wait_ge(tok_done, s)
                pv = [pv_bank[t][:, :].rearrange("p (h e) -> p h e", e=2 * DH) for t in range(TB)]
                for t in range(TB):
                    dve.reciprocal(RS[v][:, t, :], pv[t][:, :, DH]).then_inc(rs_ready, 1)
                dve.wait_ge(rs_ready, TB * s)
                for t in range(TB):
                    ins = dve.tensor_tensor(
                        ON[v][:, t, :].rearrange("p (h e) -> p h e", e=DH), pv[t][:, :, 0:DH],
                        RS[v][:, t, :].rearrange("p (h o) -> p h o", o=1).to_broadcast([P, H, DH]), ALU.mult)
                ins.then_inc(on_ready, 1)
            if nxt2:
                dve.wait_ge(x_loaded[u], 16 * (i + (c + 2) // 2 + 1))
                for t in range(TB):
                    dve.bn_stats(bn1[u][:, t, :], X[u][:, t, :]).then_inc(stats1_a, 1)
                dve.wait_ge(stats1_a, TB * (s + 3))
                dve.sem_inc(dve_passed, 1)
                for t in range(TB):
                    ins = dve.bn_aggr(mv1[u][:, t, :], bn1[u][:, t, :])
                ins.then_inc(stats1_ready, 1)
            row_max(0)
            row_max(1)
            if nxt2:
                dve.wait_ge(rstd1_ready, s + 3)
                for t in range(TB):
                    ins = dve.tensor_scalar(XN[u][:, t, :], X[u][:, t, :], mv1[u][:, t, 0:1], rstd1[u][:, t:t + 1],
                                            ALU.subtract, ALU.mult)
                ins.then_inc(xn_ready, 1)
            row_max(2)
            row_max(3)
            if fin:
                dve.wait_ge(proj_done, s)
                dve.wait_ge(xb_ready, s)
                if not isinstance(s, int) or s >= 3:
                    dve.wait_ge(x1_stored[v], 16 * (i + (c - 1) // 2))
                dve.tensor_tensor(X1[v][:, :, :], misc_b[:, :].rearrange("p (t d) -> p t d", d=D), XB[v][:, :, :],
                                  ALU.add).then_inc(x1_ready, 1)
                dve.wait_ge(x1_ready, s)
                for t in range(TB):
                    dve.bn_stats(bn2[v][:, t, :], X1[v][:, t, :]).then_inc(stats2_a, 1)
                dve.wait_ge(stats2_a, TB * s)
                dve.sem_inc(dve_passed, 1)
                for t in range(TB):
                    ins = dve.bn_aggr(mv2[v][:, t, :], bn2[v][:, t, :])
                ins.then_inc(stats2_ready, 1)
            row_max(4)
            if nxt2:
                dve.wait_ge(kh_ready, s + 3)
                wait(dve, klp_ready, s + 1)
                for half in range(2):
                    rows = slice(HP * half, HP * (half + 1))
                    ins = dve.tensor_tensor(KL[u][rows, half, :, :], misc_a[rows, 0:KD * M].rearrange("p (k m) -> p k m", m=M),
                                            KH[u][rows, half, :, :].bitcast(FP32), ALU.subtract)
                ins.then_inc(kl_ready, 1)
            if fin:
                dve.wait_ge(rstd2_ready, s)
                if not isinstance(s, int) or s >= 3:
                    dve.wait_ge(xn2_stored[v], 16 * (i + (c - 1) // 2))
                for t in range(TB):
                    ins = dve.tensor_scalar(XN2[v][:, t, :], X1[v][:, t, :], mv2[v][:, t, 0:1], rstd2[v][:, t:t + 1],
                                            ALU.subtract, ALU.mult)
                ins.then_inc(xn2_ready, 1)
            row_max(5)
            row_max(6)
            row_max(7)

        run(dve, step)
        keep_logits(B + 1)

    @block.tensor
    def _(pe):
        pe.wait_ge(const_ready, 1)
        pe.wait_ge(wk_loaded, 16)

        def step(i, c, nxt2, nxt1, now, fin):
            s, u, v = 2 * i + c, c % 2, (c + 1) % 2

            def transpose_rows(misc, src, done):
                for k in range(KD):
                    for t in range(TB):
                        ins = pe.transpose(misc[:, k * S + t * P:k * S + (t + 1) * P], src[:, t, k * P:(k + 1) * P],
                                           ident[:, :])
                ins.then_inc(done, 1)

            def scores(j):
                if not now:
                    return
                if j == 0:
                    pe.wait_ge(nmT_ready, s + 1)
                    pe.wait_ge(klp_ready, s + 1)
                    pe.wait_ge(qhm_ready, s + 1)
                wait(pe, exp_ready, NU * s + j - 1)
                for r in range(SU):
                    h = SU * j + r
                    g, half = h // (2 * HQ), h // HQ % 2
                    o = score_bank[j % 2][0:M, r * S:(r + 1) * S]
                    pe.matmul(o, KHZ[u][:, h, :], QHL[u][:, half, g, :], start=True, stop=False)
                    ins = pe.matmul(o, KLP[u][:, h, :], QHM[u][:, half, g, :], start=False, stop=True)
                ins.then_inc(score_done, 1)

            def weigh(k, b, w):
                if k == 0:
                    wait(pe, on_ready, b)
                    pe.wait_ge(va_ready, b + 1)
                pe.wait_ge(exp_ready, NU * b + 2 * (k + 1))
                for c4 in range(4):
                    h = 4 * k + c4
                    ins = pe.matmul(pv_bank[k // 2][2 * DH * c4:2 * DH * (c4 + 1), (k % 2) * S:(k % 2 + 1) * S],
                                    VA[w][0:M, h, :], PT[w][0:M, h, :], start=True, stop=True)
                ins.then_inc(pv_done, 1)

            def max_scores(q):
                if not nxt1:
                    return
                t, hq = q // (H // MU), q % (H // MU)
                if q == 0:
                    pe.wait_ge(ql_ready, s + 2)
                    pe.wait_ge(khz_ready, s + 2)
                    wait(pe, logit_ready, s - 1)
                wait(pe, max_ready, NQ * (s + 1) + q - 1)
                pe.matmul(smax_bank[q % 2][:, 0:MU * M], QHL[v][:, hq % 2, hq // 2, t * P:(t + 1) * P],
                          KHZ[v][:, MU * hq:MU * (hq + 1), :], start=True, stop=True).then_inc(smax_done, 1)

            def keys():
                pe.wait_ge(ctx_loaded[u], 16 * (i + (c + 2) // 2 + 1))
                if fin:
                    pe.wait_ge(oT_ready, s)
                else:
                    wait(pe, kl_ready, s + 2)
                    wait(pe, nmT_ready, s + 1)
                for g in range(KD):
                    for k in range(KD):
                        ins = pe.matmul(misc_a[:, g * M:(g + 1) * M], wk_sb[:, k, g * P:(g + 1) * P], CTX[u][:, k, :],
                                        start=k == 0, stop=k == KD - 1)
                ins.then_inc(k_done, 1)

            def queries(g):
                if isinstance(s, int) and s == -2:
                    pe.wait_ge(w_loaded, 16 * 7)
                pe.wait_ge(xnT_ready, s + 3)
                for k in range(KD):
                    ins = pe.matmul(misc_b[:, g * S:(g + 1) * S], wq_sb[:, k, g * P:(g + 1) * P], XNT[u][:, k, :],
                                    start=k == 0, stop=k == KD - 1)
                if g == KD - 1:
                    ins.then_inc(q_done, 1)

            def values():
                pe.wait_ge(ctx_loaded[v], 16 * (i + (c + 1) // 2 + 1))
                pe.wait_ge(ql_ready, s + 2)
                for k in range(KD):
                    ins = pe.matmul(misc_b[0:M, 0:D], CTX[v][:, k, :], wv_sb[:, k, :], start=k == 0, stop=k == KD - 1)
                ins.then_inc(v_done, 1)

            def by_token():
                pe.wait_ge(pvs_ready, 2 * s)
                for k in range(4):
                    for t in range(TB):
                        ins = pe.transpose(pv_bank[t][:, k * P:(k + 1) * P],
                                           PVS[:, k // 2, (k % 2) * S + t * P:(k % 2) * S + (t + 1) * P], ident[:, :])
                ins.then_inc(tok_done, 1)

            def attended():
                pe.wait_ge(on_ready, s)
                wait(pe, nmT_ready, s + 1 if now else 0)
                transpose_rows(misc_a, ON[v], oT_done)

            def project(t):
                pe.wait_ge(oT_ready, s)
                if nxt1:
                    pe.wait_ge(va_ready, s + 2)
                else:
                    wait(pe, x1_ready, s - 1)
                for k in range(KD):
                    ins = pe.matmul(misc_b[:, t * D:(t + 1) * D], OT[v][:, k, t * P:(t + 1) * P], wp_sb[:, k, :],
                                    start=k == 0, stop=k == KD - 1)
                if t == TB - 1:
                    ins.then_inc(proj_done, 1)

            def normalised():
                pe.wait_ge(xn2_ready, s)
                if now:
                    pe.wait_ge(pvs_ready, 2 * s + 1)
                transpose_rows(pv_bank[0], XN2[v], xn2T_done)

            def router_logits():
                pe.wait_ge(xn2T_ready, s)
                if nxt1:
                    pe.wait_ge(max_ready, NQ * (s + 1) + (NQ - 1))
                for t in range(TB):
                    for k in range(KD):
                        ins = pe.matmul(smax_bank[0][:, t * E:(t + 1) * E], XN2T[v][:, k, t * P:(t + 1) * P], rw_sb[:, k, :],
                                        start=k == 0, stop=k == KD - 1)
                ins.then_inc(logit_done, 1)

            def next_rows():
                pe.wait_ge(xn_ready, s + 3)
                if fin:
                    pe.wait_ge(x1_ready, s)
                elif nxt1:
                    pe.wait_ge(va_ready, s + 2)
                transpose_rows(misc_b, XN[u], xnT_done)

            def maxima():
                pe.wait_ge(max_ready, NQ * (s + 2))
                if nxt2:
                    pe.wait_ge(kl_ready, s + 3)
                elif fin:
                    pe.wait_ge(oT_ready, s)
                for t in range(TB):
                    ins = pe.transpose(misc_a[:, t * P:(t + 1) * P], NM[v][:, t, :], ident[:, :])
                ins.then_inc(nmT_done, 1)

            scores(0)
            if fin:
                weigh(3, s - 1, v)
            scores(1)
            scores(2)
            if fin:
                by_token()
            scores(3)
            if nxt1:
                values()
            max_scores(0)
            if fin:
                attended()
            if now:
                weigh(0, s, u)
            max_scores(1)
            scores(4)
            max_scores(2)
            if fin:
                project(0)
            max_scores(3)
            if fin:
                project(1)
            max_scores(4)
            if nxt2:
                keys()
            max_scores(5)
            scores(5)
            if now:
                weigh(1, s, u)
            if nxt2:
                next_rows()
            scores(6)
            if now:
                weigh(2, s, u)
            max_scores(6)
            scores(7)
            if fin:
                normalised()
            max_scores(7)
            if nxt2:
                queries(0)
            if nxt1:
                maxima()
            if nxt2:
                queries(1)
            if fin:
                router_logits()

        run(pe, step)


def search_constants(pool, consts, same_e, same_e_below, same_e16, zero_row):
    pool.memset(same_e[:, :], 0.0).then_inc(consts, 1)
    pool.memset(zero_row[:, :], 0.0).then_inc(consts, 1)
    n = 2
    for k in range(-(NC - 1), NC):
        pool.wait_ge(consts, n)
        pool.affine_select(out=same_e[:, :], in_=same_e[:, :], compare_op=ALU.not_equal, fill=1.0, base=k * E,
                           pattern=[[-1, P]], channel_multiplier=1).then_inc(consts, 1)
        n += 1
    pool.wait_ge(consts, n)
    pool.affine_select(out=same_e_below[:, :], in_=same_e[:, :], compare_op=ALU.is_gt, fill=0.0, base=0,
                       pattern=[[1, P]], channel_multiplier=-1).then_inc(consts, 1)
    pool.tensor_copy(same_e16[:, :], same_e[:, :]).then_inc(consts, 1)


def sum_experts(eng, tree, src, ready):
    for k, dst in enumerate(tree):
        w = E >> (k + 1)
        if k:
            eng.wait_ge(ready, k)
        eng.tensor_tensor(dst[:, :, :], src[:, :, 0:w], src[:, :, w:2 * w], ALU.add).then_inc(ready, 1)
        src = dst


def search_phase(nc, ctx, sem, bank, ident, L, probs, same_e, same_e_below, same_e16, zero_row):
    def sb(name, shape, dt):
        return ctx.enter_context(nc.sbuf_tensor(name, shape, dt))

    LT = sb("LT", [P, CT], FP32)
    LP = sb("LP", [P, TC, NC * E], FP32)
    junk = sb("junk", [P, CT], FP32)
    eq = sb("eq", [P, CT], FP32)
    gt = sb("gt", [P, CT], FP32)
    prefix = sb("prefix", [P, CT], FP32)
    chosen = sb("chosen", [P, CT], FP32)
    slot = sb("slot", [P, CT], FP32)
    cand, missed, both = (sb(n, [P, 1], U32) for n in ("cand", "missed", "both"))
    bit = [sb(f"bit{u}", [P, 1], U32) for u in range(2)]
    missed_i, cand_i = (sb(n, [P, 1], I32) for n in ("missed_i", "cand_i"))
    count16 = sb("count16", [P, 1], FP16)
    counts = sb("counts", [P, 2], FP32)
    need = sb("need", [P, 8], FP32)

    tree = [sb(f"tree{k}", [P, NT, E >> (k + 1)], FP32) for k in range(4)]
    expl = sb("expl", [P, NT, E], FP32)
    mx, rsm = sb("mx", [P, NT, 1], FP32), sb("rsm", [P, NT, 1], FP32)

    logits_t = bank[0:2]
    cnt_bank = bank[2]
    slots_t = bank[3:5]

    lp_ready, lt_done = sem("lp_ready"), sem("lt_done")
    step_dve, bit_ready = sem("step_dve"), sem("bit_ready")
    count_ready, total_done = sem("count_ready"), sem("total_done")
    mx_ready, lx_ready, ex_ready = sem("mx_ready"), sem("lx_ready"), sem("ex_ready")
    sum_ready, rsm_ready, probs_ready = sem("sum_ready"), sem("rsm_ready"), sem("probs_ready")
    slot_ready = sem("slot_ready")

    block = ctx.enter_context(nc.Block())

    @block.gpsimd
    def _(pool):
        pool.wait_ge(mx_ready, 1)
        pool.tensor_tensor(expl[:, :, :], L[:, :, :], mx[:, :, :].to_broadcast([P, NT, E]), ALU.subtract) \
            .then_inc(lx_ready, 1)
        pool.wait_ge(ex_ready, 1)
        sum_experts(pool, tree, expl, sum_ready)
        pool.wait_ge(rsm_ready, 1)
        pool.tensor_tensor(probs[:, :, :], expl[:, :, :], rsm[:, :, :].to_broadcast([P, NT, E]), ALU.mult) \
            .then_inc(probs_ready, 1)

    @block.scalar
    def _(act):
        act.wait_ge(lx_ready, 1)
        act.activation(expl[:, :, :], expl[:, :, :], ACT.Exp).then_inc(ex_ready, 1)

    @block.vector
    def _(dve):
        n = [0]

        def then(ins):
            n[0] += 1
            ins.then_inc(step_dve, 1)
            dve.wait_ge(step_dve, n[0])

        dve.tensor_copy(LP[:, :, :].rearrange("p j (c e) -> p j c e", e=E),
                        L[:, :, :].rearrange("p (c j) e -> p j c e", j=TC)).then_inc(lp_ready, 1)
        dve.tensor_reduce(mx[:, :, 0], L[:, :, :], axis=AX.X, op=ALU.max).then_inc(mx_ready, 1)
        dve.wait_ge(lt_done, 1)
        for j in range(2):
            ins = dve.tensor_copy(LT[:, 512 * j:512 * (j + 1)], logits_t[j][:, :])
        then(ins)

        dve.tensor_scalar(junk[:, :], LT[:, :], 0.0, None, ALU.is_ge, ALU.add, accum_out=count16[:, :]) \
            .then_inc(count_ready, 1)
        dve.memset(bit[0][:, :], 1 << 30).then_inc(bit_ready, 1)
        dve.wait_ge(total_done, 1)
        then(dve.tensor_scalar(missed_i[:, :], cnt_bank[:, 0:1], GMAX, None, ALU.is_lt))
        then(dve.tensor_scalar(cand_i[:, :], missed_i[:, :], 31, 31, ALU.logical_shift_left, ALU.arith_shift_right))
        dve.wait_ge(bit_ready, 1)
        then(dve.tensor_scalar(cand[:, :], cand_i[:, :].bitcast(U32), bit[0][:, :], None, ALU.bitwise_xor))
        base = n[0]

        def decide(turn, r):
            m = 3 * ROUNDS * turn + (base + 3 * r)
            dve.tensor_scalar(junk[:, :], LT[:, :], cand[:, :].bitcast(FP32), None, ALU.is_ge, ALU.add,
                              accum_out=count16[:, :]).then_inc(count_ready, 1)
            dve.tensor_scalar(bit[(r + 1) % 2][:, :], bit[r % 2][:, :], 1, None, ALU.logical_shift_right) \
                .then_inc(bit_ready, 1)
            dve.wait_ge(bit_ready, ROUNDS * turn + (r + 2))
            dve.tensor_tensor(both[:, :], cand[:, :], bit[(r + 1) % 2][:, :], ALU.bitwise_xor).then_inc(step_dve, 1)
            dve.wait_ge(total_done, ROUNDS * turn + (r + 2))
            dve.tensor_scalar(missed[:, :], cnt_bank[:, 0:1], GMAX, bit[r % 2][:, :], ALU.is_lt, ALU.mult) \
                .then_inc(step_dve, 1)
            dve.wait_ge(step_dve, m + 2)
            dve.tensor_tensor(cand[:, :], both[:, :], missed[:, :], ALU.bitwise_xor).then_inc(step_dve, 1)
            dve.wait_ge(step_dve, m + 3)

        for r in range(31 % ROUNDS):
            decide(0, r)
        with dve.Fori(0, 31 // ROUNDS) as turn:
            for r in range(31 % ROUNDS, 31 % ROUNDS + ROUNDS):
                decide(turn, r)
        n[0] = base + 3 * 31
        dve.wait_ge(sum_ready, 4)
        dve.reciprocal(rsm[:, :, :], tree[3][:, :, :]).then_inc(rsm_ready, 1)
        thr = cand[:, :].bitcast(FP32)
        dve.tensor_scalar(gt[:, :], LT[:, :], thr, None, ALU.is_gt, ALU.add, accum_out=counts[:, 0:1]) \
            .then_inc(step_dve, 1)
        dve.tensor_scalar(eq[:, :], LT[:, :], thr, None, ALU.is_equal, ALU.add, accum_out=counts[:, 1:2]) \
            .then_inc(step_dve, 1)
        n[0] += 2
        dve.wait_ge(step_dve, n[0])
        dve.sem_inc(count_ready, 1)
        dve.wait_ge(total_done, 33)
        then(dve.tensor_copy(need[:, 0:4], cnt_bank[:, 0:4]))
        then(dve.tensor_scalar(need[:, 4:5], need[:, 0:1], -1.0, float(CAP), ALU.mult, ALU.add))
        then(dve.tensor_tensor(need[:, 5:6], need[:, 3:4], need[:, 4:5], ALU.min))
        then(dve.tensor_tensor(need[:, 6:7], need[:, 5:6], need[:, 2:3], ALU.add))
        then(dve.tensor_tensor_scan(prefix[:, :], eq[:, :], zero_row[:, :], need[:, 3:4], ALU.add, ALU.add))
        then(dve.scalar_tensor_tensor(eq[:, :], prefix[:, :], need[:, 4:5], eq[:, :], ALU.is_le, ALU.mult))
        then(dve.tensor_tensor(chosen[:, :], gt[:, :], eq[:, :], ALU.add))
        then(dve.tensor_tensor_scan(prefix[:, :], chosen[:, :], zero_row[:, :], need[:, 6:7], ALU.add, ALU.add))
        dve.tensor_tensor(slot[:, :], prefix[:, :], chosen[:, :], ALU.mult).then_inc(slot_ready, 1)

    @block.tensor
    def _(pe):
        pe.wait_ge(lp_ready, 1)
        for j in range(TC):
            ins = pe.transpose(logits_t[j // 4][:, P * (j % 4):P * (j % 4 + 1)],
                               LP[:, j, :], ident[:, :])
        ins.then_inc(lt_done, 1)

        def total(turn, r):
            pe.wait_ge(count_ready, ROUNDS * turn + (r + 1))
            pe.matmul(cnt_bank[:, 0:1], same_e16[:, :], count16[:, :], start=True, stop=True).then_inc(total_done, 1)

        for r in range(32 % ROUNDS or ROUNDS):
            total(0, r)
        with pe.Fori(1, 32 // ROUNDS) as turn:
            for r in range(ROUNDS):
                total(turn, r)
        pe.wait_ge(count_ready, 33)
        pe.matmul(cnt_bank[:, 0:2], same_e[:, :], counts[:, :], start=True, stop=True)
        pe.matmul(cnt_bank[:, 2:4], same_e_below[:, :], counts[:, :], start=True, stop=True).then_inc(total_done, 1)
        pe.wait_ge(slot_ready, 1)
        for j in range(TC):
            ins = pe.transpose(slots_t[j // 4][:, P * (j % 4):P * (j % 4 + 1)], slot[:, P * j:P * (j + 1)], ident[:, :])


def front_tensors(nc, ctx, sem):
    def sb(name, shape, dt):
        return ctx.enter_context(nc.sbuf_tensor(name, shape, dt))

    return {
        "W1": sb("W1", [P, KD, F], FP32), "W2": sb("W2", [P, KF, D], FP32),
        "W1H": sb("W1H", [P, KD, F], FP32R), "W1L": sb("W1L", [P, KD, F], FP32R),
        "W2H": sb("W2H", [P, KF, D], FP32R), "W2L": sb("W2L", [P, KF, D], FP32R),
        "B1": sb("B1", [P, E * KF], FP32), "NW": sb("NW", [P, KD], FP32),
        "XG": [sb(f"XG{u}", [P, GT, D], FP32) for u in range(2)],
        "G": [sb(f"G{u}", [P, GT], FP32) for u in range(2)],
        "w1_loaded": sem("w1_loaded"), "w2_loaded": sem("w2_loaded"), "c_loaded": sem("c_loaded"),
        "w1h_ready": sem("w1h_ready"), "w1l_ready": sem("w1l_ready"),
        "w2h_ready": sem("w2h_ready"), "w2l_ready": sem("w2l_ready"),
        "ids": [sb(f"ids{g}", [P, SB // GT, 3, GT], I32) for g in range(E // EG)],
        "gathered": [sem(f"gathered{u}") for u in range(2)], "ids_moved": [sem(f"ids_moved{g}") for g in range(E // EG)],
    }


def slots_phase(nc, ctx, sem, bank, probs, front, idx, gate_table, xn_table, w1T, b1, w2T, nw):
    def sb(name, shape, dt):
        return ctx.enter_context(nc.sbuf_tensor(name, shape, dt))

    def pair(name, shape, dt):
        return [sb(f"{name}{u}", shape, dt) for u in range(2)]

    slot_t = sb("slot_t", [P, NT, E], I32)
    half_i = pair("half_i", [P, NT, E], I32)
    slot_a, slot_b = sb("slot_a", [P, NT, E], BF16), sb("slot_b", [P, NT, E], BF16)
    taken = sb("taken", [P, NT, E], FP32)
    gates = sb("gates", [P, NT, E], FP32)
    tree = [sb(f"gate_tree{k}", [P, NT, E >> (k + 1)], FP32) for k in range(4)]
    no_gate, gate_sum, gate_scale = (sb(n, [P, NT, 1], FP32) for n in ("no_gate", "gate_sum", "gate_scale"))
    p_col = sb("p_col", [P, 1], FP32)
    e_col = sb("e_col", [P, E // EG], FP32)
    t_val = sb("t_val", [P, NT, EG], BF16)
    hot_a = pair("hot_a", [P, SA, NT * EG], BF16)
    hot_b = pair("hot_b", [P, SB, NT * EG], BF16)
    val_b = pair("val_b", [P, 2, SB, NT * EG], BF16)
    pt = [sb(f"pt{g}", [P, 2, SB], FP32) for g in range(E // EG)]
    scaled = [sb(f"scaled{g}", [P, 3, SB], FP32) for g in range(E // EG)]
    ids = front["ids"]

    slots_t = bank[3:5]
    idx_bank = bank[5:7]
    step_dve, consts = sem("slots_dve"), sem("slots_consts")
    taken_ready, gate_sum_ready, gate_scale_ready = sem("taken_ready"), sem("gate_sum_ready"), sem("gate_scale_ready")
    slot_t_ready, half_ready = sem("slot_t_ready"), sem("half_ready")
    hot_b_ready, val_ready, hot_ready = sem("hot_b_ready"), sem("val_ready"), sem("hot_ready")
    idx_done, ids_ready = sem("idx_done"), sem("ids_ready")
    gates_ready, gates_stored = sem("gates_ready"), sem("gates_stored")
    ids_moved, gathered = front["ids_moved"], front["gathered"]

    block = ctx.enter_context(nc.Block())

    @block.sync
    def _(sp):
        sp.dma_start(front["W1"][:, :, :], w1T[0:1, :, :].rearrange("o (k p) f -> p (o k) f", p=P)) \
            .then_inc(front["w1_loaded"], 16)
        sp.dma_start(front["W2"][:, :, :], w2T[0:1, :, :].rearrange("o (k p) d -> p (o k) d", p=P)) \
            .then_inc(front["w2_loaded"], 16)
        sp.dma_start(front["NW"][:, :], nw).then_inc(front["c_loaded"], 16)
        sp.dma_start(front["B1"][:, :], b1).then_inc(front["c_loaded"], 16)
        sp.wait_ge(gates_ready, 1)
        sp.dma_start(gate_table.rearrange("(p r) o -> p (r o)", p=P), gates[:, :, :].rearrange("p t e -> p (t e)")) \
            .then_inc(gates_stored, 16)
        for g in range(E // EG):
            sp.wait_ge(ids_ready, 3 * (g + 1))
            for e in range(EG):
                sp.dma_start(idx[:, EG * g + e, :, :].rearrange("p k r -> p (k r)"),
                             ids[g][SA * e:SA * (e + 1), :, :, :].rearrange("a q k r -> a (q k r)")) \
                    .then_inc(ids_moved[g], 16)
        sp.wait_ge(gates_stored, 16)

    @block.gpsimd
    def _(pool):
        pool.iota(p_col[:, :], pattern=[[0, 1]], base=0, channel_multiplier=1,
                  allow_small_or_imprecise_dtypes=True).then_inc(consts, 1)
        pool.iota(t_val[:, :, :], pattern=[[1, NT], [0, EG]], base=0, channel_multiplier=0,
                  allow_small_or_imprecise_dtypes=True).then_inc(consts, 1)

        pool.wait_ge(taken_ready, 1)
        pool.tensor_tensor(gates[:, :, :], probs[:, :, :], taken[:, :, :], ALU.mult).then_inc(taken_ready, 1)
        pool.wait_ge(taken_ready, 2)
        sum_experts(pool, tree, gates, gate_sum_ready)
        pool.wait_ge(gate_scale_ready, 1)
        pool.tensor_tensor(gates[:, :, :], probs[:, :, :], gate_scale[:, :, :].to_broadcast([P, NT, E]), ALU.mult) \
            .then_inc(gates_ready, 1)

        for w in ("1", "2"):
            pool.wait_ge(front[f"w{w}h_ready"], 1)
            pool.tensor_tensor(front[f"W{w}L"][:, :, :], front[f"W{w}"][:, :, :], front[f"W{w}H"][:, :, :].bitcast(FP32),
                               ALU.subtract).then_inc(front[f"w{w}l_ready"], 1)
        pool.wait_ge(ids_moved[0], 16 * EG)
        pool.wait_ge(gates_stored, 16)
        for e in range(2):
            for g in range(GT):
                pool.indirect_dma_start(out=front["XG"][e][:, g, :], out_offset=None, in_=xn_table,
                                        in_offset=bass.IndirectOffsetOnAxis(ap=idx[:, e, 0, g:g + 1], axis=0)) \
                    .then_inc(gathered[e], 16)
                pool.indirect_dma_start(out=front["G"][e][:, g:g + 1], out_offset=None, in_=gate_table,
                                        in_offset=bass.IndirectOffsetOnAxis(ap=idx[:, e, 2, g:g + 1], axis=0)) \
                    .then_inc(gathered[e], 16)

    @block.scalar
    def _(act):
        act.wait_ge(consts, 2)
        for g in range(E // EG):
            act.wait_ge(hot_b_ready, g + 1)
            if g >= 2:
                act.wait_ge(idx_done, g - 1)
            act.activation(val_b[g % 2][:, 0, :, :], hot_b[g % 2][:, :, :], ACT.Copy, scale=p_col[:, :]) \
                .then_inc(val_ready, 1)
            if g < 2:
                w = str(g + 1)
                act.wait_ge(front[f"w{w}_loaded"], 16)
                act.activation(front[f"W{w}H"][:, :, :], front[f"W{w}"][:, :, :], ACT.Copy) \
                    .then_inc(front[f"w{w}h_ready"], 1)

    @block.vector
    def _(dve):
        n = [0]

        def then(ins):
            n[0] += 1
            ins.then_inc(step_dve, 1)
            dve.wait_ge(step_dve, n[0])

        for j in range(TC):
            ins = dve.tensor_scalar(slot_t[:, j::TC, :],
                                    slots_t[j // 4][:, P * (j % 4):P * (j % 4 + 1)].rearrange("p (c e) -> p c e", e=E),
                                    -1.0, None, ALU.add)
        ins.then_inc(slot_t_ready, 1)
        dve.wait_ge(slot_t_ready, 1)
        dve.tensor_scalar(half_i[0][:, :, :], slot_t[:, :, :], 4, None, ALU.arith_shift_right).then_inc(half_ready, 1)
        dve.tensor_scalar(half_i[1][:, :, :], slot_t[:, :, :], SB - 1, None, ALU.bitwise_and).then_inc(half_ready, 1)
        dve.wait_ge(half_ready, 2)
        dve.tensor_copy(slot_a[:, :, :], half_i[0][:, :, :]).then_inc(half_ready, 1)
        dve.tensor_copy(slot_b[:, :, :], half_i[1][:, :, :]).then_inc(half_ready, 1)
        dve.tensor_scalar(taken[:, :, :], slot_t[:, :, :], 0.0, None, ALU.is_ge).then_inc(taken_ready, 1)
        dve.wait_ge(half_ready, 4)
        dve.wait_ge(consts, 2)

        def hot(g):
            es, w = slice(EG * g, EG * (g + 1)), g % 2
            if g >= 2:
                dve.wait_ge(idx_done, g - 1)
            for b in range(SB):
                ins = dve.tensor_scalar(hot_b[w][:, b, :].rearrange("p (t e) -> p t e", e=EG), slot_b[:, :, es], float(b),
                                        None, ALU.is_equal)
            ins.then_inc(hot_b_ready, 1)
            dve.wait_ge(hot_b_ready, g + 1)
            dve.tensor_tensor(val_b[w][:, 1, :, :], hot_b[w][:, :, :],
                              t_val[:, :, :].rearrange("p (o t) e -> p o (t e)", o=1).to_broadcast([P, SB, NT * EG]),
                              ALU.mult)
            for a in range(SA):
                ins = dve.tensor_scalar(hot_a[w][:, a, :].rearrange("p (t e) -> p t e", e=EG), slot_a[:, :, es], float(a),
                                        None, ALU.is_equal)
            ins.then_inc(hot_ready, 1)

        def by_four(a):
            return a.rearrange("p (q r) -> p q r", r=GT)

        def finish_ids(g):
            dve.wait_ge(idx_done, g + 1)
            if g == 0:
                dve.wait_ge(consts, 2 + E)
            then(dve.tensor_copy(pt[g][:, :, :], idx_bank[g % 2][:, 0:2 * SB].rearrange("p (k b) -> p k b", k=2)))
            dve.tensor_scalar(scaled[g][:, 0, :], pt[g][:, 0, :], float(NT), None, ALU.mult).then_inc(step_dve, 1)
            dve.tensor_scalar(scaled[g][:, 1, :], pt[g][:, 1, :], float(P), None, ALU.mult).then_inc(step_dve, 1)
            n[0] += 2
            dve.wait_ge(step_dve, n[0])
            dve.tensor_tensor(ids[g][:, :, 0, :], by_four(scaled[g][:, 0, :]), by_four(pt[g][:, 1, :]), ALU.add).then_inc(ids_ready, 1)
            dve.tensor_tensor(ids[g][:, :, 1, :], by_four(scaled[g][:, 1, :]), by_four(pt[g][:, 0, :]), ALU.add).then_inc(ids_ready, 1)
            then(dve.tensor_tensor(scaled[g][:, 2, :], scaled[g][:, 0, :], pt[g][:, 1, :], ALU.add))
            dve.tensor_scalar(ids[g][:, :, 2, :], by_four(scaled[g][:, 2, :]), float(E), e_col[:, g:g + 1], ALU.mult, ALU.add) \
                .then_inc(ids_ready, 1)

        hot(0)
        for e in range(EG):
            for g in range(E // EG):
                dve.memset(e_col[SA * e:SA * (e + 1), g:g + 1], float(EG * g + e)).then_inc(consts, 1)
        dve.wait_ge(gate_sum_ready, 4)
        then(dve.tensor_scalar(no_gate[:, :, :], tree[3][:, :, :], 0.0, None, ALU.is_equal))
        then(dve.tensor_tensor(gate_sum[:, :, :], tree[3][:, :, :], no_gate[:, :, :], ALU.add))
        dve.reciprocal(gate_scale[:, :, :], gate_sum[:, :, :]).then_inc(gate_scale_ready, 1)
        for g in range(1, E // EG):
            hot(g)
            finish_ids(g - 1)
        finish_ids(E // EG - 1)

    @block.tensor
    def _(pe):
        for g in range(E // EG):
            pe.wait_ge(hot_ready, g + 1)
            pe.wait_ge(val_ready, g + 1)
            if g >= 2:
                pe.wait_ge(ids_ready, 3 * (g - 1))
            for t in range(NT):
                for e in range(EG):
                    ins = pe.matmul(idx_bank[g % 2][SA * e:SA * (e + 1), 0:2 * SB], hot_a[g % 2][:, :, EG * t + e],
                                    val_b[g % 2][:, :, :, EG * t + e], start=t == 0, stop=t == NT - 1)
            ins.then_inc(idx_done, 1)


def expert_phase(nc, ctx, sem, bank, ident, front, idx, gate_table, xn_table, w1T, w2T, b2, out):
    def sb(name, shape, dt):
        return ctx.enter_context(nc.sbuf_tensor(name, shape, dt))

    def pair(name, shape, dt):
        return [sb(f"{name}{u}", shape, dt) for u in range(2)]

    W1, W2, W1H, W1L, W2H, W2L, B1, NW = (front[n] for n in ("W1", "W2", "W1H", "W1L", "W2H", "W2L", "B1", "NW"))
    XG, G, gathered, ids_moved = (front[n] for n in ("XG", "G", "gathered", "ids_moved"))
    B2 = pair("B2", [P, D], FP32)
    II, IG, IO = pair("II", [P, GT], I32), pair("IG", [P, GT], I32), pair("IO", [P, GT], I32)
    GK = pair("GK", [P, GT], FP32)
    XTH, XTL = pair("XTH", [P, KD, CAP], FP32R), pair("XTL", [P, KD, CAP], FP32R)
    HF = [sb(f"HF{n}", [P, CAP], FP32) for n in range(4)]
    HH, HL = pair("HH", [P, KF, CAP], FP32R), pair("HL", [P, KF, CAP], FP32R)
    Y0 = sb("Y0", [P, GT, D], FP32)
    C = pair("C", [P, GT, D], FP32)

    xt_bank = bank[0:2]
    h_bank = bank[2:6]
    y_bank = bank[6:8]

    b2_loaded = [sem(f"b2_loaded{u}") for u in range(2)]
    w1_loaded, w2_loaded, c_loaded = front["w1_loaded"], front["w2_loaded"], front["c_loaded"]
    w1h_ready, w1l_ready, w2h_ready, w2l_ready = (front[n] for n in ("w1h_ready", "w1l_ready", "w2h_ready", "w2l_ready"))
    idx_ready = sem("idx_ready")
    xt_done, xth_ready, xt_ready = sem("xt_done"), sem("xth_ready"), sem("xt_ready")
    h_done, hf_ready, hh_ready, hl_ready = sem("h_done"), sem("hf_ready"), sem("hh_ready"), sem("hl_ready")
    y_done, y0_ready, c_ready = sem("y_done"), sem("y0_ready"), sem("c_ready")
    added, gk_ready = sem("added"), sem("gk_ready")
    y_half, c_half = sem("y_half"), sem("c_half")
    pool_passed = sem("pool_passed_e")

    block = ctx.enter_context(nc.Block())

    @block.sync
    def _(sp):
        def load_1(e):
            sp.wait_ge(w1l_ready, e)
            sp.dma_start(W1[:, :, :], w1T[bass.ds(e, 1), :, :].rearrange("o (k p) f -> p (o k) f", p=P)) \
                .then_inc(w1_loaded, 16)

        def load_2(e):
            sp.wait_ge(w2l_ready, e)
            sp.dma_start(W2[:, :, :], w2T[bass.ds(e, 1), :, :].rearrange("o (k p) d -> p (o k) d", p=P)) \
                .then_inc(w2_loaded, 16)

        def load_b(e, u, first=False):
            if not first:
                sp.wait_ge(y0_ready, e - 1)
            sp.dma_start(B2[u][:, :], b2[bass.ds(e, 1), :].to_broadcast([P, D])).then_inc(b2_loaded[u], 16)

        load_1(1)
        load_b(0, 0, True)
        load_b(1, 1, True)
        load_2(1)
        with sp.Fori(1, E // 2) as i:
            for u in range(2):
                load_1(2 * i + u)
                load_2(2 * i + u)
                load_b(2 * i + u, u)

    @block.gpsimd
    def _(pool):
        def gather(i, u):
            e = 2 * i + u
            pool.wait_ge(idx_ready, e - 1)
            pool.wait_ge(xt_done, e - 1)
            pool.wait_ge(gk_ready, e - 1)
            pool.sem_inc(pool_passed, 1)
            for g in range(GT):
                pool.indirect_dma_start(out=XG[u][:, g, :], out_offset=None, in_=xn_table,
                                        in_offset=bass.IndirectOffsetOnAxis(ap=II[u][:, g:g + 1], axis=0)) \
                    .then_inc(gathered[u], 16)
                pool.indirect_dma_start(out=G[u][:, g:g + 1], out_offset=None, in_=gate_table,
                                        in_offset=bass.IndirectOffsetOnAxis(ap=IG[u][:, g:g + 1], axis=0)) \
                    .then_inc(gathered[u], 16)

        def add_up(i, u, first):
            e = 2 * i + u
            pool.wait_ge(c_ready, e + 1)
            if not first:
                pool.wait_ge(added, 16 * GT * e)
            pool.sem_inc(pool_passed, 1)
            for g in range(GT):
                pool.indirect_dma_start(out=out, in_=C[u][:, g, :], in_offset=None, compute_op=ALU.add,
                                        out_offset=bass.IndirectOffsetOnAxis(ap=IO[u][:, g:g + 1], axis=0)) \
                    .then_inc(added, 16)

        gather(1, 0)
        with pool.Fori(1, E // 2 - 1) as i:
            gather(i, 1)
            add_up(i - 1, 0, False)
            gather(i + 1, 0)
            add_up(i - 1, 1, False)
        gather(E // 2 - 1, 1)
        add_up(E // 2 - 2, 0, False)
        add_up(E // 2 - 2, 1, False)
        add_up(E // 2 - 1, 0, False)
        for half, ready, count in ((0, c_half, 1), (1, c_ready, E)):
            pool.wait_ge(ready, count)
            if half == 0:
                pool.wait_ge(added, 16 * GT * (E - 1))
            pool.sem_inc(pool_passed, 1)
            for g in range(2 * half, 2 * half + 2):
                pool.indirect_dma_start(out=out, in_=C[1][:, g, :], in_offset=None, compute_op=ALU.add,
                                        out_offset=bass.IndirectOffsetOnAxis(ap=IO[1][:, g:g + 1], axis=0)) \
                    .then_inc(added, 16)
        pool.wait_ge(added, 16 * GT * E)

    @block.vector
    def _(dve):
        def indices(i, u, first):
            e = 2 * i + u
            if not first:
                dve.wait_ge(gathered[u], 16 * 2 * GT * i)
            dve.tensor_copy(II[u][:, :], idx[:, bass.ds(e, 1), 0, :].rearrange("p o g -> p (o g)"))
            dve.tensor_copy(IG[u][:, :], idx[:, bass.ds(e, 1), 2, :].rearrange("p o g -> p (o g)")).then_inc(idx_ready, 1)

        def split_1(e):
            dve.wait_ge(w1h_ready, e + 1)
            dve.wait_ge(h_done, KF * e)
            dve.tensor_tensor(W1L[:, :, :], W1[:, :, :], W1H[:, :, :].bitcast(FP32), ALU.subtract).then_inc(w1l_ready, 1)

        def split_2(e):
            dve.wait_ge(w2h_ready, e + 1)
            dve.wait_ge(y_done, e)
            dve.tensor_tensor(W2L[:, :, :], W2[:, :, :], W2H[:, :, :].bitcast(FP32), ALU.subtract).then_inc(w2l_ready, 1)

        def columns(i, u):
            e = 2 * i + u
            dve.wait_ge(xt_done, e + 1)
            for k in range(KD):
                ins = dve.tensor_scalar(XTH[u][:, k, :], xt_bank[k][:, :], NW[:, k:k + 1], None, ALU.mult)
            ins.then_inc(xth_ready, 1)
            dve.wait_ge(xth_ready, e + 1)
            for k in range(KD):
                ins = dve.scalar_tensor_tensor(XTL[u][:, k, :], xt_bank[k][:, :], NW[:, k:k + 1],
                                               XTH[u][:, k, :].bitcast(FP32), ALU.mult, ALU.subtract)
            ins.then_inc(xt_ready, 1)

        def keep_gates(i, u):
            e = 2 * i + u
            if not isinstance(e, int) or e >= 2:
                dve.wait_ge(c_ready, e - 1)
            dve.wait_ge(gathered[u], 16 * 2 * GT * (i + 1))
            dve.tensor_copy(GK[u][:, :], G[u][:, :]).then_inc(gk_ready, 1)

        def hidden(i, u):
            e = 2 * i + u
            for f in range(KF):
                dve.wait_ge(hh_ready, KF * e + (f + 1))
                dve.tensor_tensor(HL[u][:, f, :], HF[f % 4][:, :], HH[u][:, f, :].bitcast(FP32), ALU.subtract) \
                    .then_inc(hl_ready, 1)

        def contributions(i, u, first=False):
            e = 2 * i + u
            if not first:
                dve.wait_ge(added, 16 * GT * (e - 1))
            if not first or u:
                dve.wait_ge(c_ready, e)
            dve.tensor_copy(IO[u][:, :], idx[:, bass.ds(e, 1), 1, :].rearrange("p o g -> p (o g)"))
            dve.wait_ge(y_done, e + 1)
            dve.wait_ge(b2_loaded[u], 16 * (i + 1))
            for j in range(2):
                ins = dve.tensor_tensor(Y0[:, 2 * j:2 * j + 2, :], y_bank[j][:, :].rearrange("p (g d) -> p g d", d=D),
                                        B2[u][:, :].rearrange("p (o d) -> p o d", o=1).to_broadcast([P, 2, D]), ALU.add)
            ins.then_inc(y0_ready, 1)
            dve.wait_ge(y0_ready, e + 1)
            for g in range(GT):
                ins = dve.tensor_scalar(C[u][:, g, :], Y0[:, g, :], GK[u][:, g:g + 1], None, ALU.mult)
            ins.then_inc(c_ready, 1)

        def turn(i, u, ahead=True, first=False):
            e = 2 * i + u
            split_1(e)
            if ahead:
                indices(i + u, 1 - u, isinstance(e, int) and e == 2)
            columns(i, u)
            contributions(i - 1, u, first)
            keep_gates(i, u)
            split_2(e - 1)
            hidden(i, u)

        dve.wait_ge(c_loaded, 32)
        columns(0, 0)
        keep_gates(0, 0)
        hidden(0, 0)
        split_1(1)
        for g in range(E // EG):
            dve.wait_ge(ids_moved[g], 16 * EG)
        indices(1, 0, True)
        columns(0, 1)
        keep_gates(0, 1)
        hidden(0, 1)
        turn(1, 0, first=True)
        turn(1, 1, first=True)
        with dve.Fori(2, E // 2 - 1) as i:
            turn(i, 0)
            turn(i, 1)
        turn(E // 2 - 1, 0)
        turn(E // 2 - 1, 1, ahead=False)
        split_2(E - 1)
        contributions(E // 2 - 1, 0)
        dve.wait_ge(added, 16 * GT * (E - 2))
        dve.wait_ge(c_ready, E - 1)
        dve.tensor_copy(IO[1][:, :], idx[:, E - 1, 1, :])
        dve.wait_ge(b2_loaded[1], 16 * (E // 2))
        for half, done, count in ((0, y_half, 1), (1, y_done, E)):
            dve.wait_ge(done, count)
            dve.tensor_tensor(Y0[:, 2 * half:2 * half + 2, :], y_bank[half][:, :].rearrange("p (g d) -> p g d", d=D),
                              B2[1][:, :].rearrange("p (o d) -> p o d", o=1).to_broadcast([P, 2, D]), ALU.add) \
                .then_inc(y0_ready, 1)
            dve.wait_ge(y0_ready, E + half)
            for g in range(2 * half, 2 * half + 2):
                ins = dve.tensor_scalar(C[1][:, g, :], Y0[:, g, :], GK[1][:, g:g + 1], None, ALU.mult)
            ins.then_inc((c_half, c_ready)[half], 1)

    @block.scalar
    def _(act):
        act.wait_ge(c_loaded, 32)

        def split_1(e):
            act.wait_ge(w1_loaded, 16 * (e + 1))
            act.wait_ge(h_done, KF * e)
            act.activation(W1H[:, :, :], W1[:, :, :], ACT.Copy).then_inc(w1h_ready, 1)

        def split_2(e):
            act.wait_ge(w2_loaded, 16 * (e + 1))
            act.wait_ge(y_done, e)
            act.activation(W2H[:, :, :], W2[:, :, :], ACT.Copy).then_inc(w2h_ready, 1)

        def hidden(i, u, first):
            e = 2 * i + u

            def high(f):
                act.wait_ge(hf_ready, KF * e + (f + 1))
                act.activation(HH[u][:, f, :], HF[f % 4][:, :], ACT.Copy).then_inc(hh_ready, 1)

            for f in range(KF):
                act.wait_ge(h_done, KF * e + (f + 1))
                if not isinstance(e, int) or e > 0 or f >= 4:
                    act.wait_ge(hl_ready, KF * e + (f - 3))
                act.activation(HF[f % 4][:, :], h_bank[f % 4][:, :], ACT.Gelu,
                               bias=B1[:, bass.ds(KF * e + f, 1)]).then_inc(hf_ready, 1)
                if f == 0 and not first:
                    act.wait_ge(y_done, e - 1)
                if f:
                    high(f - 1)
            high(KF - 1)

        hidden(0, 0, True)
        split_1(1)
        hidden(0, 1, True)
        with act.Fori(1, E // 2) as i:
            for u in range(2):
                split_1(2 * i + u)
                split_2(2 * i + (u - 1))
                hidden(i, u, False)
        split_2(E - 1)

    @block.tensor
    def _(pe):
        def columns(i, u, first):
            e = 2 * i + u
            pe.wait_ge(gathered[u], 16 * 2 * GT * (i + 1))
            if not first:
                pe.wait_ge(xt_ready, e)
            for k in range(KD):
                for g in range(GT):
                    ins = pe.transpose(xt_bank[k][:, g * P:(g + 1) * P], XG[u][:, g, k * P:(k + 1) * P], ident[:, :])
            ins.then_inc(xt_done, 1)

        def three(o, wh, wl, xh, xl, first, last):
            pe.matmul(o, wh, xh, start=first, stop=False)
            pe.matmul(o, wh, xl, start=False, stop=False)
            return pe.matmul(o, wl, xh, start=False, stop=last)

        def up(i, u, first):
            e = 2 * i + u
            pe.wait_ge(xt_ready, e + 1)
            pe.wait_ge(w1l_ready, e + 1)
            for f in range(KF):
                if not first or f >= 4:
                    pe.wait_ge(hf_ready, KF * e + (f - 3))
                for k in range(KD):
                    w = slice(f * P, (f + 1) * P)
                    ins = three(h_bank[f % 4][:, :], W1H[:, k, w], W1L[:, k, w], XTH[u][:, k, :], XTL[u][:, k, :],
                                k == 0, k == KD - 1)
                ins.then_inc(h_done, 1)

        def down(i, u, first):
            e = 2 * i + u
            if not first:
                pe.wait_ge(y0_ready, e)
            pe.wait_ge(w2l_ready, e + 1)
            pe.wait_ge(hl_ready, KF * (e + 1))
            for g in range(GT):
                for f in range(KF):
                    w = slice(g * P, (g + 1) * P)
                    ins = three(y_bank[g // 2][:, (g % 2) * D:(g % 2 + 1) * D], HH[u][:, f, w], HL[u][:, f, w],
                                W2H[:, f, :], W2L[:, f, :], f == 0, f == KF - 1)
                if isinstance(e, int) and e == E - 1 and g == 1:
                    ins.then_inc(y_half, 1)
            ins.then_inc(y_done, 1)

        columns(0, 0, True)
        up(0, 0, True)
        columns(0, 1, False)
        up(0, 1, False)
        columns(1, 0, False)
        down(0, 0, True)
        with pe.Fori(1, E // 2 - 1) as i:
            up(i, 0, False)
            columns(i, 1, False)
            down(i - 1, 1, False)
            up(i, 1, False)
            columns(i + 1, 0, False)
            down(i, 0, False)
        up(E // 2 - 1, 0, False)
        columns(E // 2 - 1, 1, False)
        down(E // 2 - 2, 1, False)
        up(E // 2 - 1, 1, False)
        down(E // 2 - 1, 0, False)
        down(E // 2 - 1, 1, False)


def program(nc, x, ctxT, wq, wk, wv, wp, bp, nw, rw, rb, w1T, b1, w2T, b2, out):
    xn_table = nc.dram_tensor("xn_table", [N, D], FP32, kind="Internal").ap()
    gate_table = nc.dram_tensor("gate_table", [N * E, 1], FP32, kind="Internal").ap()
    with ExitStack() as ctx:
        def sem(name):
            return ctx.enter_context(nc.semaphore(name))

        bank = [ctx.enter_context(nc.psum_tensor(f"bank{n}", [P, 512], FP32)) for n in range(8)]
        ident = ctx.enter_context(nc.sbuf_tensor("ident", [P, P], FP32))
        L = ctx.enter_context(nc.sbuf_tensor("L", [P, NT, E], FP32))
        idx = ctx.enter_context(nc.sbuf_tensor("idx", [P, E, 3, GT], I32))
        search_consts = [ctx.enter_context(nc.sbuf_tensor(name, shape, dt)) for name, shape, dt in
                         (("same_e", [P, P], FP32), ("same_e_below", [P, P], FP32), ("same_e16", [P, P], FP16),
                          ("zero_row", [P, CT], FP32))]
        with ExitStack() as phase:
            attention_phase(nc, phase, sem, bank, ident, L, search_consts, x, ctxT, wq, wk, wv, wp, bp, nw, rw, rb, out, xn_table)
        with ExitStack() as routed:
            probs = routed.enter_context(nc.sbuf_tensor("probs", [P, NT, E], FP32))
            with ExitStack() as phase:
                search_phase(nc, phase, sem, bank, ident, L, probs, *search_consts)
            front = front_tensors(nc, routed, sem)
            with ExitStack() as phase:
                slots_phase(nc, phase, sem, bank, probs, front, idx, gate_table, xn_table,
                            w1T, b1, w2T, nw)
            with ExitStack() as phase:
                expert_phase(nc, phase, sem, bank, ident, front, idx, gate_table, xn_table,
                             w1T, w2T, b2, out.rearrange("b s d -> (b s) d"))


def kernel(**inputs):
    import numpy as np
    import concourse.bacc as bacc
    from concourse.bass_utils import run_bass_kernel_spmd

    t = np.ascontiguousarray
    laid = {
        "x": t(inputs["x"]),
        "ctxT": t(np.transpose(inputs["ctx_1024"], (0, 2, 1))),
        "wq": t(inputs["L0_xattn_Wq"]), "wk": t(inputs["L0_xattn_Wk"]),
        "wv": t(inputs["L0_xattn_Wv"]), "wp": t(inputs["L0_xattn_Wp"]), "bp": t(inputs["L0_xattn_bp"]),
        "nw": t(np.transpose(np.reshape(inputs["L0_ffn_norm_weight"], (KD, P)))),
        "rw": t(np.transpose(inputs["L0_ffn_router_weight"])), "rb": t(inputs["L0_ffn_router_bias"]),
        "w1T": t(np.transpose(inputs["L0_ffn_fc1_weight"], (0, 2, 1))),
        "b1": t(np.transpose(np.reshape(inputs["L0_ffn_fc1_bias"], (E * KF, P)))),
        "w2T": t(np.transpose(inputs["L0_ffn_fc2_weight"], (0, 2, 1))),
        "b2": t(inputs["L0_ffn_fc2_bias"]),
    }
    nc = bacc.Bacc("TRN2", target_bir_lowering=False, num_devices=1)
    args = [nc.dram_tensor(f"{name}_dram", a.shape, mybir.dt.from_np(a.dtype), kind="ExternalInput").ap()
            for name, a in laid.items()]
    out = nc.dram_tensor("out_dram", (B, S, D), FP32, kind="ExternalOutput").ap()
    program(nc, *args, out)
    r = run_bass_kernel_spmd(nc, [{f"{name}_dram": a for name, a in laid.items()}], core_ids=[0])
    return r.results[0]["out_dram"]
```
